# Optimizing a Trainium2 kernel written in Bass

```python
import numpy as np
import jax
import jax.numpy as jnp

def _softmax(x, axis=-1):
    return jax.nn.softmax(x, axis=axis)

def _gelu(x):
    return jax.nn.gelu(x, approximate=True)

def _silu(x):
    return jax.nn.silu(x)

def _sigmoid(x):
    return jax.nn.sigmoid(x)

def _layernorm(x, axis=-1, eps=1e-05):
    m = jnp.mean(x, axis=axis, keepdims=True)
    v = jnp.var(x, axis=axis, keepdims=True)
    return (x - m) / jnp.sqrt(v + eps)

def _scatter_add(tgt, idx, src, axis=0):
    return tgt.at[idx].add(src)

def _segment_sum(src, seg, n):
    return jax.ops.segment_sum(src, seg, n)
kernel_name = 'mk_seq_postln_d2_jaxref_r8_122af3'

def setup_inputs(seed: int=0):
    np.random.seed(seed)
    _w = jnp.asarray

    def _L0_attn_setup():
        import jax, jax.numpy as jnp
        import numpy as np
        EMBED = 128
        HEADS = 16
        PER_DIM = EMBED // HEADS
        C, T = (64, 128)

        def entmax15(x, axis=-1):
            x = x / 2.0
            x = x - jnp.max(x, axis=axis, keepdims=True)
            xs = -jnp.sort(-x, axis=axis)
            n = x.shape[axis]
            k = jnp.arange(1, n + 1, dtype=x.dtype)
            cum = jnp.cumsum(xs, axis=axis)
            cumsq = jnp.cumsum(xs * xs, axis=axis)
            mean = cum / k
            ss = cumsq - cum * mean
            delta = jnp.clip((1.0 - ss) / k, 0.0)
            tau = mean - jnp.sqrt(delta)
            k_star = jnp.sum((tau <= xs).astype(jnp.int32), axis=axis, keepdims=True) - 1
            tau_star = jnp.take_along_axis(tau, k_star, axis=axis)
            return jnp.square(jnp.clip(x - tau_star, 0.0))
        key = jax.random.key(seed)
        ks = jax.random.split(key, 7)
        s = 1.0 / np.sqrt(PER_DIM)
        return {'y_de': jax.random.normal(ks[0], (C, T, EMBED), dtype=jnp.float32), 'Wq': jax.random.normal(ks[1], (PER_DIM, PER_DIM), dtype=jnp.float32) * s, 'bq': jax.random.normal(ks[2], (PER_DIM,), dtype=jnp.float32) * s, 'Wk': jax.random.normal(ks[3], (PER_DIM, PER_DIM), dtype=jnp.float32) * s, 'bk': jax.random.normal(ks[4], (PER_DIM,), dtype=jnp.float32) * s, 'Wv': jax.random.normal(ks[5], (PER_DIM, PER_DIM), dtype=jnp.float32) * s, 'bv': jax.random.normal(ks[6], (PER_DIM,), dtype=jnp.float32) * s}
    _L0_attn_in = _L0_attn_setup()

    def _L0_ffn_setup():
        import jax, jax.numpy as jnp
        import numpy as np
        DIM = 128
        DEPTH = 6
        HEADS = 16
        DIM_HEAD = 64
        WINDOW = 32
        INNER = HEADS * DIM_HEAD
        DIM_INNER = int(DIM * 4 * 2 / 3)
        QK_SCALE = 8.0

        def shift_tokens(t):
            a, s = jnp.split(t, 2, -1)
            s = jnp.pad(s, ((0, 0), (1, 0), (0, 0)))[:, :-1]
            return jnp.concatenate([a, s], -1)

        def l2norm(t):
            return t / jnp.maximum(jnp.linalg.norm(t, axis=-1, keepdims=True), 1e-12)

        def rotate_half(x):
            x1, x2 = jnp.split(x, 2, -1)
            return jnp.concatenate([-x2, x1], -1)

        def rotary_tables(n):
            half = jnp.arange(0, DIM_HEAD, 2, dtype=jnp.float32)
            inv_freq = 1.0 / 10000.0 ** (half / DIM_HEAD)
            t = jnp.arange(n, dtype=jnp.float32)
            freqs = t[:, None] * inv_freq[None, :]
            freqs = jnp.concatenate([freqs, freqs], -1)
            base_scale = (half + 0.4 * DIM_HEAD) / (1.4 * DIM_HEAD)
            power = (t - n // 2) / (WINDOW // 2)
            scale = base_scale[None, :] ** power[:, None]
            scale = jnp.concatenate([scale, scale], -1)
            return (freqs, scale)

        def local_attention(q, k, v):
            b, h, n, d = q.shape
            w = WINDOW
            nw = n // w
            bq = q.reshape(b, h, nw, w, d)
            bk = k.reshape(b, h, nw, w, d)
            bv = v.reshape(b, h, nw, w, d)

            def look(t):
                p = jnp.pad(t, ((0, 0), (0, 0), (1, 0), (0, 0), (0, 0)))
                return jnp.concatenate([p[:, :, :nw], p[:, :, 1:]], axis=3)
            bk2, bv2 = (look(bk), look(bv))
            seq = jnp.arange(n).reshape(nw, w)
            seq_p = jnp.pad(seq, ((1, 0), (0, 0)), constant_values=-1)
            jt = jnp.concatenate([seq_p[:nw], seq_p[1:]], axis=1)
            it = seq[:, :, None]
            jb = jt[:, None, :]
            mask = (it < jb) | (it > jb + w) | (jb == -1)
            sim = jnp.einsum('bhwie,bhwje->bhwij', bq, bk2) * QK_SCALE
            sim = jnp.where(mask, -jnp.finfo(sim.dtype).max, sim)
            attn = jax.nn.softmax(sim, -1)
            out = jnp.einsum('bhwij,bhwje->bhwie', attn, bv2)
            return out.reshape(b, h, n, d)

        def attn_layer(x, Wqkv, qs, ksc, Wo):
            b, n, _ = x.shape
            qkv = x @ Wqkv
            q, k, v = jnp.split(qkv, 3, -1)
            sh = lambda t: t.reshape(b, n, HEADS, DIM_HEAD).transpose(0, 2, 1, 3)
            q, k, v = (sh(q), sh(k), sh(v))
            q = l2norm(q) * qs
            k = l2norm(k) * ksc
            freqs, scale = rotary_tables(n)
            cos, sin = (jnp.cos(freqs), jnp.sin(freqs))
            q = q * cos * scale + rotate_half(q) * sin * scale
            inv = 1.0 / scale
            k = k * cos * inv + rotate_half(k) * sin * inv
            out = local_attention(q, k, v)
            out = out.transpose(0, 2, 1, 3).reshape(b, n, INNER)
            return out @ Wo

        def ffn_layer(x, g, bln, W1, b1, W2, b2):
            mu = x.mean(-1, keepdims=True)
            var = ((x - mu) ** 2).mean(-1, keepdims=True)
            xn = (x - mu) / jnp.sqrt(var + 1e-05) * g + bln
            hg = xn @ W1 + b1
            a, gate = jnp.split(hg, 2, -1)
            return a * jax.nn.gelu(gate, approximate=False) @ W2 + b2
        key = jax.random.key(seed)
        ks = jax.random.split(key, 8)
        B, N = (2, 256)
        init = lambda k, shape: jax.random.normal(k, shape, jnp.float32) * 0.02
        return {'x': jax.random.normal(ks[0], (B, N, DIM), jnp.float32), 'Wqkv': init(ks[1], (DEPTH, DIM, 3 * INNER)), 'q_scale': jnp.ones((DEPTH, DIM_HEAD), jnp.float32), 'k_scale': jnp.ones((DEPTH, DIM_HEAD), jnp.float32), 'Wo': init(ks[2], (DEPTH, INNER, DIM)), 'ln_g': jnp.ones((DEPTH, DIM), jnp.float32), 'ln_b': jnp.zeros((DEPTH, DIM), jnp.float32), 'W1': init(ks[3], (DEPTH, DIM, 2 * DIM_INNER)), 'b1': jnp.zeros((DEPTH, 2 * DIM_INNER), jnp.float32), 'W2': init(ks[4], (DEPTH, DIM_INNER, DIM)), 'b2': jnp.zeros((DEPTH, DIM), jnp.float32)}
    _L0_ffn_in = _L0_ffn_setup()

    def _L1_attn_setup():
        import jax, jax.numpy as jnp
        import numpy as np
        DIMS = 128
        HEAD = 16
        HD = DIMS // HEAD
        CTX = 256
        B = 1

        def _ln(x, w, b, eps=1e-05):
            m = jnp.mean(x, axis=-1, keepdims=True)
            v = jnp.var(x, axis=-1, keepdims=True)
            return (x - m) * jax.lax.rsqrt(v + eps) * w + b

        def _rotary(x, xa, rh_w, rh_b):
            c = x.shape[2]
            d2 = x.shape[-1] // 2
            mel_max = 2595.0 * np.log10(1.0 + 4000.0 / 200.0)
            scale = jnp.power(10.0, jnp.linspace(0.0, mel_max, d2, dtype=jnp.float32) / 2595.0) - 1.0
            fb = 200.0 * scale / 1000.0
            freqs = jnp.arange(c, dtype=jnp.float32)[:, None] * fb[None, :]
            per_step = (xa @ rh_w + rh_b)[..., 0]
            radius = jnp.clip(per_step / 100.0, 0.5, 2.0)
            fr = radius[:, :, None] * jnp.cos(freqs)[None]
            fi = radius[:, :, None] * jnp.sin(freqs)[None]
            xr = x[..., 0::2]
            xi = x[..., 1::2]
            out_r = xr * fr[:, None] - xi * fi[:, None]
            out_i = xr * fi[:, None] + xi * fr[:, None]
            return jnp.stack([out_r, out_i], axis=-1).reshape(x.shape)
        key = jax.random.key(seed)
        ks = jax.random.split(key, 8)
        s = 0.02
        return {'x': jax.random.normal(ks[0], (B, CTX, DIMS), dtype=jnp.float32), 'qn_w': jnp.ones((DIMS,), jnp.float32), 'qn_b': jnp.zeros((DIMS,), jnp.float32), 'q_w': jax.random.normal(ks[1], (DIMS, DIMS), jnp.float32) * s, 'q_b': jnp.zeros((DIMS,), jnp.float32), 'kvn_w': jnp.ones((DIMS,), jnp.float32), 'kvn_b': jnp.zeros((DIMS,), jnp.float32), 'kv_w': jax.random.normal(ks[2], (DIMS, 2 * DIMS), jnp.float32) * s, 'kv_b': jnp.zeros((2 * DIMS,), jnp.float32), 'out_w': jax.random.normal(ks[3], (DIMS, DIMS), jnp.float32) * s, 'out_b': jnp.zeros((DIMS,), jnp.float32), 'ln_w': jnp.ones((HD,), jnp.float32), 'ln_b': jnp.zeros((HD,), jnp.float32), 'rh_w': jax.random.normal(ks[4], (DIMS, 1), jnp.float32) * s, 'rh_b': jnp.zeros((1,), jnp.float32)}
    _L1_attn_in = _L1_attn_setup()

    def _L1_ffn_setup():
        import jax, jax.numpy as jnp
        import numpy as np
        B, S, D = (2, 256, 128)
        H, HKV = (16, 4)
        HD = D // H
        F, E, K = (256, 8, 2)
        THETA = 10000.0
        EPS = 1e-05

        def _rmsnorm(x, w):
            return x * jax.lax.rsqrt(jnp.mean(x * x, axis=-1, keepdims=True) + EPS) * w

        def _rope_cos_sin(seq_len, head_dim, theta):
            inv_freq = 1.0 / theta ** (jnp.arange(0, head_dim, 2, dtype=jnp.float32) / head_dim)
            freqs = jnp.arange(seq_len, dtype=jnp.float32)[:, None] * inv_freq
            return (jnp.cos(freqs), jnp.sin(freqs))

        def _apply_rope(x, cos, sin):
            x1, x2 = jnp.split(x, 2, axis=-1)
            c = cos[None, :, None, :]
            s = sin[None, :, None, :]
            return jnp.concatenate([x1 * c - x2 * s, x2 * c + x1 * s], axis=-1)
        key = jax.random.key(seed)
        ks = jax.random.split(key, 12)
        s = 0.02
        return {'hidden_states': jax.random.normal(ks[0], (B, S, D), jnp.float32), 'ln1_w': 1.0 + 0.1 * jax.random.normal(ks[1], (D,), jnp.float32), 'ln2_w': 1.0 + 0.1 * jax.random.normal(ks[2], (D,), jnp.float32), 'Wq': s * jax.random.normal(ks[3], (D, H * HD), jnp.float32), 'Wk': s * jax.random.normal(ks[4], (D, HKV * HD), jnp.float32), 'Wv': s * jax.random.normal(ks[5], (D, HKV * HD), jnp.float32), 'Wo': s * jax.random.normal(ks[6], (H * HD, D), jnp.float32), 'Wr': s * jax.random.normal(ks[7], (D, E), jnp.float32), 'Wg': s * jax.random.normal(ks[8], (E, D, F), jnp.float32), 'Wu': s * jax.random.normal(ks[9], (E, D, F), jnp.float32), 'Wd': s * jax.random.normal(ks[10], (E, F, D), jnp.float32)}
    _L1_ffn_in = _L1_ffn_setup()
    _d = {'L0_attn_y_de': _L0_attn_in['y_de'], 'L0_attn_Wq': _L0_attn_in['Wq'], 'L0_attn_bq': _L0_attn_in['bq'], 'L0_attn_Wk': _L0_attn_in['Wk'], 'L0_attn_bk': _L0_attn_in['bk'], 'L0_attn_Wv': _L0_attn_in['Wv'], 'L0_attn_bv': _L0_attn_in['bv'], 'L0_ffn_Wqkv': _L0_ffn_in['Wqkv'], 'L0_ffn_q_scale': _L0_ffn_in['q_scale'], 'L0_ffn_k_scale': _L0_ffn_in['k_scale'], 'L0_ffn_Wo': _L0_ffn_in['Wo'], 'L0_ffn_ln_g': _L0_ffn_in['ln_g'], 'L0_ffn_ln_b': _L0_ffn_in['ln_b'], 'L0_ffn_W1': _L0_ffn_in['W1'], 'L0_ffn_b1': _L0_ffn_in['b1'], 'L0_ffn_W2': _L0_ffn_in['W2'], 'L0_ffn_b2': _L0_ffn_in['b2'], 'L1_attn_qn_w': _L1_attn_in['qn_w'], 'L1_attn_qn_b': _L1_attn_in['qn_b'], 'L1_attn_q_w': _L1_attn_in['q_w'], 'L1_attn_q_b': _L1_attn_in['q_b'], 'L1_attn_kvn_w': _L1_attn_in['kvn_w'], 'L1_attn_kvn_b': _L1_attn_in['kvn_b'], 'L1_attn_kv_w': _L1_attn_in['kv_w'], 'L1_attn_kv_b': _L1_attn_in['kv_b'], 'L1_attn_out_w': _L1_attn_in['out_w'], 'L1_attn_out_b': _L1_attn_in['out_b'], 'L1_attn_ln_w': _L1_attn_in['ln_w'], 'L1_attn_ln_b': _L1_attn_in['ln_b'], 'L1_attn_rh_w': _L1_attn_in['rh_w'], 'L1_attn_rh_b': _L1_attn_in['rh_b'], 'L1_ffn_ln1_w': _L1_ffn_in['ln1_w'], 'L1_ffn_ln2_w': _L1_ffn_in['ln2_w'], 'L1_ffn_Wq': _L1_ffn_in['Wq'], 'L1_ffn_Wk': _L1_ffn_in['Wk'], 'L1_ffn_Wv': _L1_ffn_in['Wv'], 'L1_ffn_Wo': _L1_ffn_in['Wo'], 'L1_ffn_Wr': _L1_ffn_in['Wr'], 'L1_ffn_Wg': _L1_ffn_in['Wg'], 'L1_ffn_Wu': _L1_ffn_in['Wu'], 'L1_ffn_Wd': _L1_ffn_in['Wd']}
    _x0 = _d['L0_attn_y_de']
    _d['L0_attn_y_de'] = jax.random.normal(jax.random.fold_in(jax.random.key(seed), 1), (16, 256, 128), dtype=_x0.dtype)
    del _x0
    return _d

def reference(L0_attn_y_de, L0_attn_Wq, L0_attn_bq, L0_attn_Wk, L0_attn_bk, L0_attn_Wv, L0_attn_bv, L0_ffn_Wqkv, L0_ffn_q_scale, L0_ffn_k_scale, L0_ffn_Wo, L0_ffn_ln_g, L0_ffn_ln_b, L0_ffn_W1, L0_ffn_b1, L0_ffn_W2, L0_ffn_b2, L1_attn_qn_w, L1_attn_qn_b, L1_attn_q_w, L1_attn_q_b, L1_attn_kvn_w, L1_attn_kvn_b, L1_attn_kv_w, L1_attn_kv_b, L1_attn_out_w, L1_attn_out_b, L1_attn_ln_w, L1_attn_ln_b, L1_attn_rh_w, L1_attn_rh_b, L1_ffn_ln1_w, L1_ffn_ln2_w, L1_ffn_Wq, L1_ffn_Wk, L1_ffn_Wv, L1_ffn_Wo, L1_ffn_Wr, L1_ffn_Wg, L1_ffn_Wu, L1_ffn_Wd):

    def _L0_attn_ref(y_de, Wq, bq, Wk, bk, Wv, bv):
        import jax, jax.numpy as jnp
        import numpy as np
        EMBED = 128
        HEADS = 16
        PER_DIM = EMBED // HEADS
        C, T = (64, 128)

        def entmax15(x, axis=-1):
            x = x / 2.0
            x = x - jnp.max(x, axis=axis, keepdims=True)
            xs = -jnp.sort(-x, axis=axis)
            n = x.shape[axis]
            k = jnp.arange(1, n + 1, dtype=x.dtype)
            cum = jnp.cumsum(xs, axis=axis)
            cumsq = jnp.cumsum(xs * xs, axis=axis)
            mean = cum / k
            ss = cumsq - cum * mean
            delta = jnp.clip((1.0 - ss) / k, 0.0)
            tau = mean - jnp.sqrt(delta)
            k_star = jnp.sum((tau <= xs).astype(jnp.int32), axis=axis, keepdims=True) - 1
            tau_star = jnp.take_along_axis(tau, k_star, axis=axis)
            return jnp.square(jnp.clip(x - tau_star, 0.0))
        c, t, e = y_de.shape
        mask = jnp.tril(jnp.ones((t, e), dtype=y_de.dtype), k=-1)
        x = (y_de * mask).reshape(c, t, HEADS, PER_DIM)
        q = x @ Wq.T + bq
        k_ = x @ Wk.T + bk
        v = x @ Wv.T + bv
        scale = 1.0 / e ** 0.5
        scores = jnp.einsum('cthd,ctgd->cthg', q, k_) * scale
        attn = entmax15(scores, axis=-1)
        out = jnp.einsum('cthg,ctgd->cthd', attn, v)
        return out.reshape(c, t, e)

    def _L0_ffn_ref(x, Wqkv, q_scale, k_scale, Wo, ln_g, ln_b, W1, b1, W2, b2):
        import jax, jax.numpy as jnp
        import numpy as np
        DIM = 128
        DEPTH = 6
        HEADS = 16
        DIM_HEAD = 64
        WINDOW = 32
        INNER = HEADS * DIM_HEAD
        DIM_INNER = int(DIM * 4 * 2 / 3)
        QK_SCALE = 8.0

        def shift_tokens(t):
            a, s = jnp.split(t, 2, -1)
            s = jnp.pad(s, ((0, 0), (1, 0), (0, 0)))[:, :-1]
            return jnp.concatenate([a, s], -1)

        def l2norm(t):
            return t / jnp.maximum(jnp.linalg.norm(t, axis=-1, keepdims=True), 1e-12)

        def rotate_half(x):
            x1, x2 = jnp.split(x, 2, -1)
            return jnp.concatenate([-x2, x1], -1)

        def rotary_tables(n):
            half = jnp.arange(0, DIM_HEAD, 2, dtype=jnp.float32)
            inv_freq = 1.0 / 10000.0 ** (half / DIM_HEAD)
            t = jnp.arange(n, dtype=jnp.float32)
            freqs = t[:, None] * inv_freq[None, :]
            freqs = jnp.concatenate([freqs, freqs], -1)
            base_scale = (half + 0.4 * DIM_HEAD) / (1.4 * DIM_HEAD)
            power = (t - n // 2) / (WINDOW // 2)
            scale = base_scale[None, :] ** power[:, None]
            scale = jnp.concatenate([scale, scale], -1)
            return (freqs, scale)

        def local_attention(q, k, v):
            b, h, n, d = q.shape
            w = WINDOW
            nw = n // w
            bq = q.reshape(b, h, nw, w, d)
            bk = k.reshape(b, h, nw, w, d)
            bv = v.reshape(b, h, nw, w, d)

            def look(t):
                p = jnp.pad(t, ((0, 0), (0, 0), (1, 0), (0, 0), (0, 0)))
                return jnp.concatenate([p[:, :, :nw], p[:, :, 1:]], axis=3)
            bk2, bv2 = (look(bk), look(bv))
            seq = jnp.arange(n).reshape(nw, w)
            seq_p = jnp.pad(seq, ((1, 0), (0, 0)), constant_values=-1)
            jt = jnp.concatenate([seq_p[:nw], seq_p[1:]], axis=1)
            it = seq[:, :, None]
            jb = jt[:, None, :]
            mask = (it < jb) | (it > jb + w) | (jb == -1)
            sim = jnp.einsum('bhwie,bhwje->bhwij', bq, bk2) * QK_SCALE
            sim = jnp.where(mask, -jnp.finfo(sim.dtype).max, sim)
            attn = jax.nn.softmax(sim, -1)
            out = jnp.einsum('bhwij,bhwje->bhwie', attn, bv2)
            return out.reshape(b, h, n, d)

        def attn_layer(x, Wqkv, qs, ksc, Wo):
            b, n, _ = x.shape
            qkv = x @ Wqkv
            q, k, v = jnp.split(qkv, 3, -1)
            sh = lambda t: t.reshape(b, n, HEADS, DIM_HEAD).transpose(0, 2, 1, 3)
            q, k, v = (sh(q), sh(k), sh(v))
            q = l2norm(q) * qs
            k = l2norm(k) * ksc
            freqs, scale = rotary_tables(n)
            cos, sin = (jnp.cos(freqs), jnp.sin(freqs))
            q = q * cos * scale + rotate_half(q) * sin * scale
            inv = 1.0 / scale
            k = k * cos * inv + rotate_half(k) * sin * inv
            out = local_attention(q, k, v)
            out = out.transpose(0, 2, 1, 3).reshape(b, n, INNER)
            return out @ Wo

        def ffn_layer(x, g, bln, W1, b1, W2, b2):
            mu = x.mean(-1, keepdims=True)
            var = ((x - mu) ** 2).mean(-1, keepdims=True)
            xn = (x - mu) / jnp.sqrt(var + 1e-05) * g + bln
            hg = xn @ W1 + b1
            a, gate = jnp.split(hg, 2, -1)
            return a * jax.nn.gelu(gate, approximate=False) @ W2 + b2
        for i in range(DEPTH):
            x = attn_layer(shift_tokens(x), Wqkv[i], q_scale[i], k_scale[i], Wo[i]) + x
            x = ffn_layer(shift_tokens(x), ln_g[i], ln_b[i], W1[i], b1[i], W2[i], b2[i]) + x
        return x

    def _L1_attn_ref(x, qn_w, qn_b, q_w, q_b, kvn_w, kvn_b, kv_w, kv_b, out_w, out_b, ln_w, ln_b, rh_w, rh_b):
        import jax, jax.numpy as jnp
        import numpy as np
        DIMS = 128
        HEAD = 16
        HD = DIMS // HEAD
        CTX = 256
        B = 1

        def _ln(x, w, b, eps=1e-05):
            m = jnp.mean(x, axis=-1, keepdims=True)
            v = jnp.var(x, axis=-1, keepdims=True)
            return (x - m) * jax.lax.rsqrt(v + eps) * w + b

        def _rotary(x, xa, rh_w, rh_b):
            c = x.shape[2]
            d2 = x.shape[-1] // 2
            mel_max = 2595.0 * np.log10(1.0 + 4000.0 / 200.0)
            scale = jnp.power(10.0, jnp.linspace(0.0, mel_max, d2, dtype=jnp.float32) / 2595.0) - 1.0
            fb = 200.0 * scale / 1000.0
            freqs = jnp.arange(c, dtype=jnp.float32)[:, None] * fb[None, :]
            per_step = (xa @ rh_w + rh_b)[..., 0]
            radius = jnp.clip(per_step / 100.0, 0.5, 2.0)
            fr = radius[:, :, None] * jnp.cos(freqs)[None]
            fi = radius[:, :, None] * jnp.sin(freqs)[None]
            xr = x[..., 0::2]
            xi = x[..., 1::2]
            out_r = xr * fr[:, None] - xi * fi[:, None]
            out_i = xr * fi[:, None] + xi * fr[:, None]
            return jnp.stack([out_r, out_i], axis=-1).reshape(x.shape)
        b, c, dims = x.shape
        kv = _ln(x, kvn_w, kvn_b) @ kv_w + kv_b
        kv = kv.reshape(b, c, 2, HEAD, HD).transpose(2, 0, 3, 1, 4)
        k, v = (kv[0], kv[1])
        q = (_ln(x, qn_w, qn_b) @ q_w + q_b).reshape(b, c, HEAD, HD).transpose(0, 2, 1, 3)
        q = _rotary(q, x, rh_w, rh_b)
        k = _rotary(k, x, rh_w, rh_b)
        qn = _ln(q, ln_w, ln_b)
        kn = _ln(k, ln_w, ln_b)
        scores = jnp.einsum('bhqd,bhkd->bhqk', qn, kn) / np.sqrt(HD).astype(np.float32)
        attn = jax.nn.softmax(scores, axis=-1)
        a = jnp.einsum('bhqk,bhkd->bhqd', attn, v)
        a = a.transpose(0, 2, 1, 3).reshape(b, c, dims)
        return a @ out_w + out_b

    def _L1_ffn_ref(hidden_states, ln1_w, ln2_w, Wq, Wk, Wv, Wo, Wr, Wg, Wu, Wd):
        import jax, jax.numpy as jnp
        import numpy as np
        B, S, D = (2, 256, 128)
        H, HKV = (16, 4)
        HD = D // H
        F, E, K = (256, 8, 2)
        THETA = 10000.0
        EPS = 1e-05

        def _rmsnorm(x, w):
            return x * jax.lax.rsqrt(jnp.mean(x * x, axis=-1, keepdims=True) + EPS) * w

        def _rope_cos_sin(seq_len, head_dim, theta):
            inv_freq = 1.0 / theta ** (jnp.arange(0, head_dim, 2, dtype=jnp.float32) / head_dim)
            freqs = jnp.arange(seq_len, dtype=jnp.float32)[:, None] * inv_freq
            return (jnp.cos(freqs), jnp.sin(freqs))

        def _apply_rope(x, cos, sin):
            x1, x2 = jnp.split(x, 2, axis=-1)
            c = cos[None, :, None, :]
            s = sin[None, :, None, :]
            return jnp.concatenate([x1 * c - x2 * s, x2 * c + x1 * s], axis=-1)
        b, s, d = hidden_states.shape
        residual = hidden_states
        h = _rmsnorm(hidden_states, ln1_w)
        q = (h @ Wq).reshape(b, s, H, HD)
        k = (h @ Wk).reshape(b, s, HKV, HD)
        v = (h @ Wv).reshape(b, s, HKV, HD)
        cos, sin = _rope_cos_sin(s, HD, THETA)
        q = _apply_rope(q, cos, sin)
        k = _apply_rope(k, cos, sin)
        rep = H // HKV
        k = jnp.repeat(k, rep, axis=2)
        v = jnp.repeat(v, rep, axis=2)
        scores = jnp.einsum('bqhd,bkhd->bhqk', q, k) / np.sqrt(HD).astype(np.float32)
        causal = jnp.tril(jnp.ones((s, s), dtype=bool))
        scores = jnp.where(causal[None, None], scores, jnp.finfo(scores.dtype).min)
        attn = jax.nn.softmax(scores, axis=-1)
        ctx = jnp.einsum('bhqk,bkhd->bqhd', attn, v).reshape(b, s, H * HD)
        attn_out = ctx @ Wo
        h = jnp.clip(residual + attn_out, -100.0, 100.0)
        residual = h
        hn = _rmsnorm(h, ln2_w)
        flat = hn.reshape(b * s, d)
        logits = flat @ Wr
        probs = jax.nn.softmax(logits, axis=-1)
        topv, topi = jax.lax.top_k(probs, K)
        topv = topv / jnp.sum(topv, axis=-1, keepdims=True)
        w = jnp.sum(jax.nn.one_hot(topi, E, dtype=flat.dtype) * topv[..., None], axis=1)
        g = jnp.einsum('td,edf->etf', flat, Wg)
        u = jnp.einsum('td,edf->etf', flat, Wu)
        a = jax.nn.silu(g) * u
        o = jnp.einsum('etf,efd->etd', a, Wd)
        moe_out = jnp.einsum('te,etd->td', w, o).reshape(b, s, d)
        out = jnp.clip(residual + moe_out, -100.0, 100.0)
        return out
    x = L0_attn_y_de
    x = _layernorm(x + _L0_attn_ref(x, L0_attn_Wq, L0_attn_bq, L0_attn_Wk, L0_attn_bk, L0_attn_Wv, L0_attn_bv), axis=-1)
    x = _layernorm(x + _L0_ffn_ref(x, L0_ffn_Wqkv, L0_ffn_q_scale, L0_ffn_k_scale, L0_ffn_Wo, L0_ffn_ln_g, L0_ffn_ln_b, L0_ffn_W1, L0_ffn_b1, L0_ffn_W2, L0_ffn_b2), axis=-1)
    x = _layernorm(x + _L1_attn_ref(x, L1_attn_qn_w, L1_attn_qn_b, L1_attn_q_w, L1_attn_q_b, L1_attn_kvn_w, L1_attn_kvn_b, L1_attn_kv_w, L1_attn_kv_b, L1_attn_out_w, L1_attn_out_b, L1_attn_ln_w, L1_attn_ln_b, L1_attn_rh_w, L1_attn_rh_b), axis=-1)
    x = _layernorm(x + _L1_ffn_ref(x, L1_ffn_ln1_w, L1_ffn_ln2_w, L1_ffn_Wq, L1_ffn_Wk, L1_ffn_Wv, L1_ffn_Wo, L1_ffn_Wr, L1_ffn_Wg, L1_ffn_Wu, L1_ffn_Wd), axis=-1)
    return x

_drawn_inputs = setup_inputs


def setup_inputs(seed=0):
    import zlib

    import numpy as np

    out = dict(_drawn_inputs(seed))
    spreads = {'L0_ffn_q_scale': (1.0, 0.6),
     'L0_ffn_k_scale': (1.0, 0.6),
     'L0_ffn_ln_g': (1.0, 0.6),
     'L0_ffn_ln_b': (0.0, 0.8),
     'L0_ffn_b1': (0.0, 0.8),
     'L0_ffn_b2': (0.0, 0.1),
     'L1_attn_qn_w': (1.0, 0.6),
     'L1_attn_qn_b': (0.0, 0.8),
     'L1_attn_q_b': (0.0, 0.8),
     'L1_attn_kvn_w': (1.0, 0.6),
     'L1_attn_kvn_b': (0.0, 0.8),
     'L1_attn_kv_b': (0.0, 0.353),
     'L1_attn_out_b': (0.0, 0.1),
     'L1_attn_ln_w': (1.0, 0.6),
     'L1_attn_ln_b': (0.0, 0.8)}
    factors = {'L0_attn_bk': 8.0,
     'L0_ffn_W1': 3.732,
     'L0_ffn_W2': 3.65,
     'L1_attn_q_w': 8.0,
     'L1_attn_kv_w': 2.858,
     'L1_ffn_ln1_w': 8.0,
     'L1_ffn_ln2_w': 8.0,
     'L1_ffn_Wq': 8.0,
     'L1_ffn_Wk': 8.0,
     'L1_ffn_Wv': 5.611,
     'L1_ffn_Wo': 5.509,
     'L1_ffn_Wr': 8.0,
     'L1_ffn_Wg': 8.0,
     'L1_ffn_Wu': 8.0,
     'L1_ffn_Wd': 8.0}
    for name, (base, spread) in spreads.items():
        noise = np.random.default_rng([zlib.crc32(name.encode()), seed]).standard_normal(out[name].shape)
        drawn = base * np.exp(spread * noise) if base else spread * noise
        out[name] = jnp.asarray(drawn.astype(out[name].dtype))
    for name, factor in factors.items():
        out[name] = (out[name] * factor).astype(out[name].dtype)
    return out
```

```python
from contextlib import ExitStack

import concourse.bass as bass
from concourse import mybir

ALU = mybir.AluOpType
ACT = mybir.ActivationFunctionType
F32 = mybir.dt.float32
BF16 = mybir.dt.bfloat16
X_AXIS = mybir.AxisListType.X

P = 128
B, T, E = 16, 256, 128
HALVES = T // P
TILES = B * HALVES
LN_EPS = 1e-5
MASKED = -1e30
STAGES = (1, 2, 3, 4)
DEPTH = 6


class Core:

    def __init__(self, nc, stage):
        self.nc, self.stage, self.ctx = nc, stage, ExitStack()

    def __enter__(self):
        return self

    def __exit__(self, *a):
        return self.ctx.__exit__(*a)

    def sb(self, name, shape, dt=F32):
        return self.ctx.enter_context(self.nc.sbuf_tensor(f"{self.stage}_{name}", [P] + list(shape), dt))

    def ps(self, name, shape, dt=F32):
        return self.ctx.enter_context(self.nc.psum_tensor(f"{self.stage}_{name}", [P] + list(shape), dt))

    def sem(self, name):
        return self.ctx.enter_context(self.nc.semaphore(f"{self.stage}_{name}"))

    def signals(self, **per_turn):
        made = [Signal(self.sem(n), k) for n, k in per_turn.items()]
        return made, made

    def block(self):
        return self.ctx.enter_context(self.nc.Block())


class Signal:

    def __init__(self, sem, per_turn):
        self.sem, self.per_turn = sem, per_turn

    def __call__(self, turn, k):
        return self.sem, turn * self.per_turn + (k + 1)


class Chain:

    def __init__(self, eng, ends, turn):
        self.eng, self.ends, self.turn, self.n = eng, ends, turn, 0

    def __call__(self, ins):
        self.free(ins)
        self.eng.wait_ge(*self.ends(self.turn, self.n))

    def free(self, ins):
        self.n += 1
        ins.then_inc(self.ends.sem, 1)


def hold(eng, scrap):
    eng.memset(scrap[:], 0.0)


def bc(ap, axis, n):
    ap = ap.unsqueeze(axis)
    return ap.broadcast_to([n if i == axis else d for i, d in enumerate(ap.shape)])


def layer_norm(nc, dve, link, h, stats, mv, veps, rstd, scrap, n, var_made, rstd_made, turn):
    for j in range(n):
        link.free(nc.vector.bn_stats(stats[:, j, :], h[:, j, :]))
    dve.wait_ge(*link.ends(turn, link.n))
    hold(nc.vector, scrap)
    for j in range(n):
        link.free(nc.vector.bn_aggr(mv[:, j, :], stats[:, j, :]))
    dve.wait_ge(*link.ends(turn, link.n))
    nc.vector.tensor_scalar(veps[:], mv[:, :, 1], LN_EPS, None, ALU.add).then_inc(var_made.sem, 1)
    link(nc.vector.tensor_tensor(h[:], h[:], bc(mv[:, :, 0], 2, E), ALU.subtract))
    dve.wait_ge(*rstd_made(turn, 1))


def load_x(nc, x_in, X):
    with Core(nc, "load") as m:
        landed = m.sem("landed")
        block = m.block()

        @block.sync
        def _(sp):
            sp.dma_start(X[:], x_in.rearrange("(i p) e -> p i e", p=P)).then_inc(landed, 16)
            sp.wait_ge(landed, 16)


def copy_x(nc, X, X0):
    with Core(nc, "keep") as m:
        kept = m.sem("kept")
        block = m.block()

        @block.sync
        def _(sp):
            sp.dma_start(X0[:], X[:]).then_inc(kept, 16)
            sp.wait_ge(kept, 16)


def store_x(nc, X, out):
    with Core(nc, "store") as m:
        stored = m.sem("stored")
        block = m.block()

        @block.sync
        def _(sp):
            sp.dma_start(out.rearrange("(i p) e -> p i e", p=P), X[:]).then_inc(stored, 16)
            sp.wait_ge(stored, 16)


def head_mixer(nc, X, ident_in, half_in, mask_in, w_in, bias_in, invk_in, idx_in):
    H, D = 16, 8
    G = H
    CH = 8
    TURNS = TILES // CH
    R = CH * H
    SCALE = 0.5 / float(E) ** 0.5
    QKV = 3 * E
    with Core(nc, "mix") as m:
        ident = m.sb("ident", [P])
        mask = m.sb("mask", [HALVES, E])
        w = m.sb("w", [QKV])
        bias = m.sb("bias", [QKV])
        invk = m.sb("invk", [G])
        idx = m.sb("idx", [G])
        neg_half = m.sb("neg_half", [CH])
        xm = m.sb("xm", [CH, E])
        xT = m.sb("xT", [CH, P])
        qkv = m.sb("qkv", [CH, QKV])
        prod = m.sb("prod", [2, H * G * D])
        S = m.sb("S", [G, R])
        U = m.sb("U", [G, R])
        V = m.sb("V", [G, R])
        C1 = m.sb("C1", [G, R])
        C2 = m.sb("C2", [G, R])
        top = m.sb("top", [R])
        tau = m.sb("tau", [R])
        o = m.sb("o", [CH, E])
        scrap = m.sb("scrap", [1])
        stats = m.sb("stats", [CH, 6])
        mv = m.sb("mv", [CH, 2])
        veps = m.sb("veps", [CH])
        rstd = m.sb("rstd", [CH])
        xT_ps = m.ps("xT_ps", [2, 4, P])
        qkv_ps = m.ps("qkv_ps", [4, 512])

        consts, const_set = m.sem("consts"), m.sem("const_set")
        DVE_STEPS = 100
        (masked, xT_made, xT_kept, qkv_made, qkv_kept, qk_mult, qk_summed, attn_made, av_mult, av_summed,
         delta_made, root_made, var_made, rstd_made, dve_step), signals = m.signals(
            masked=1, xT_made=2, xT_kept=2, qkv_made=CH, qkv_kept=CH, qk_mult=CH, qk_summed=CH, attn_made=1,
            av_mult=CH, av_summed=CH, delta_made=1, root_made=1, var_made=1, rstd_made=1, dve_step=DVE_STEPS)
        block = m.block()

        @block.sync
        def _(sp):
            for signal in signals:
                sp.sem_inc(signal.sem, 1)
            for dst, src in ((ident, ident_in), (mask, mask_in), (w, w_in)):
                sp.dma_start(dst[:], src).then_inc(consts, 16)
            for dst, src in ((bias, bias_in), (invk, invk_in), (idx, idx_in)):
                sp.dma_start(dst[:], src.partition_broadcast(P)).then_inc(consts, 16)

        @block.gpsimd
        def _(pool):
            pool.memset(neg_half[:], -0.5).then_inc(const_set, 1)
            pool.wait_ge(consts, 96)
            pool.wait_ge(const_set, 1)
            with pool.Fori(0, TURNS) as c:
                pool.wait_ge(*xT_made(c, 0))
                pool.tensor_tensor(xm[:].rearrange("p (a b) e -> p a b e", b=HALVES),
                                   X[:, bass.ds(c * CH, CH), :].rearrange("p (a b) e -> p a b e", b=HALVES),
                                   bc(mask[:], 1, CH // HALVES), ALU.mult).then_inc(masked.sem, 1)
                for j in range(CH):
                    pool.wait_ge(*qkv_kept(c, j + 1))
                    if j >= 2:
                        pool.wait_ge(*qk_summed(c, j - 1))
                    else:
                        pool.wait_ge(*av_summed(c, 0))
                    q = qkv[:, j, 0:E].rearrange("p (h d) -> p h d", d=D)
                    k = qkv[:, j, E:2 * E].rearrange("p (g d) -> p g d", d=D)
                    pool.tensor_tensor(prod[:, j % 2, :].rearrange("p (h g d) -> p h g d", h=H, g=G),
                                       bc(q, 2, G), bc(k, 1, H), ALU.mult).then_inc(qk_mult.sem, 1)
                pool.wait_ge(*attn_made(c, 1))
                for j in range(CH):
                    if j >= 2:
                        pool.wait_ge(*av_summed(c, j - 1))
                    a = S[:, :, j * H:(j + 1) * H].rearrange("p g h -> p h g")
                    v = qkv[:, j, 2 * E:3 * E].rearrange("p (g d) -> p d g", d=D)
                    pool.tensor_tensor(prod[:, j % 2, :].rearrange("p (h d g) -> p h d g", h=H, g=G),
                                       bc(a, 2, D), bc(v, 1, H), ALU.mult).then_inc(av_mult.sem, 1)
                pool.wait_ge(*var_made(c, 1))
                pool.tensor_tensor(rstd[:], veps[:], neg_half[:], ALU.pow).then_inc(rstd_made.sem, 1)

        @block.scalar
        def _(act):
            with act.Fori(0, TURNS) as c:
                for n in range(2):
                    act.wait_ge(*xT_made(c, n + 1))
                    act.wait_ge(*qkv_made(c, 0))
                    nc.scalar.copy(xT[:, 4 * n:4 * n + 4, :], xT_ps[:, n, :, :]).then_inc(xT_kept.sem, 1)
                act.wait_ge(*delta_made(c, 1))
                nc.scalar.activation(U[:], U[:], ACT.Sqrt).then_inc(root_made.sem, 1)

        @block.tensor
        def _(pe):
            pe.wait_ge(consts, 96)
            with pe.Fori(0, TURNS) as c:
                pe.wait_ge(*masked(c, 1))
                pe.wait_ge(*xT_kept(c, 0))
                for j in range(CH):
                    t = nc.tensor.transpose(xT_ps[:, j // 4, j % 4, :], xm[:, j, :], ident[:])
                    if j % 4 == 3:
                        t.then_inc(xT_made.sem, 1)
                for j in range(CH):
                    pe.wait_ge(*xT_kept(c, j // 4 + 1))
                    if j >= 4:
                        pe.wait_ge(*qkv_kept(c, j - 3))
                    else:
                        pe.wait_ge(*qkv_kept(c, 0))
                    nc.tensor.matmul(qkv_ps[:, j % 4, 0:QKV], xT[:, j, :], w[:], start=True, stop=True) \
                        .then_inc(qkv_made.sem, 1)

        def dve_turn(dve, c):
            link = Chain(dve, dve_step, c)
            tt, ts = nc.vector.tensor_tensor, nc.vector.tensor_scalar
            for j in range(CH):
                dve.wait_ge(*qkv_made(c, j + 1))
                if j == 0:
                    dve.wait_ge(*av_mult(c, 0))
                tt(qkv[:, j, :], qkv_ps[:, j % 4, 0:QKV], bias[:], ALU.add).then_inc(qkv_kept.sem, 1)
            for j in range(CH):
                dve.wait_ge(*qk_mult(c, j + 1))
                ins = nc.vector.tensor_reduce(S[:, :, j * H:(j + 1) * H].rearrange("p g h -> p h g"),
                                              prod[:, j % 2, :].rearrange("p (h g d) -> p h g d", h=H, g=G),
                                              op=ALU.add, axis=X_AXIS)
                ins.then_inc(qk_summed.sem, 1)
            dve.wait_ge(*qk_summed(c, CH))
            link(nc.vector.tensor_reduce(top[:], S[:].rearrange("p g r -> p r g"), op=ALU.max, axis=X_AXIS))
            link(tt(S[:], S[:], bc(top[:], 1, G), ALU.subtract))
            link(ts(S[:], S[:], SCALE, None, ALU.mult))
            src, dst = S, U
            for k in (2, 4, 8, 16):
                j = k // 2
                while j:
                    for up in (0, 1) if k < G else (0,):
                        v = lambda t, hi: (t[:].rearrange("p (a u b z l) r -> p a u b z (l r)", u=2, b=k // (2 * j), z=2, l=j)[:, :, up, :, hi, :]
                                           if k < G else
                                           t[:].rearrange("p (b z l) r -> p b z (l r)", z=2, l=j)[:, :, hi, :])
                        link(tt(v(dst, up), v(src, 0), v(src, 1), ALU.max))
                        link(tt(v(dst, 1 - up), v(src, 0), v(src, 1), ALU.min))
                    src, dst = dst, (V if dst is U else U)
                    j //= 2
            xs, tmp = src, dst
            assert xs is V and tmp is U
            link(tt(C2[:], xs[:], xs[:], ALU.mult))
            link(nc.vector.tensor_copy(C1[:, 0, :], xs[:, 0, :]))
            for k in range(1, G):
                link.free(tt(C1[:, k, :], C1[:, k - 1, :], xs[:, k, :], ALU.add))
                link(tt(C2[:, k, :], C2[:, k - 1, :], C2[:, k, :], ALU.add))
            ik = bc(invk[:], 2, R)
            link(tt(tmp[:], C1[:], ik, ALU.mult))
            link(tt(C1[:], C1[:], tmp[:], ALU.mult))
            link(tt(C2[:], C2[:], C1[:], ALU.subtract))
            link(ts(C2[:], C2[:], -1.0, 1.0, ALU.mult, ALU.add))
            link(tt(C1[:], C2[:], ik, ALU.mult))
            link(nc.vector.tensor_copy(C2[:], tmp[:]))
            ts(U[:], C1[:], 0.0, None, ALU.max).then_inc(delta_made.sem, 1)
            dve.wait_ge(*root_made(c, 1))
            link(tt(C2[:], C2[:], U[:], ALU.subtract))
            link(tt(U[:], C2[:], xs[:], ALU.is_le))
            link(nc.vector.tensor_reduce(top[:], U[:].rearrange("p g r -> p r g"), op=ALU.add, axis=X_AXIS))
            link(tt(U[:], bc(top[:], 1, G), bc(idx[:], 2, R), ALU.is_equal))
            link(tt(U[:], U[:], C2[:], ALU.mult))
            link(nc.vector.tensor_reduce(tau[:], U[:].rearrange("p g r -> p r g"), op=ALU.add, axis=X_AXIS))
            link(tt(S[:], S[:], bc(tau[:], 1, G), ALU.subtract))
            link(ts(S[:], S[:], 0.0, None, ALU.max))
            tt(S[:], S[:], S[:], ALU.mult).then_inc(attn_made.sem, 1)
            for j in range(CH):
                dve.wait_ge(*av_mult(c, j + 1))
                nc.vector.tensor_reduce(o[:, j, :].rearrange("p (h d) -> p h d", d=D),
                                        prod[:, j % 2, :].rearrange("p (h d g) -> p h d g", h=H, g=G),
                                        op=ALU.add, axis=X_AXIS).then_inc(av_summed.sem, 1)
            dve.wait_ge(*av_summed(c, CH))
            xv = X[:, bass.ds(c * CH, CH), :]
            link(tt(o[:], o[:], xv, ALU.add))
            layer_norm(nc, dve, link, o, stats, mv, veps, rstd, scrap, CH, var_made, rstd_made, c)
            link(tt(xv, o[:], bc(rstd[:], 2, E), ALU.mult))
            assert link.n == DVE_STEPS, link.n

        @block.vector
        def _(dve):
            dve.wait_ge(consts, 96)
            with dve.Fori(0, TURNS) as c:
                dve_turn(dve, c)


def layer_stack(nc, X, X0, a):
    H, D, W = 16, 64, 32
    NW = T // W
    PAIRS = H // 2
    QUADS, OCTS = 4, 2
    INNER = H * D
    F = int(E * 4 * 2 / 3)
    FC = [(f, min(P, F - f)) for f in range(0, F, P)]
    PROJ = QUADS * HALVES
    with Core(nc, "stack") as m:
        ident, identb = m.sb("ident", [P]), m.sb("identb", [P], BF16)
        mask = m.sb("mask", [PAIRS // OCTS, 2, 2 * W], BF16)
        cos0 = m.sb("cos0", [HALVES, 2, D])
        sin0 = m.sb("sin0", [HALVES, 2, D])
        cosq = m.sb("cosq", [HALVES, 2, D])
        sinq = m.sb("sinq", [HALVES, 2, D])
        qks = m.sb("qks", [2, D])
        wqk = m.sb("wqk", [QUADS, 2, 4 * D])
        wv = m.sb("wv", [INNER])
        wo = m.sb("wo", [PAIRS, E])
        w1 = m.sb("w1", [2 * F])
        w2 = m.sb("w2", [len(FC), E])
        lng, lnb = m.sb("lng", [1]), m.sb("lnb", [1])
        b1 = m.sb("b1", [2, len(FC)])
        b2 = m.sb("b2", [E])
        neg_half = m.sb("neg_half", [8])
        scrap = m.sb("scrap", [1])
        consts, const_set = m.sem("consts"), m.sem("const_set")
        CONSTS = 6 * 16
        (weights_in,), sig0 = m.signals(weights_in=16 * 11)
        (tables_made, ffn_done), sig1 = m.signals(tables_made=1, ffn_done=1)

        xs = m.sb("xs", [HALVES, E])
        hT = m.sb("hT", [W + T])
        sq = m.sb("sq", [2, 8 * D])
        ss = m.sb("ss", [PROJ, 8])
        rn = m.sb("rn", [PROJ, 8])
        qn = m.sb("qn", [2, 8 * D])
        t1 = m.sb("t1", [2, 8 * D])
        t2 = m.sb("t2", [2, 8 * D])
        QT = m.sb("QT", [PAIRS, T])
        KT = m.sb("KT", [PAIRS, W + T])
        V = m.sb("V", [2, HALVES, INNER])
        pr = m.sb("pr", [OCTS, 2, 4 * P])
        top = m.sb("top", [OCTS, 2, 8])
        den = m.sb("den", [OCTS, 2, 8])
        inv = m.sb("inv", [OCTS, 2, 8])
        PT = m.sb("PT", [OCTS, 2, 4, P])
        OT = m.sb("OT", [PAIRS, T])
        FS = 2
        FT = FS * HALVES
        fx = m.sb("fx", [FT, E])
        fhT = m.sb("fhT", [FS, T])
        stats = m.sb("stats", [FT, 6])
        mv = m.sb("mv", [FT, 2])
        veps = m.sb("veps", [FT])
        rstd = m.sb("rstd", [FT])
        xn = m.sb("xn", [FT, E])
        xnT = m.sb("xnT", [FS * T])
        gl = m.sb("gl", [len(FC), FS * T])
        hh = m.sb("hh", [len(FC), FS * T])
        yb = m.sb("yb", [FT, E])

        qk_ps = [m.ps(f"qk_ps{i}", [512]) for i in range(2)]
        tr_ps = [m.ps(f"tr_ps{i}", [4, P]) for i in range(2)]
        s_ps = [m.ps(f"s_ps{i}", [512]) for i in range(2)]
        o_ps = [m.ps(f"o_ps{i}", [512]) for i in range(2)]

        DVE_A = 2 * PROJ + 4 * OCTS
        TRU = 1 + PROJ + 2 * OCTS
        (xs_made, hT_made, qk_made, sq_made, ss_made, rn_made, qn_made, t2_made, r_made, tr_made, tr_kept,
         v_made, v_kept, s_made, p_shifted, p_exp, inv_made, p_normed, o_made, o_kept, y_made, x_made,
         dve_step), sig2 = m.signals(
            xs_made=1, hT_made=1, qk_made=8, sq_made=8, ss_made=8, rn_made=8, qn_made=8, t2_made=8, r_made=8,
            tr_made=TRU, tr_kept=TRU, v_made=8, v_kept=8, s_made=4, p_shifted=4, p_exp=4, inv_made=4,
            p_normed=4, o_made=4, o_kept=4, y_made=1, x_made=1, dve_step=DVE_A)
        NF = len(FC)
        DVE_F = 2 * FT + 1
        (fx_made, fT_made, fT_kept, fh_made, fvar_made, frstd_made, fxn_made, fnT_made, fnT_kept,
         f1_made, fgelu_made, fhh_made, fy_made, fx_done, fdve_step), sig3 = m.signals(
            fx_made=1, fT_made=1, fT_kept=2, fh_made=1, fvar_made=1, frstd_made=1, fxn_made=FT, fnT_made=1,
            fnT_kept=1, f1_made=NF, fgelu_made=NF, fhh_made=NF, fy_made=1, fx_done=1, fdve_step=DVE_F)

        ORDER = [("x", 0)]
        for i in range(PROJ + 2):
            if i < PROJ:
                ORDER += [("proj", i), ("v", i), ("norm", i)]
            if 1 <= i <= PROJ:
                ORDER += [("rope", i - 1)]
            if i >= 2:
                ORDER += [("add", i - 2), ("qkT", i - 2)]
            ORDER += {5: [("scores", 0)], 6: [("shift", 0)], 7: [("sum", 0)], 8: [("pT", 0)],
                      9: [("pv", 0)]}.get(i, [])
        ORDER += [("scores", 1), ("shift", 1), ("sum", 1), ("pT", 1), ("pv", 1), ("out", 0)]

        USES = [("x", 0)]
        for step, n in ORDER:
            if step == "qkT":
                USES.append(("qkT", n))
            if step == "pT":
                USES += [("pT", 2 * n), ("pT", 2 * n + 1)]
        use_of = {u: i for i, u in enumerate(USES)}
        assert len(USES) == TRU

        def head_groups(ap):
            return ap.rearrange("p (g d) -> p g d", d=D)

        def swap_halves(out, x, table, t):
            for half in range(2):
                o = out.rearrange("p (c g z d) -> p c g z d", c=2, g=4, z=2)[:, :, :, half, :]
                i = x.rearrange("p (c g z d) -> p c g z d", c=2, g=4, z=2)[:, :, :, 1 - half, :]
                s = table[:, t, :, :].rearrange("p c (z d) -> p c z d", z=2)[:, :, half, :]
                yield o, i, bc(s, 2, 4)

        block = m.block()

        @block.sync
        def _(sp):
            for signal in sig0 + sig1 + sig2 + sig3:
                sp.sem_inc(signal.sem, 1)
            sp.dma_start(X0[:], X[:]).then_inc(consts, 16)
            for dst, src in ((ident, "ident"), (identb, "identb"), (mask, "win_mask"), (cos0, "cos0"), (sin0, "sin0")):
                sp.dma_start(dst[:], a[src]).then_inc(consts, 16)
            with sp.Fori(0, DEPTH) as l:
                sp.wait_ge(*ffn_done(l, 0))
                one = lambda ap: ap[bass.ds(l, 1)].rearrange("o p n -> (o p) n")
                row = lambda ap: ap[bass.ds(l, 1), :].rearrange("o n -> (o n)")
                wsrc = one(a["wqkv"])
                up = weights_in.sem
                for c in range(2):
                    sp.dma_start(wqk[:, :, c, :], wsrc[:, c * INNER:(c + 1) * INNER].rearrange("p (q n) -> p q n", q=QUADS)).then_inc(up, 16)
                sp.dma_start(wv[:], wsrc[:, 2 * INNER:3 * INNER]).then_inc(up, 16)
                sp.dma_start(wo[:], one(a["wo"]).rearrange("(c p) n -> p c n", p=P)).then_inc(up, 16)
                sp.dma_start(w1[:], one(a["w1"])).then_inc(up, 16)
                sp.dma_start(w2[:], one(a["w2"]).rearrange("(c p) n -> p c n", p=P)).then_inc(up, 16)
                sp.dma_start(qks[:].rearrange("p c d -> p (c d)"), row(a["qk_scale"]).partition_broadcast(P)).then_inc(up, 16)
                sp.dma_start(b2[:], row(a["b2"]).partition_broadcast(P)).then_inc(up, 16)
                sp.dma_start(lng[:], one(a["ln_g"])).then_inc(up, 16)
                sp.dma_start(lnb[:], one(a["ln_b"])).then_inc(up, 16)
                sp.dma_start(b1[:].rearrange("p c k -> p (c k)"), one(a["b1"])).then_inc(up, 16)

        @block.gpsimd
        def _(pool):
            pool.memset(neg_half[:], -0.5).then_inc(const_set, 1)
            pool.memset(KT[:, :, 0:W], 0.0).then_inc(const_set, 1)
            pool.memset(hT[:, 0:W + 1], 0.0).then_inc(const_set, 1)
            pool.memset(fhT[:, :, 0:1], 0.0).then_inc(const_set, 1)
            pool.wait_ge(const_set, 4)
            with pool.Fori(0, DEPTH) as l:
                with pool.Fori(0, B) as b:
                    i = l * B + b
                    for step, n in ORDER:
                        if step == "norm":
                            pool.wait_ge(*ss_made(i, n + 1))
                            pool.tensor_tensor(rn[:, n, :], ss[:, n, :], neg_half[:], ALU.pow).then_inc(rn_made.sem, 1)
                        elif step == "rope":
                            pool.wait_ge(*qn_made(i, n + 1))
                            if n >= 2:
                                pool.wait_ge(*r_made(i, n - 1))
                            for o, x, s in swap_halves(t2[:, n % 2, :], qn[:, n % 2, :], sinq, n % 2):
                                last = pool.tensor_tensor(o, x, s, ALU.mult)
                            last.then_inc(t2_made.sem, 1)
                        elif step == "sum":
                            for h in range(2):
                                pool.wait_ge(*inv_made(i, 2 * n + h + 1))
                                v = pr[:, n, h, :].rearrange("p (g k) -> p g k", k=2 * W)
                                pool.tensor_tensor(v, v, bc(inv[:, n, h, :], 2, 2 * W), ALU.mult).then_inc(p_normed.sem, 1)
                with pool.Fori(0, B // FS) as b:
                    i = l * (B // FS) + b
                    pool.wait_ge(*fvar_made(i, 1))
                    pool.tensor_tensor(rstd[:], veps[:], neg_half[:, 0:FT], ALU.pow).then_inc(frstd_made.sem, 1)

        @block.scalar
        def _(act):
            act.wait_ge(const_set, 4)
            with act.Fori(0, DEPTH) as l:
                act.wait_ge(*fx_done(l * (B // FS), 0))
                with act.Fori(0, B) as b:
                    i = l * B + b
                    for step, n in ORDER:
                        if step == "x":
                            act.wait_ge(*tr_made(i, 0))
                            nc.scalar.copy(xs[:], X[:, bass.ds(b * HALVES, HALVES), :]).then_inc(xs_made.sem, 1)
                            act.wait_ge(*tr_made(i, 1))
                            act.wait_ge(*v_made(i, 0))
                            xv = tr_ps[0][:, 0:HALVES, :].rearrange("p t c -> p (t c)")
                            nc.scalar.copy(hT[0:64, W:W + T], xv[0:64, :]).then_inc(hT_made.sem, 1)
                            nc.scalar.copy(hT[64:128, W + 1:W + T], xv[64:128, 0:T - 1]).then_inc(tr_kept.sem, 1)
                        elif step == "proj":
                            act.wait_ge(*qk_made(i, n + 1))
                            if n >= 2:
                                act.wait_ge(*ss_made(i, n - 1))
                            nc.scalar.activation(sq[:, n % 2, :], qk_ps[n % 2][:], ACT.Square).then_inc(sq_made.sem, 1)
                        elif step == "v":
                            act.wait_ge(*v_made(i, n + 1))
                            if n == 0:
                                act.wait_ge(*o_made(i, 0))
                            nc.scalar.copy(V[:, n // 4, n // 2 % 2, (n % 2) * 512:(n % 2) * 512 + 512], o_ps[n % 2][:]) \
                                .then_inc(v_kept.sem, 1)
                        elif step == "qkT":
                            u = use_of["qkT", n]
                            act.wait_ge(*tr_made(i, u + 1))
                            if n == 0:
                                act.wait_ge(*s_made(i, 0))
                            q, t = n // 2, n % 2
                            nc.scalar.copy(QT[:, 2 * q:2 * q + 2, t * P:(t + 1) * P], tr_ps[u % 2][:, 0:2, :])
                            nc.scalar.copy(KT[:, 2 * q:2 * q + 2, W + t * P:W + (t + 1) * P], tr_ps[u % 2][:, 2:4, :]) \
                                .then_inc(tr_kept.sem, 1)
                        elif step == "shift":
                            for h in range(2):
                                act.wait_ge(*p_shifted(i, 2 * n + h + 1))
                                nc.scalar.activation(pr[:, n, h, :], pr[:, n, h, :], ACT.Exp).then_inc(p_exp.sem, 1)
                        elif step == "pT":
                            for h in range(2):
                                u = use_of["pT", 2 * n + h]
                                act.wait_ge(*tr_made(i, u + 1))
                                if h == 0:
                                    act.wait_ge(*o_made(i, 2 * n))
                                nc.scalar.copy(PT[:, n, h, :, :], tr_ps[u % 2][:]).then_inc(tr_kept.sem, 1)
                        elif step == "pv":
                            for j in range(2):
                                act.wait_ge(*o_made(i, 2 * n + j + 1))
                                if n == 0 and j == 0:
                                    act.wait_ge(*y_made(i, 0))
                                ov = OT[:, 4 * n:4 * n + 4, :].rearrange("p c (t j x) -> p c t j x", t=HALVES, j=2)
                                nc.scalar.copy(ov[:, :, :, j, :], o_ps[j][:].rearrange("p (c t x) -> p c t x", c=4, t=HALVES)) \
                                    .then_inc(o_kept.sem, 1)
                act.wait_ge(*x_made((l + 1) * B, 0))
                with act.Fori(0, B // FS) as b:
                    i = l * (B // FS) + b
                    act.wait_ge(*fT_made(i, 0))
                    nc.scalar.copy(fx[:], X[:, bass.ds(b * FT, FT), :]).then_inc(fx_made.sem, 1)
                    act.wait_ge(*fT_made(i, 1))
                    act.wait_ge(*fh_made(i, 0))
                    xv = tr_ps[0][:].rearrange("p (s t) c -> p s (t c)", s=FS)
                    nc.scalar.copy(fhT[0:64, :, :], xv[0:64]).then_inc(fT_kept.sem, 1)
                    nc.scalar.copy(fhT[64:128, :, 1:T], xv[64:128, :, 0:T - 1]).then_inc(fT_kept.sem, 1)
                    act.wait_ge(*fnT_made(i, 1))
                    act.wait_ge(*f1_made(i, 0))
                    act.wait_ge(*weights_in(l, 176))
                    nc.scalar.activation(xnT[:], tr_ps[0][:].rearrange("p t c -> p (t c)"), ACT.Identity,
                                         bias=lnb[:, 0:1], scale=lng[:, 0:1]).then_inc(fnT_kept.sem, 1)
                    for k, (f, n) in enumerate(FC):
                        act.wait_ge(*f1_made(i, k + 1))
                        nc.scalar.activation(gl[0:n, k, :], qk_ps[k % 2][0:n, :], ACT.Gelu,
                                             bias=b1[0:n, 1, k:k + 1]).then_inc(fgelu_made.sem, 1)

        @block.tensor
        def _(pe):
            pe.wait_ge(consts, CONSTS)
            pe.wait_ge(const_set, 4)
            mm = nc.tensor.matmul
            with pe.Fori(0, DEPTH) as l:
                with pe.Fori(0, B) as b:
                    i = l * B + b
                    pe.wait_ge(*weights_in(l, 176))
                    for step, n in ORDER:
                        if step == "x":
                            pe.wait_ge(*tr_kept(i, 0))
                            pe.wait_ge(*xs_made(i, 1))
                            for t in range(HALVES):
                                last = nc.tensor.transpose(tr_ps[0][:, t, :], xs[:, t, :], ident[:])
                            last.then_inc(tr_made.sem, 1)
                            pe.wait_ge(*hT_made(i, 1))
                            pe.wait_ge(*tr_kept(i, 1))
                        elif step == "proj":
                            if n >= 2:
                                pe.wait_ge(*qn_made(i, n - 1))
                            else:
                                pe.wait_ge(*qn_made(i, 0))
                                pe.wait_ge(*x_made(i, 0))
                            t = n % 2
                            mm(qk_ps[n % 2][:], hT[:, W + t * P:W + (t + 1) * P],
                               wqk[:, n // 2, :, :].rearrange("p c n -> p (c n)"), start=True, stop=True).then_inc(qk_made.sem, 1)
                        elif step == "v":
                            back, t, c = n // 4, n // 2 % 2, n % 2
                            if n >= 2:
                                pe.wait_ge(*v_kept(i, n - 1))
                            else:
                                pe.wait_ge(*o_kept(i, 0))
                            at = W * (1 - back) + t * P
                            mm(o_ps[c][:], hT[:, at:at + P], wv[:, c * 512:(c + 1) * 512], start=True, stop=True) \
                                .then_inc(v_made.sem, 1)
                        elif step == "qkT":
                            u = use_of["qkT", n]
                            pe.wait_ge(*r_made(i, n + 1))
                            pe.wait_ge(*tr_kept(i, u - 1))
                            for c in range(4):
                                last = nc.tensor.transpose(tr_ps[u % 2][:, c, :], qn[:, n % 2, c * P:(c + 1) * P], ident[:])
                            last.then_inc(tr_made.sem, 1)
                        elif step == "scores":
                            pe.wait_ge(*tr_kept(i, use_of["qkT", 4 * n + 3] + 1))
                            pe.wait_ge(*p_shifted(i, 2 * n))
                            for h in range(2):
                                mm(s_ps[h][:], identb[:], mask[:].rearrange("p c j k -> p (c j k)"),
                                   start=True, stop=False, skip_group_check=True)
                            for c in range(4):
                                for j in range(2):
                                    for ts in range(4):
                                        for h in range(2):
                                            w = 4 * (ts // 2) + 2 * j + ts % 2
                                            r = slice(64 * h, 64 * h + 64)
                                            last = mm(s_ps[h][32 * ts:32 * ts + 32, c * P + 64 * j:c * P + 64 * j + 64],
                                                      QT[r, 4 * n + c, W * w:W * w + W], KT[r, 4 * n + c, W * w:W * w + 2 * W],
                                                      start=False, stop=(c == 3 and j == 1), skip_group_check=True,
                                                      tile_position=(64 * h, 32 * ts))
                                            if c == 3 and j == 1 and ts == 3:
                                                last.then_inc(s_made.sem, 1)
                        elif step == "pT":
                            for h in range(2):
                                u = use_of["pT", 2 * n + h]
                                pe.wait_ge(*p_normed(i, 2 * n + h + 1))
                                pe.wait_ge(*tr_kept(i, u - 1))
                                for c in range(4):
                                    last = nc.tensor.transpose(tr_ps[u % 2][:, c, :], pr[:, n, h, c * P:(c + 1) * P], ident[:])
                                last.then_inc(tr_made.sem, 1)
                        elif step == "pv":
                            pe.wait_ge(*tr_kept(i, use_of["pT", 2 * n + 1] + 1))
                            pe.wait_ge(*(v_kept(i, 8) if n == 0 else o_kept(i, 2 * n)))
                            mm(o_ps[0][:, 0:1], identb[:], identb[:, 0:1], start=True, stop=True)
                            for j in range(2):
                                for c in range(4):
                                    for ts in range(4):
                                        for h in range(2):
                                            r = slice(64 * j, 64 * j + 64)
                                            g = (4 * n + c) * P + 64 * h
                                            last = mm(o_ps[j][64 * h:64 * h + 64, c * P + 32 * ts:c * P + 32 * ts + 32],
                                                      V[r, 1 - ts % 2, ts // 2, g:g + 64], PT[r, n, h, c, 32 * ts:32 * ts + 32],
                                                      start=True, stop=True, tile_position=(64 * j, 64 * h))
                                last.then_inc(o_made.sem, 1)
                        elif step == "out":
                            pe.wait_ge(*o_kept(i, 4))
                            pe.wait_ge(*qn_made(i, 8))
                            for t in range(HALVES):
                                for c in range(PAIRS):
                                    last = mm(qk_ps[0][:, t * P:(t + 1) * P], OT[:, c, t * P:(t + 1) * P], wo[:, c, :],
                                              start=(c == 0), stop=(c == PAIRS - 1))
                            last.then_inc(y_made.sem, 1)
                with pe.Fori(0, B // FS) as b:
                    i = l * (B // FS) + b
                    pe.wait_ge(*x_made((l + 1) * B, 0))
                    pe.wait_ge(*fx_made(i, 1))
                    pe.wait_ge(*fnT_kept(i, 0))
                    for t in range(FT):
                        last = nc.tensor.transpose(tr_ps[0][:, t, :], fx[:, t, :], ident[:])
                    last.then_inc(fT_made.sem, 1)
                    pe.wait_ge(*fT_kept(i, 2))
                    pe.wait_ge(*fxn_made(i, 0))
                    for t in range(FT):
                        last = nc.tensor.transpose(tr_ps[1][:, t, :], fhT[:, t // 2, (t % 2) * P:(t % 2) * P + P], ident[:])
                    last.then_inc(fh_made.sem, 1)
                    pe.wait_ge(*fxn_made(i, FT))
                    for t in range(FT):
                        last = nc.tensor.transpose(tr_ps[0][:, t, :], xn[:, t, :], ident[:])
                    last.then_inc(fnT_made.sem, 1)
                    pe.wait_ge(*fnT_kept(i, 1))
                    for k, (f, n) in enumerate(FC):
                        pe.wait_ge(*fhh_made(i, k - 1) if k >= 2 else fhh_made(i, 0))
                        mm(qk_ps[k % 2][0:n, :], w1[:, F + f:F + f + n], xnT[:], start=True, stop=True)
                        mm(s_ps[k % 2][0:n, :], w1[:, f:f + n], xnT[:], start=True, stop=True).then_inc(f1_made.sem, 1)
                    pe.wait_ge(*fx_done(i, 0))
                    pe.wait_ge(*fhh_made(i, NF))
                    for t in range(FT):
                        for k, (f, n) in enumerate(FC):
                            last = mm(o_ps[0][:, t * P:(t + 1) * P], hh[0:n, k, t * P:(t + 1) * P], w2[0:n, k, :],
                                      start=(k == 0), stop=(k == NF - 1))
                    last.then_inc(fy_made.sem, 1)
                pe.wait_ge(*fx_done((l + 1) * (B // FS), 0))
                mm(o_ps[0][:, 0:1], identb[:], identb[:, 0:1], start=True, stop=True).then_inc(ffn_done.sem, 1)

        @block.vector
        def _(dve):
            tt, ts_, red = nc.vector.tensor_tensor, nc.vector.tensor_scalar, nc.vector.tensor_reduce
            dve.wait_ge(consts, CONSTS)
            with dve.Fori(0, DEPTH) as l:
                dve.wait_ge(*weights_in(l, 176))
                for t in range(HALVES):
                    tt(cosq[:, t], cos0[:, t], qks[:], ALU.mult)
                    for half in range(2):
                        v = lambda ap: ap.rearrange("p c (z d) -> p c z d", z=2)
                        last = tt(v(sinq[:, t])[:, :, half, :], v(sin0[:, t])[:, :, half, :], v(qks[:])[:, :, 1 - half, :], ALU.mult)
                last.then_inc(tables_made.sem, 1)
                with dve.Fori(0, B) as b:
                    i = l * B + b
                    dve.wait_ge(*tables_made(l, 1))
                    link = Chain(dve, dve_step, i)
                    for step, n in ORDER:
                        if step == "norm":
                            dve.wait_ge(*sq_made(i, n + 1))
                            link(red(ss[:, n, :], head_groups(sq[:, n % 2, :]), op=ALU.add, axis=X_AXIS))
                            ts_(ss[:, n, :], ss[:, n, :], 1e-24, None, ALU.max).then_inc(ss_made.sem, 1)
                        elif step == "rope":
                            dve.wait_ge(*rn_made(i, n + 1))
                            if n >= 2:
                                dve.wait_ge(*tr_made(i, use_of["qkT", n - 2] + 1))
                            tt(head_groups(qn[:, n % 2, :]), head_groups(qk_ps[n % 2][:]), bc(rn[:, n, :], 2, D), ALU.mult) \
                                .then_inc(qn_made.sem, 1)
                            dve.wait_ge(*qn_made(i, n + 1))
                            v = lambda ap: ap.rearrange("p (c g d) -> p c g d", c=2, g=4)
                            link.free(tt(v(t1[:, n % 2, :]), v(qn[:, n % 2, :]), bc(cosq[:, n % 2], 2, 4), ALU.mult))
                        elif step == "add":
                            dve.wait_ge(*t2_made(i, n + 1))
                            dve.wait_ge(*dve_step(i, link.n))
                            tt(qn[:, n % 2, :], t1[:, n % 2, :], t2[:, n % 2, :], ALU.add).then_inc(r_made.sem, 1)
                        elif step == "shift":
                            for h in range(2):
                                dve.wait_ge(*s_made(i, 2 * n + h + 1))
                                v = lambda ap: ap.rearrange("p (g k) -> p g k", k=2 * W)
                                link(red(top[:, n, h, :], v(s_ps[h][:]), op=ALU.max, axis=X_AXIS))
                                tt(v(pr[:, n, h, :]), v(s_ps[h][:]), bc(top[:, n, h, :], 2, 2 * W), ALU.subtract) \
                                    .then_inc(p_shifted.sem, 1)
                        elif step == "sum":
                            for h in range(2):
                                dve.wait_ge(*p_exp(i, 2 * n + h + 1))
                                link(red(den[:, n, h, :], pr[:, n, h, :].rearrange("p (g k) -> p g k", k=2 * W), op=ALU.add, axis=X_AXIS))
                                nc.vector.reciprocal(inv[:, n, h, :], den[:, n, h, :]).then_inc(inv_made.sem, 1)
                        elif step == "out":
                            dve.wait_ge(*y_made(i, 1))
                            xv = X[:, bass.ds(b * HALVES, HALVES), :].rearrange("p t e -> p (t e)")
                            tt(xv, xv, qk_ps[0][:, 0:HALVES * E], ALU.add).then_inc(x_made.sem, 1)
                    assert link.n == DVE_A, link.n
                with dve.Fori(0, B // FS) as b:
                    i = l * (B // FS) + b
                    link = Chain(dve, fdve_step, i)
                    dve.wait_ge(*fh_made(i, 1))
                    for t in range(FT):
                        link(nc.vector.bn_stats(stats[:, t, :], tr_ps[1][:, t, :]))
                    for t in range(FT):
                        hold(nc.vector, scrap)
                        link(nc.vector.bn_aggr(mv[:, t, :], stats[:, t, :]))
                    ts_(veps[:], mv[:, :, 1], LN_EPS, None, ALU.add).then_inc(fvar_made.sem, 1)
                    dve.wait_ge(*frstd_made(i, 1))
                    for t in range(FT):
                        ts_(xn[:, t, :], tr_ps[1][:, t, :], mv[:, t, 0:1], rstd[:, t:t + 1], ALU.subtract, ALU.mult).then_inc(fxn_made.sem, 1)
                    for k, (f, n) in enumerate(FC):
                        dve.wait_ge(*fgelu_made(i, k + 1))
                        nc.vector.scalar_tensor_tensor(hh[0:n, k, :], s_ps[k % 2][0:n, :], b1[0:n, 0, k:k + 1], gl[0:n, k, :],
                                                       ALU.add, ALU.mult).then_inc(fhh_made.sem, 1)
                    dve.wait_ge(*fy_made(i, 1))
                    link(tt(yb[:], o_ps[0][:].rearrange("p (t e) -> p t e", e=E), bc(b2[:], 1, FT), ALU.add))
                    xv = X[:, bass.ds(b * FT, FT), :]
                    tt(xv, xv, yb[:], ALU.add).then_inc(fx_done.sem, 1)
                    assert link.n == DVE_F, link.n


def add_norm(nc, X0, X, stage):
    N = 8
    with Core(nc, stage) as m:
        h = m.sb("h", [N, E])
        neg_half = m.sb("neg_half", [N])
        scrap = m.sb("scrap", [1])
        stats, mv = m.sb("stats", [N, 6]), m.sb("mv", [N, 2])
        veps, rstd = m.sb("veps", [N]), m.sb("rstd", [N])
        const_set = m.sem("const_set")
        STEPS = 2 * N + 3
        (var_made, rstd_made, step_done), signals = m.signals(var_made=1, rstd_made=1, step_done=STEPS)
        block = m.block()

        @block.sync
        def _(sp):
            for signal in signals:
                sp.sem_inc(signal.sem, 1)

        @block.gpsimd
        def _(pool):
            pool.memset(neg_half[:], -0.5).then_inc(const_set, 1)
            pool.wait_ge(const_set, 1)
            with pool.Fori(0, TILES // N) as c:
                pool.wait_ge(*var_made(c, 1))
                pool.tensor_tensor(rstd[:], veps[:], neg_half[:], ALU.pow).then_inc(rstd_made.sem, 1)

        @block.vector
        def _(dve):
            with dve.Fori(0, TILES // N) as c:
                link = Chain(dve, step_done, c)
                link(nc.vector.tensor_tensor(h[:], X0[:, bass.ds(c * N, N), :], X[:, bass.ds(c * N, N), :], ALU.add))
                layer_norm(nc, dve, link, h, stats, mv, veps, rstd, scrap, N, var_made, rstd_made, c)
                link(nc.vector.tensor_tensor(X[:, bass.ds(c * N, N), :], h[:], bc(rstd[:], 2, E), ALU.mult))
                assert link.n == STEPS, link.n


def small_heads(nc, X, a, causal):
    H, D, HP = 16, 8, 32
    KV = 4 if causal else H
    G = H // 4
    QKV = (H + 2 * KV) * D
    QK = H + KV
    SCALE = 1.0 / float(D) ** 0.5
    with Core(nc, "causal" if causal else "rotary") as m:
        ident, identb = m.sb("ident", [P]), m.sb("identb", [P], BF16)
        w = m.sb("w", [QKV])
        w_out = m.sb("w_out", [E])
        aff = m.sb("aff", [4])
        cos, sin = m.sb("cos", [HALVES, D]), m.sb("sin", [HALVES, D])
        neg_half = m.sb("neg_half", [2 * QK])
        scrap = m.sb("scrap", [1])
        if causal:
            mask = m.sb("mask", [HALVES, T], BF16)
            maskT = m.sb("maskT", [HALVES, T], BF16)
            dmas = [(mask, "causal"), (maskT, "causal_t")]
            rows = []
        else:
            bias = m.sb("bias", [QKV])
            b_out = m.sb("b_out", [E])
            w_rad = m.sb("w_rad", [E])
            b_rad = m.sb("b_rad", [1])
            w_ln, b_ln = m.sb("w_ln", [D]), m.sb("b_ln", [D])
            dmas = []
            rows = [(bias, "rot_bias"), (b_out, "rot_b_out"), (w_rad, "rot_w_rad"), (b_rad, "rot_b_rad"),
                    (w_ln, "rot_w_ln"), (b_ln, "rot_b_ln")]
        pre = "cau" if causal else "rot"
        dmas += [(ident, "ident"), (identb, "identb"), (w, f"{pre}_w"), (w_out, f"{pre}_w_out"), (aff, f"{pre}_aff"),
                 (cos, f"{pre}_cos"), (sin, f"{pre}_sin")]
        xh = m.sb("xh", [HALVES, E])
        sqx = m.sb("sqx", [HALVES, E])
        stats, mv = m.sb("stats", [HALVES, 6]), m.sb("mv", [HALVES, 2])
        veps, rstd = m.sb("veps", [HALVES]), m.sb("rstd", [HALVES])
        xqT, xkT = m.sb("xqT", [T]), m.sb("xkT", [T])
        rad = m.sb("rad", [HALVES])
        qkv = m.sb("qkv", [HALVES, QKV])
        t1, t2 = m.sb("t1", [HALVES, QK * D]), m.sb("t2", [HALVES, QK * D])
        mean = m.sb("mean", [HALVES, QK])
        hvar = m.sb("hvar", [HALVES, QK])
        hrstd = m.sb("hrstd", [HALVES, QK])
        QK_pad = m.sb("QK_pad", [HALVES, 2, H, HP])
        V_pad = m.sb("V_pad", [HALVES, KV, HP])
        QT, KT, QmT = m.sb("QT", [G, T]), m.sb("KT", [G, T]), m.sb("QmT", [G, T])
        top = m.sb("top", [H, HALVES])
        PT = m.sb("PT", [3, HALVES, T])
        OT = m.sb("OT", [G, T])
        rec = m.sb("rec", [HALVES, H])
        att = m.sb("att", [HALVES, E])
        attT = m.sb("attT", [T])
        y = m.sb("y", [HALVES, E])

        s1_ps = [m.ps(f"s1_ps{i}", [HALVES, T]) for i in range(2)]
        s2_ps = [m.ps(f"s2_ps{i}", [HALVES, T]) for i in range(2)]
        o_ps = [m.ps(f"o_ps{i}", [512]) for i in range(2)]
        tr_ps = [m.ps(f"tr_ps{i}", [4, P]) for i in range(2)]

        USES = [("x", 0)] + [("qk", n) for n in range(4)] + [("qm", g) for g in range(G)] + [("o", 0), ("o", 1), ("att", 0)]
        use_of = {u: i for i, u in enumerate(USES)}
        TRU = len(USES)
        assert TRU % 2 == 0
        DVE_STEPS = 15 if causal else 39
        consts, const_set = m.sem("consts"), m.sem("const_set")
        CONSTS = 16 * (len(dmas) + len(rows))
        (var_made, rstd_made, xh_made, tr_made, tr_kept, xT_kept, qkv_made, qkv_kept, hvar_made, hrstd_made,
         pad_made, v_padded, s1_made, top_made, negm_made, s2_made, p_made, o_made, o_kept, att_made, y_made,
         var2_made, rstd2_made, x_made, step_done), signals = m.signals(
            var_made=1, rstd_made=1, xh_made=1, tr_made=TRU, tr_kept=TRU, xT_kept=1, qkv_made=1, qkv_kept=1,
            hvar_made=1, hrstd_made=1, pad_made=1, v_padded=1, s1_made=H, top_made=H, negm_made=G, s2_made=H,
            p_made=H, o_made=H, o_kept=G, att_made=2, y_made=1, var2_made=1, rstd2_made=1, x_made=1,
            step_done=DVE_STEPS)
        LAG = 5
        ORDER = []
        for h in range(H + LAG + 1):
            if h < H:
                ORDER.append(("s1", h))
                if h % 4 == 3:
                    ORDER.append(("qm", h // 4))
            if 0 <= h - LAG < H:
                ORDER.append(("s2", h - LAG))
            if h - LAG - 1 >= 0:
                ORDER.append(("pv", h - LAG - 1))
        block = m.block()

        @block.sync
        def _(sp):
            for signal in signals:
                sp.sem_inc(signal.sem, 1)
            for dst, name in dmas:
                sp.dma_start(dst[:], a[name]).then_inc(consts, 16)
            for dst, name in rows:
                sp.dma_start(dst[:], a[name].partition_broadcast(P)).then_inc(consts, 16)

        @block.gpsimd
        def _(pool):
            pool.memset(neg_half[:], -0.5).then_inc(const_set, 1)
            pool.memset(QK_pad[:], 0.0).then_inc(const_set, 1)
            pool.memset(V_pad[:], 0.0).then_inc(const_set, 1)
            pool.wait_ge(const_set, 3)
            pool.memset(QK_pad[:, :, 1, :, D:D + 1], 1.0).then_inc(const_set, 1)
            pool.memset(V_pad[:, :, :, D:D + 1], 1.0).then_inc(const_set, 1)
            power = lambda o, i, n: pool.tensor_tensor(o, i, neg_half[:, 0:n], ALU.pow)
            with pool.Fori(0, B) as b:
                pool.wait_ge(*var_made(b, 1))
                power(rstd[:], veps[:], HALVES).then_inc(rstd_made.sem, 1)
                if not causal:
                    pool.wait_ge(*hvar_made(b, 1))
                    power(hrstd[:].rearrange("p t h -> p (t h)"), hvar[:].rearrange("p t h -> p (t h)"), 2 * QK) \
                        .then_inc(hrstd_made.sem, 1)
                    pool.wait_ge(*var2_made(b, 1))
                    power(rstd[:], veps[:], HALVES).then_inc(rstd2_made.sem, 1)

        @block.scalar
        def _(act):
            act.wait_ge(consts, CONSTS)
            ident_fn = ACT.Identity
            with act.Fori(0, B) as b:
                act.wait_ge(*tr_made(b, 1))
                act.wait_ge(*qkv_made(b, 0))
                xT = tr_ps[0][:, 0:HALVES, :].rearrange("p t c -> p (t c)")
                nc.scalar.activation(xqT[:], xT, ident_fn, bias=aff[:, 1:2], scale=aff[:, 0:1])
                last = nc.scalar.activation(xkT[:], xT, ident_fn, bias=aff[:, 3:4], scale=aff[:, 2:3])
                last.then_inc(tr_kept.sem, 1)
                for n in range(4):
                    u = use_of["qk", n]
                    act.wait_ge(*tr_made(b, u + 1))
                    dst = (QT, KT)[n // 2]
                    nc.scalar.copy(dst[:, :, (n % 2) * P:(n % 2) * P + P], tr_ps[u % 2][:]).then_inc(tr_kept.sem, 1)
                for step, n in ORDER:
                    if step == "qm":
                        u = use_of["qm", n]
                        act.wait_ge(*tr_made(b, u + 1))
                        nc.scalar.copy(QmT[:, n, :], tr_ps[u % 2][:, 0:HALVES, :].rearrange("p t c -> p (t c)")) \
                            .then_inc(tr_kept.sem, 1)
                    elif step == "s2":
                        act.wait_ge(*s2_made(b, n + 1))
                        act.wait_ge(*o_made(b, max(n - 2, 0)))
                        nc.scalar.activation(PT[:, n % 3], s2_ps[n % 2][:], ACT.Exp, scale=SCALE).then_inc(p_made.sem, 1)
                    elif step == "pv" and n % 4 == 3:
                        g = n // 4
                        act.wait_ge(*o_made(b, n + 1))
                        act.wait_ge(*tr_made(b, 0))
                        nc.scalar.copy(OT[:, g, :], o_ps[g % 2][:, 0:T]).then_inc(o_kept.sem, 1)
                act.wait_ge(*tr_made(b, TRU))
                nc.scalar.copy(attT[:], tr_ps[(TRU - 1) % 2][:, 0:HALVES, :].rearrange("p t c -> p (t c)")) \
                    .then_inc(tr_kept.sem, 1)

        @block.tensor
        def _(pe):
            mm, flip = nc.tensor.matmul, nc.tensor.transpose
            pe.wait_ge(consts, CONSTS)
            pe.wait_ge(const_set, 5)
            with pe.Fori(0, B) as b:
                pe.wait_ge(*xh_made(b, 1))
                pe.wait_ge(*tr_kept(b, 0))
                for t in range(HALVES):
                    last = flip(tr_ps[0][:, t, :], xh[:, t, :], ident[:])
                last.then_inc(tr_made.sem, 1)
                pe.wait_ge(*tr_kept(b, 1))
                pe.wait_ge(*x_made(b, 0))
                for t in range(HALVES):
                    mm(s1_ps[t][:, 0, 0:E], xqT[:, t * P:(t + 1) * P], w[:, 0:E], start=True, stop=True)
                    last = mm(s1_ps[t][:, 1, 0:QKV - E], xkT[:, t * P:(t + 1) * P], w[:, E:QKV], start=True, stop=True)
                last.then_inc(qkv_made.sem, 1)
                pe.wait_ge(*pad_made(b, 1))
                for n in range(4):
                    u = use_of["qk", n]
                    pe.wait_ge(*tr_kept(b, max(u - 1, 0)))
                    for g in range(G):
                        last = flip(tr_ps[u % 2][:, g, :], QK_pad[:, n % 2, n // 2, 4 * g:4 * g + 4, :].rearrange("p h d -> p (h d)"), ident[:])
                    last.then_inc(tr_made.sem, 1)
                pe.wait_ge(*tr_kept(b, use_of["qk", 3] + 1))
                for step, n in ORDER:
                    g, r = n // 4, n % 4
                    if step == "s1":
                        pe.wait_ge(*top_made(b, max(n - 1, 0)))
                        if causal:
                            mm(s1_ps[n % 2][:].rearrange("p a k -> p (a k)"), identb[:], mask[:].rearrange("p a k -> p (a k)"),
                               start=True, stop=False, skip_group_check=True)
                        else:
                            pe.wait_ge(consts, CONSTS)
                        for t in range(HALVES):
                            last = mm(s1_ps[n % 2][:, t, :], QT[HP * r:HP * r + D, g, t * P:(t + 1) * P], KT[HP * r:HP * r + D, g, :],
                                      start=not causal, stop=True, skip_group_check=True, tile_position=(HP * r, 0))
                        last.then_inc(s1_made.sem, 1)
                    elif step == "qm":
                        u = use_of["qm", n]
                        pe.wait_ge(*negm_made(b, n + 1))
                        pe.wait_ge(*tr_kept(b, u - 1))
                        for t in range(HALVES):
                            last = flip(tr_ps[u % 2][:, t, :], QK_pad[:, t, 0, 4 * n:4 * n + 4, :].rearrange("p h d -> p (h d)"), ident[:])
                        last.then_inc(tr_made.sem, 1)
                    elif step == "s2":
                        if r == 0:
                            pe.wait_ge(*tr_kept(b, use_of["qm", g] + 1))
                        pe.wait_ge(*p_made(b, max(n - 1, 0)))
                        if causal:
                            mm(s2_ps[n % 2][:].rearrange("p a k -> p (a k)"), identb[:], maskT[:].rearrange("p a k -> p (a k)"),
                               start=True, stop=False, skip_group_check=True)
                        for t in range(HALVES):
                            last = mm(s2_ps[n % 2][:, t, :], KT[HP * r:HP * r + D + 1, g, t * P:(t + 1) * P], QmT[HP * r:HP * r + D + 1, g, :],
                                      start=not causal, stop=True, skip_group_check=True, tile_position=(HP * r, 0))
                        last.then_inc(s2_made.sem, 1)
                    elif step == "pv":
                        pe.wait_ge(*p_made(b, n + 1))
                        if r == 0:
                            pe.wait_ge(*o_kept(b, max(g - 1, 0)))
                            if n == 0:
                                pe.wait_ge(*v_padded(b, 1))
                        for t in range(HALVES):
                            last = mm(o_ps[g % 2][HP * r:HP * r + HP, 0:T], V_pad[:, t, n * KV // H, :], PT[:, n % 3, t, :],
                                      start=(t == 0), stop=(t == 1), skip_group_check=True, tile_position=(0, HP * r))
                        last.then_inc(o_made.sem, 1)
                for t in range(HALVES):
                    u = use_of["o", t]
                    if t == 0:
                        pe.wait_ge(*o_kept(b, G))
                    pe.wait_ge(*tr_kept(b, u - 1))
                    for g in range(G):
                        last = flip(tr_ps[u % 2][:, g, :], OT[:, g, t * P:(t + 1) * P], ident[:])
                    last.then_inc(tr_made.sem, 1)
                u = use_of["att", 0]
                pe.wait_ge(*att_made(b, 2))
                for t in range(HALVES):
                    last = flip(tr_ps[u % 2][:, t, :], att[:, t, :], ident[:])
                last.then_inc(tr_made.sem, 1)
                pe.wait_ge(*tr_kept(b, TRU))
                for t in range(HALVES):
                    last = mm(s1_ps[0][:, t, 0:E], attT[:, t * P:(t + 1) * P], w_out[:], start=True, stop=True)
                last.then_inc(y_made.sem, 1)

        @block.vector
        def _(dve):
            tt, ts, red = nc.vector.tensor_tensor, nc.vector.tensor_scalar, nc.vector.tensor_reduce
            dve.wait_ge(consts, CONSTS)
            dve.wait_ge(const_set, 5)
            with dve.Fori(0, B) as b:
                link = Chain(dve, step_done, b)
                xv = X[:, bass.ds(b * HALVES, HALVES), :]
                if causal:
                    link(tt(sqx[:], xv, xv, ALU.mult))
                    link(red(mv[:, :, 0], sqx[:], op=ALU.add, axis=X_AXIS))
                    ts(veps[:], mv[:, :, 0], 1.0 / E, LN_EPS, ALU.mult, ALU.add).then_inc(var_made.sem, 1)
                    dve.wait_ge(*rstd_made(b, 1))
                    tt(xh[:], xv, bc(rstd[:], 2, E), ALU.mult).then_inc(xh_made.sem, 1)
                else:
                    link(nc.vector.tensor_copy(xh[:], xv))
                    layer_norm(nc, dve, link, xh, stats, mv, veps, rstd, scrap, HALVES, var_made, rstd_made, b)
                    tt(xh[:], xh[:], bc(rstd[:], 2, E), ALU.mult).then_inc(xh_made.sem, 1)
                    link(tt(sqx[:], xv, bc(w_rad[:], 1, HALVES), ALU.mult))
                    link(red(rad[:], sqx[:], op=ALU.add, axis=X_AXIS))
                    link(ts(rad[:], rad[:], b_rad[:, 0:1], None, ALU.add))
                    link(ts(rad[:], rad[:], 0.01, 0.5, ALU.mult, ALU.max))
                    link(ts(rad[:], rad[:], 2.0, None, ALU.min))
                dve.wait_ge(*qkv_made(b, 1))
                dve.wait_ge(*s1_made(b, 0))
                for t in range(HALVES):
                    for lo, hi, o in ((0, E, 0), (E, QKV, 1)):
                        src = s1_ps[t][:, o, 0:hi - lo]
                        if causal:
                            link.free(nc.vector.tensor_copy(qkv[:, t, lo:hi], src))
                        else:
                            link.free(tt(qkv[:, t, lo:hi], src, bias[:, lo:hi], ALU.add))
                dve.wait_ge(*step_done(b, link.n))
                dve.wait_ge(*o_made(b, 0))
                heads = lambda ap, n: ap.rearrange("p t (h d) -> p t h d", h=n)
                nc.vector.tensor_copy(V_pad[:, :, :, 0:D], heads(qkv[:, :, QK * D:QKV], KV)).then_inc(v_padded.sem, 1)
                qk = qkv[:, :, 0:QK * D]
                for t in range(HALVES):
                    link.free(tt(t1[:, t].rearrange("p (h d) -> p h d", h=QK), qk[:, t].rearrange("p (h d) -> p h d", h=QK),
                                 bc(cos[:, t], 1, QK), ALU.mult))
                    for z in range(2):
                        if causal:
                            v = lambda ap: ap.rearrange("p (h z d) -> p h z d", h=QK, z=2)
                            s = sin[:, t].rearrange("p (z d) -> p z d", z=2)[:, z]
                            link.free(tt(v(t2[:, t])[:, :, z], v(qk[:, t])[:, :, 1 - z], bc(s, 1, QK), ALU.mult))
                        else:
                            v = lambda ap: ap.rearrange("p (h d z) -> p h d z", h=QK, z=2)
                            s = sin[:, t].rearrange("p (d z) -> p d z", z=2)[:, :, z]
                            link.free(tt(v(t2[:, t])[:, :, :, z], v(qk[:, t])[:, :, :, 1 - z], bc(s, 1, QK), ALU.mult))
                dve.wait_ge(*step_done(b, link.n))
                dve.wait_ge(*tr_made(b, 0))
                if causal:
                    tt(QK_pad[:, :, 0, :, 0:D], heads(t1[:, :, 0:E], H), heads(t2[:, :, 0:E], H), ALU.add)
                    for t in range(HALVES):
                        v = lambda ap: bc(ap[:, t, E:QK * D].rearrange("p (h d) -> p h d", h=KV), 2, H // KV)
                        last = tt(QK_pad[:, t, 1, :, 0:D].rearrange("p (h r) d -> p h r d", h=KV), v(t1), v(t2), ALU.add)
                    last.then_inc(pad_made.sem, 1)
                else:
                    link(tt(t1[:], t1[:], t2[:], ALU.add))
                    link(tt(t1[:], t1[:], bc(rad[:], 2, QK * D), ALU.mult))
                    th = heads(t1[:], QK)
                    link(red(mean[:], th, op=ALU.add, axis=X_AXIS))
                    link(ts(mean[:], mean[:], 1.0 / D, None, ALU.mult))
                    link(tt(th, th, bc(mean[:], 3, D), ALU.subtract))
                    link(tt(t2[:], t1[:], t1[:], ALU.mult))
                    link(red(hvar[:], heads(t2[:], QK), op=ALU.add, axis=X_AXIS))
                    ts(hvar[:], hvar[:], 1.0 / D, LN_EPS, ALU.mult, ALU.add).then_inc(hvar_made.sem, 1)
                    dve.wait_ge(*hrstd_made(b, 1))
                    link(tt(th, th, bc(hrstd[:], 3, D), ALU.mult))
                    flat = t1[:].rearrange("p t (h d) -> p (t h) d", h=QK)
                    link(tt(flat, flat, bc(w_ln[:], 1, 2 * QK), ALU.mult))
                    tt(QK_pad[:].rearrange("p t c h d -> p (t c h) d")[:, :, 0:D], flat, bc(b_ln[:], 1, 2 * QK), ALU.add) \
                        .then_inc(pad_made.sem, 1)
                for step, n in ORDER:
                    if step == "s1":
                        dve.wait_ge(*s1_made(b, n + 1))
                        red(top[:, n, :], s1_ps[n % 2][:], op=ALU.max, axis=X_AXIS).then_inc(top_made.sem, 1)
                    elif step == "qm":
                        dve.wait_ge(*top_made(b, 4 * n + 4))
                        ts(QK_pad[:, :, 0, 4 * n:4 * n + 4, D], top[:, 4 * n:4 * n + 4, :].rearrange("p h t -> p t h"), -1.0, None, ALU.mult) \
                            .then_inc(negm_made.sem, 1)
                for t in range(HALVES):
                    u = use_of["o", t]
                    dve.wait_ge(*tr_made(b, u + 1))
                    o = tr_ps[u % 2][:].rearrange("p g (r d) -> p (g r) d", d=HP)
                    link(nc.vector.reciprocal(rec[:, t, :], o[:, :, D]))
                    tt(att[:, t].rearrange("p (h d) -> p h d", d=D), o[:, :, 0:D], bc(rec[:, t, :], 2, D), ALU.mult) \
                        .then_inc(att_made.sem, 1)
                    dve.wait_ge(*att_made(b, t + 1))
                    nc.vector.memset(scrap[:], 0.0).then_inc(tr_kept.sem, 1)
                dve.wait_ge(*y_made(b, 1))
                yv = s1_ps[0][:, :, 0:E]
                if causal:
                    link(tt(y[:], yv, xv, ALU.add))
                    ts(xv, y[:], 100.0, -100.0, ALU.min, ALU.max).then_inc(x_made.sem, 1)
                else:
                    link(tt(y[:], yv, bc(b_out[:], 1, HALVES), ALU.add))
                    link(tt(y[:], y[:], xv, ALU.add))
                    layer_norm(nc, dve, link, y, stats, mv, veps, rstd, scrap, HALVES, var2_made, rstd2_made, b)
                    tt(xv, y[:], bc(rstd[:], 2, E), ALU.mult).then_inc(x_made.sem, 1)
                dve.wait_ge(*x_made(b, 1))
                assert link.n == DVE_STEPS, link.n


def experts(nc, X, a):
    N, F = 8, 256
    FK = F // P
    FS = 2
    FT = FS * HALVES
    TURNS = B // FS
    with Core(nc, "moe") as m:
        ident = m.sb("ident", [P])
        w_r = m.sb("w_r", [N])
        w_g, w_u = m.sb("w_g", [N, F]), m.sb("w_u", [N, F])
        w_d = m.sb("w_d", [N, FK, E])
        g2 = m.sb("g2", [1])
        lower = m.sb("lower", [N, N])
        neg_half = m.sb("neg_half", [FT])
        sqx, xh = m.sb("sqx", [FT, E]), m.sb("xh", [FT, E])
        ssq, veps, rstd = m.sb("ssq", [FT]), m.sb("veps", [FT]), m.sb("rstd", [FT])
        xT = m.sb("xT", [FT * P])
        prob, top, den = m.sb("prob", [FT, N]), m.sb("top", [FT]), m.sb("den", [FT])
        cmp1, cmp2 = m.sb("cmp1", [FT, N, N]), m.sb("cmp2", [FT, N, N])
        rank, gate = m.sb("rank", [FT, N]), m.sb("gate", [FT, N])
        act_g = m.sb("act_g", [2, FT * P])
        hid = m.sb("hid", [2, FK, FT * P])
        acc = m.sb("acc", [FT, E])
        g_ps = [m.ps(f"g_ps{i}", [FT * P]) for i in range(2)]
        u_ps = [m.ps(f"u_ps{i}", [FT * P]) for i in range(2)]
        d_ps = [m.ps(f"d_ps{i}", [FT, E]) for i in range(2)]
        tr_ps = m.ps("tr_ps", [FT, P])
        r_ps = m.ps("r_ps", [FT, N])
        consts, const_set = m.sem("consts"), m.sem("const_set")
        STEPS = 17 + (FT - 1) * N
        (var_made, rstd_made, xh_made, xT_made, xT_kept, route_made, shift_made, exp_made, gu_made, silu_made,
         hid_made, down_made, added, x_made, step_done), signals = m.signals(
            var_made=1, rstd_made=1, xh_made=1, xT_made=1, xT_kept=1, route_made=1, shift_made=1, exp_made=1,
            gu_made=N * FK, silu_made=N * FK, hid_made=N * FK, down_made=N, added=N, x_made=1, step_done=STEPS)
        dmas = [(ident, "ident"), (w_r, "moe_w_r"), (g2, "moe_g2")]
        block = m.block()

        @block.sync
        def _(sp):
            for signal in signals:
                sp.sem_inc(signal.sem, 1)
            for dst, name in dmas:
                sp.dma_start(dst[:], a[name]).then_inc(consts, 16)
            sp.dma_start(w_g[:], a["moe_w_g"].rearrange("e p f -> p e f")).then_inc(consts, 16)
            sp.dma_start(w_u[:], a["moe_w_u"].rearrange("e p f -> p e f")).then_inc(consts, 16)
            sp.dma_start(w_d[:], a["moe_w_d"].rearrange("e (k p) n -> p e k n", p=P)).then_inc(consts, 16)
            sp.dma_start(lower[:].rearrange("p a b -> p (a b)"), a["moe_lower"].partition_broadcast(P)).then_inc(consts, 16)

        @block.gpsimd
        def _(pool):
            pool.memset(neg_half[:], -0.5).then_inc(const_set, 1)
            pool.wait_ge(const_set, 1)
            with pool.Fori(0, TURNS) as c:
                pool.wait_ge(*var_made(c, 1))
                pool.tensor_tensor(rstd[:], veps[:], neg_half[:], ALU.pow).then_inc(rstd_made.sem, 1)

        @block.scalar
        def _(act):
            act.wait_ge(consts, 112)
            with act.Fori(0, TURNS) as c:
                act.wait_ge(*xT_made(c, 1))
                act.wait_ge(*down_made(c, 0))
                nc.scalar.activation(xT[:], tr_ps[:].rearrange("p t c -> p (t c)"), ACT.Copy, scale=g2[:, 0:1]) \
                    .then_inc(xT_kept.sem, 1)
                act.wait_ge(*shift_made(c, 1))
                nc.scalar.activation(prob[:], prob[:], ACT.Exp).then_inc(exp_made.sem, 1)
                for n in range(N * FK):
                    act.wait_ge(*gu_made(c, n + 1))
                    act.wait_ge(*hid_made(c, max(n - 1, 0)))
                    nc.scalar.activation(act_g[:, n % 2, :], g_ps[n % 2][:], ACT.Silu).then_inc(silu_made.sem, 1)

        @block.tensor
        def _(pe):
            mm = nc.tensor.matmul
            pe.wait_ge(consts, 112)

            def down(c, e):
                pe.wait_ge(*hid_made(c, FK * e + FK))
                pe.wait_ge(*added(c, max(e - 1, 0)))
                for t in range(FT):
                    for k in range(FK):
                        last = mm(d_ps[e % 2][:, t, :], hid[:, e % 2, k, t * P:(t + 1) * P], w_d[:, e, k, :],
                                  start=(k == 0), stop=(k == FK - 1))
                last.then_inc(down_made.sem, 1)

            with pe.Fori(0, TURNS) as c:
                pe.wait_ge(*xh_made(c, 1))
                pe.wait_ge(*xT_kept(c, 0))
                for t in range(FT):
                    last = nc.tensor.transpose(tr_ps[:, t, :], xh[:, t, :], ident[:])
                last.then_inc(xT_made.sem, 1)
                pe.wait_ge(*xT_kept(c, 1))
                for t in range(FT):
                    last = mm(r_ps[:, t, :], xT[:, t * P:(t + 1) * P], w_r[:], start=True, stop=True)
                last.then_inc(route_made.sem, 1)
                for e in range(N):
                    for k in range(FK):
                        n = FK * e + k
                        pe.wait_ge(*hid_made(c, max(n - 1, 0)))
                        mm(g_ps[n % 2][:], w_g[:, e, k * P:(k + 1) * P], xT[:], start=True, stop=True)
                        mm(u_ps[n % 2][:], w_u[:, e, k * P:(k + 1) * P], xT[:], start=True, stop=True).then_inc(gu_made.sem, 1)
                    if e:
                        down(c, e - 1)
                down(c, N - 1)

        @block.vector
        def _(dve):
            tt, ts, red = nc.vector.tensor_tensor, nc.vector.tensor_scalar, nc.vector.tensor_reduce
            dve.wait_ge(consts, 112)

            def add_expert(c, link, e):
                dve.wait_ge(*down_made(c, e + 1))
                for t in range(FT):
                    if e == 0:
                        ins = ts(acc[:, t, :], d_ps[0][:, t, :], gate[:, t, e:e + 1], None, ALU.mult)
                    else:
                        ins = nc.vector.scalar_tensor_tensor(acc[:, t, :], d_ps[e % 2][:, t, :], gate[:, t, e:e + 1], acc[:, t, :],
                                                             ALU.mult, ALU.add)
                    if t == FT - 1:
                        ins.then_inc(added.sem, 1)
                    else:
                        link.free(ins)
                dve.wait_ge(*added(c, e + 1))

            with dve.Fori(0, TURNS) as c:
                link = Chain(dve, step_done, c)
                xv = X[:, bass.ds(c * FT, FT), :]
                link(tt(sqx[:], xv, xv, ALU.mult))
                link(red(ssq[:], sqx[:], op=ALU.add, axis=X_AXIS))
                ts(veps[:], ssq[:], 1.0 / E, LN_EPS, ALU.mult, ALU.add).then_inc(var_made.sem, 1)
                dve.wait_ge(*rstd_made(c, 1))
                tt(xh[:], xv, bc(rstd[:], 2, E), ALU.mult).then_inc(xh_made.sem, 1)
                dve.wait_ge(*route_made(c, 1))
                link(red(top[:], r_ps[:], op=ALU.max, axis=X_AXIS))
                tt(prob[:], r_ps[:], bc(top[:], 2, N), ALU.subtract).then_inc(shift_made.sem, 1)
                dve.wait_ge(*exp_made(c, 1))
                link(red(den[:], prob[:], op=ALU.add, axis=X_AXIS))
                link(nc.vector.reciprocal(den[:], den[:]))
                link(tt(prob[:], prob[:], bc(den[:], 2, N), ALU.mult))
                other, own = bc(prob[:], 2, N), bc(prob[:], 3, N)
                link(tt(cmp1[:], other, own, ALU.is_gt))
                link(tt(cmp2[:], other, own, ALU.is_equal))
                link(tt(cmp2[:], cmp2[:], bc(lower[:], 1, FT), ALU.mult))
                link(tt(cmp1[:], cmp1[:], cmp2[:], ALU.add))
                link(red(rank[:], cmp1[:], op=ALU.add, axis=X_AXIS))
                link(ts(rank[:], rank[:], 2.0, None, ALU.is_lt))
                link(tt(gate[:], prob[:], rank[:], ALU.mult))
                link(red(den[:], gate[:], op=ALU.add, axis=X_AXIS))
                link(nc.vector.reciprocal(den[:], den[:]))
                link(tt(gate[:], gate[:], bc(den[:], 2, N), ALU.mult))
                for e in range(N):
                    for k in range(FK):
                        n = FK * e + k
                        dve.wait_ge(*silu_made(c, n + 1))
                        dve.wait_ge(*down_made(c, max(e - 1, 0)))
                        tt(hid[:, e % 2, k, :], act_g[:, n % 2, :], u_ps[n % 2][:], ALU.mult).then_inc(hid_made.sem, 1)
                    if e:
                        add_expert(c, link, e - 1)
                add_expert(c, link, N - 1)
                link(tt(acc[:], acc[:], xv, ALU.add))
                ts(xv, acc[:], 100.0, -100.0, ALU.min, ALU.max).then_inc(x_made.sem, 1)
                dve.wait_ge(*x_made(c, 1))
                assert link.n == STEPS, link.n


def build(nc, a, out):
    with Core(nc, "all") as m:
        X = m.sb("X", [TILES, E])
        X0 = m.sb("X0", [TILES, E])
        load_x(nc, a["x"], X)
        if 1 in STAGES:
            head_mixer(nc, X, a["ident"], None, a["mix_mask"], a["mix_w"], a["mix_bias"], a["inv_count"], a["count"])
        if 2 in STAGES:
            layer_stack(nc, X, X0, a)
            add_norm(nc, X0, X, "norm_stack")
        if 3 in STAGES:
            small_heads(nc, X, a, causal=False)
        if 4 in STAGES:
            copy_x(nc, X, X0)
            small_heads(nc, X, a, causal=True)
            experts(nc, X, a)
            add_norm(nc, X0, X, "norm_moe")
        store_x(nc, X, out)


def kernel(**inputs):
    import numpy as np
    import ml_dtypes
    import concourse.bacc as bacc
    from concourse.bass_utils import run_bass_kernel_spmd

    f = lambda n: np.asarray(inputs[n])
    a = {"x": f("L0_attn_y_de").reshape(B * T, E), "ident": np.eye(P, dtype=np.float32)}
    w = np.zeros((E, 3, 16, 8), np.float32)
    for j, n in enumerate("qkv"):
        for h in range(16):
            w[8 * h:8 * h + 8, j, h, :] = f(f"L0_attn_W{n}").T
    a["mix_w"] = w.reshape(E, 3 * E)
    a["mix_bias"] = np.concatenate([np.tile(f(f"L0_attn_b{n}"), 16) for n in "qkv"])
    t = np.arange(T)[:, None]
    a["mix_mask"] = (np.arange(E)[None, :] < t).astype(np.float32).reshape(HALVES, P, E).transpose(1, 0, 2).copy()
    a["inv_count"] = (1.0 / np.arange(1, 17)).astype(np.float32)
    a["count"] = np.arange(1, 17).astype(np.float32)

    a["identb"] = np.eye(P).astype(ml_dtypes.bfloat16)
    W = 32
    rows, keys = np.arange(P), np.arange(2 * W)
    q = rows % W
    win = np.zeros((P, 4, 2, 2 * W))
    for j in range(2):
        bad = (keys[None, :] < q[:, None]) | (keys[None, :] > q[:, None] + W)
        bad |= (rows[:, None] < W) & (j == 0) & (keys[None, :] < W)
        win[:, :, j, :] = np.where(bad, MASKED, 0.0)[:, None, :]
    a["win_mask"] = win.astype(ml_dtypes.bfloat16)
    half = np.arange(0, 64, 2, dtype=np.float64)
    freqs = (np.arange(T, dtype=np.float32)[:, None] * (1.0 / 10000.0 ** (half / 64)).astype(np.float32)[None, :]).astype(np.float64)
    base = (half + 0.4 * 64) / (1.4 * 64)
    scale = base[None, :] ** ((np.arange(T) - T // 2) / 16)[:, None]
    two = lambda x: np.concatenate([x, x], 1)
    cos, scale = two(np.cos(freqs)), two(scale)
    sin = np.concatenate([-np.sin(freqs), np.sin(freqs)], 1)
    tok = lambda x: np.stack(x, 1).reshape(HALVES, P, len(x), -1).transpose(1, 0, 2, 3).astype(np.float32)
    a["cos0"] = tok([cos * scale * 8.0, cos / scale])
    a["sin0"] = tok([sin * scale * 8.0, sin / scale])
    F, FP = 341, 384
    a["wqkv"], a["wo"], a["w1"] = f("L0_ffn_Wqkv"), f("L0_ffn_Wo"), f("L0_ffn_W1")
    w2 = np.zeros((6, FP, E), np.float32)
    w2[:, :F] = f("L0_ffn_W2")
    b1 = np.zeros((6, 2, FP), np.float32)
    b1[:, :, :F] = f("L0_ffn_b1").reshape(6, 2, F)
    a["w2"], a["b1"], a["b2"] = w2, b1.reshape(6, 2, 3, P).transpose(0, 3, 1, 2).reshape(6, P, 6), f("L0_ffn_b2")
    a["qk_scale"] = np.concatenate([f("L0_ffn_q_scale"), f("L0_ffn_k_scale")], 1)
    a["ln_g"], a["ln_b"] = f("L0_ffn_ln_g")[:, :, None], f("L0_ffn_ln_b")[:, :, None]

    mel = 2595.0 * np.log10(1.0 + 4000.0 / 200.0)
    fb = 200.0 * (10.0 ** (np.linspace(0.0, mel, 4) / 2595.0) - 1.0) / 1000.0
    ang = (np.arange(T, dtype=np.float32)[:, None] * fb.astype(np.float32)[None, :]).astype(np.float64)
    pairs = lambda x, y: np.stack([x, y], -1).reshape(T, -1)
    halves = lambda x: x.reshape(HALVES, P, -1).transpose(1, 0, 2).astype(np.float32)
    a["rot_cos"], a["rot_sin"] = halves(pairs(np.cos(ang), np.cos(ang))), halves(pairs(-np.sin(ang), np.sin(ang)))
    a["rot_w"] = np.concatenate([f("L1_attn_q_w"), f("L1_attn_kv_w")], 1)
    a["rot_bias"] = np.concatenate([f("L1_attn_q_b"), f("L1_attn_kv_b")])
    a["rot_w_out"], a["rot_b_out"] = f("L1_attn_out_w"), f("L1_attn_out_b")
    a["rot_w_rad"], a["rot_b_rad"] = f("L1_attn_rh_w")[:, 0], f("L1_attn_rh_b")
    a["rot_w_ln"], a["rot_b_ln"] = f("L1_attn_ln_w"), f("L1_attn_ln_b")
    a["rot_aff"] = np.stack([f(f"L1_attn_{n}") for n in ("qn_w", "qn_b", "kvn_w", "kvn_b")], 1)
    ang = (np.arange(T, dtype=np.float32)[:, None] * (1.0 / 10000.0 ** (np.arange(0, 8, 2) / 8)).astype(np.float32)[None, :]).astype(np.float64)
    a["cau_cos"] = halves(np.concatenate([np.cos(ang), np.cos(ang)], 1))
    a["cau_sin"] = halves(np.concatenate([-np.sin(ang), np.sin(ang)], 1))
    a["cau_w"] = np.concatenate([f(f"L1_ffn_W{n}") for n in "qkv"], 1)
    a["cau_w_out"] = f("L1_ffn_Wo")
    g1, zero = f("L1_ffn_ln1_w"), np.zeros(E, np.float32)
    a["cau_aff"] = np.stack([g1, zero, g1, zero], 1)
    t = np.arange(T)
    see = np.where(t[None, :] <= t[:, None], 0.0, MASKED)
    fold = lambda x: x.reshape(HALVES, P, T).transpose(1, 0, 2).astype(ml_dtypes.bfloat16)
    a["causal"], a["causal_t"] = fold(see), fold(see.T)
    a["moe_w_r"], a["moe_g2"] = f("L1_ffn_Wr"), f("L1_ffn_ln2_w")[:, None]
    a["moe_w_g"], a["moe_w_u"], a["moe_w_d"] = f("L1_ffn_Wg"), f("L1_ffn_Wu"), f("L1_ffn_Wd")
    a["moe_lower"] = (np.arange(8)[None, :] < np.arange(8)[:, None]).astype(np.float32).reshape(-1)

    nc = bacc.Bacc("TRN2", target_bir_lowering=False, num_devices=1)
    arrays, aps = {}, {}
    for n, v in a.items():
        v = np.ascontiguousarray(v)
        arrays[f"in_{n}"] = v
        aps[n] = nc.dram_tensor(f"in_{n}", v.shape, mybir.dt.from_np(v.dtype), kind="ExternalInput").ap()
    out = nc.dram_tensor("out_x", (B * T, E), F32, kind="ExternalOutput").ap()
    build(nc, aps, out)
    r = run_bass_kernel_spmd(nc, [arrays], core_ids=[0])
    return np.asarray(r.results[0]["out_x"]).reshape(B, T, E)
```

```python
from contextlib import ExitStack

import concourse.bass as bass
from concourse import mybir

ALU = mybir.AluOpType
ACT = mybir.ActivationFunctionType
F32 = mybir.dt.float32
BF16 = mybir.dt.bfloat16
X_AXIS = mybir.AxisListType.X

P = 128
B, T, E = 16, 256, 128
HALVES = T // P
TILES = B * HALVES
LN_EPS = 1e-5
MASKED = -1e30
STAGES = (1, 2, 3, 4)
DEPTH = 6


class Core:

    def __init__(self, nc, stage):
        self.nc, self.stage, self.ctx = nc, stage, ExitStack()

    def __enter__(self):
        return self

    def __exit__(self, *a):
        return self.ctx.__exit__(*a)

    def sb(self, name, shape, dt=F32):
        return self.ctx.enter_context(self.nc.sbuf_tensor(f"{self.stage}_{name}", [P] + list(shape), dt))

    def ps(self, name, shape, dt=F32):
        return self.ctx.enter_context(self.nc.psum_tensor(f"{self.stage}_{name}", [P] + list(shape), dt))

    def sem(self, name):
        return self.ctx.enter_context(self.nc.semaphore(f"{self.stage}_{name}"))

    def signals(self, **per_turn):
        made = [Signal(self.sem(n), k) for n, k in per_turn.items()]
        return made, made

    def block(self):
        return self.ctx.enter_context(self.nc.Block())


class Signal:

    def __init__(self, sem, per_turn):
        self.sem, self.per_turn, self.start = sem, per_turn, per_turn + 1

    def __call__(self, turn, k):
        return self.sem, turn * self.per_turn + (self.start + k)


class Chain:

    def __init__(self, eng, ends, turn):
        self.eng, self.ends, self.turn, self.n = eng, ends, turn, 0

    def __call__(self, ins):
        self.free(ins)
        self.eng.wait_ge(*self.ends(self.turn, self.n))

    def free(self, ins):
        self.n += 1
        ins.then_inc(self.ends.sem, 1)


def hold(eng, scrap):
    eng.memset(scrap[:], 0.0)


def bc(ap, axis, n):
    ap = ap.unsqueeze(axis)
    return ap.broadcast_to([n if i == axis else d for i, d in enumerate(ap.shape)])


def layer_norm(nc, dve, link, h, stats, mv, veps, rstd, scrap, n, var_made, rstd_made, turn):
    for j in range(n):
        link.free(nc.vector.bn_stats(stats[:, j, :], h[:, j, :]))
    dve.wait_ge(*link.ends(turn, link.n))
    hold(nc.vector, scrap)
    for j in range(n):
        link.free(nc.vector.bn_aggr(mv[:, j, :], stats[:, j, :]))
    dve.wait_ge(*link.ends(turn, link.n))
    nc.vector.tensor_scalar(veps[:], mv[:, :, 1], LN_EPS, None, ALU.add).then_inc(var_made.sem, 1)
    link(nc.vector.tensor_tensor(h[:], h[:], bc(mv[:, :, 0], 2, E), ALU.subtract))
    dve.wait_ge(*rstd_made(turn, 1))


def load_x(nc, x_in, X):
    with Core(nc, "load") as m:
        landed = m.sem("landed")
        block = m.block()

        @block.sync
        def _(sp):
            sp.dma_start(X[:], x_in.rearrange("(i p) e -> p i e", p=P)).then_inc(landed, 16)
            sp.wait_ge(landed, 16)


def copy_x(nc, X, X0):
    with Core(nc, "keep") as m:
        kept = m.sem("kept")
        block = m.block()

        @block.sync
        def _(sp):
            sp.dma_start(X0[:], X[:]).then_inc(kept, 16)
            sp.wait_ge(kept, 16)


def store_x(nc, X, out):
    with Core(nc, "store") as m:
        stored = m.sem("stored")
        block = m.block()

        @block.sync
        def _(sp):
            sp.dma_start(out.rearrange("(i p) e -> p i e", p=P), X[:]).then_inc(stored, 16)
            sp.wait_ge(stored, 16)


def head_mixer(nc, X, ident_in, half_in, mask_in, w_in, bias_in, invk_in, idx_in):
    H, D = 16, 8
    G = H
    CH = 8
    TURNS = TILES // CH
    R = CH * H
    SCALE = 0.5 / float(E) ** 0.5
    QKV = 3 * E
    with Core(nc, "mix") as m:
        ident = m.sb("ident", [P])
        mask = m.sb("mask", [HALVES, E])
        w = m.sb("w", [QKV])
        bias = m.sb("bias", [QKV])
        invk = m.sb("invk", [G])
        idx = m.sb("idx", [G])
        neg_half = m.sb("neg_half", [CH])
        xm = m.sb("xm", [CH, E])
        xT = m.sb("xT", [CH, P])
        qkv = m.sb("qkv", [CH, QKV])
        prod = m.sb("prod", [2, H * G * D])
        S = m.sb("S", [G, R])
        U = m.sb("U", [G, R])
        V = m.sb("V", [G, R])
        C1 = m.sb("C1", [G, R])
        C2 = m.sb("C2", [G, R])
        top = m.sb("top", [R])
        tau = m.sb("tau", [R])
        o = m.sb("o", [CH, E])
        scrap = m.sb("scrap", [1])
        stats = m.sb("stats", [CH, 6])
        mv = m.sb("mv", [CH, 2])
        veps = m.sb("veps", [CH])
        rstd = m.sb("rstd", [CH])
        xT_ps = m.ps("xT_ps", [2, 4, P])
        qkv_ps = m.ps("qkv_ps", [4, 512])

        consts, const_set = m.sem("consts"), m.sem("const_set")
        DVE_STEPS = 100
        (masked, xT_made, xT_kept, qkv_made, qkv_kept, qk_mult, qk_summed, attn_made, av_mult, av_summed,
         delta_made, root_made, var_made, rstd_made, dve_step), signals = m.signals(
            masked=1, xT_made=2, xT_kept=2, qkv_made=CH, qkv_kept=CH, qk_mult=CH, qk_summed=CH, attn_made=1,
            av_mult=CH, av_summed=CH, delta_made=1, root_made=1, var_made=1, rstd_made=1, dve_step=DVE_STEPS)
        block = m.block()

        @block.sync
        def _(sp):
            for signal in signals:
                sp.sem_inc(signal.sem, signal.start)
            for dst, src in ((ident, ident_in), (mask, mask_in), (w, w_in)):
                sp.dma_start(dst[:], src).then_inc(consts, 16)
            for dst, src in ((bias, bias_in), (invk, invk_in), (idx, idx_in)):
                sp.dma_start(dst[:], src.partition_broadcast(P)).then_inc(consts, 16)

        @block.gpsimd
        def _(pool):
            pool.memset(neg_half[:], -0.5).then_inc(const_set, 1)
            pool.wait_ge(consts, 96)
            pool.wait_ge(const_set, 1)
            with pool.Fori(0, TURNS) as c:
                pool.wait_ge(*xT_made(c, 0))
                pool.tensor_tensor(xm[:].rearrange("p (a b) e -> p a b e", b=HALVES),
                                   X[:, bass.ds(c * CH, CH), :].rearrange("p (a b) e -> p a b e", b=HALVES),
                                   bc(mask[:], 1, CH // HALVES), ALU.mult).then_inc(masked.sem, 1)
                for j in range(CH):
                    pool.wait_ge(*qkv_kept(c, j + 1))
                    if j >= 2:
                        pool.wait_ge(*qk_summed(c, j - 1))
                    else:
                        pool.wait_ge(*av_summed(c, 0))
                    q = qkv[:, j, 0:E].rearrange("p (h d) -> p h d", d=D)
                    k = qkv[:, j, E:2 * E].rearrange("p (g d) -> p g d", d=D)
                    pool.tensor_tensor(prod[:, j % 2, :].rearrange("p (h g d) -> p h g d", h=H, g=G),
                                       bc(q, 2, G), bc(k, 1, H), ALU.mult).then_inc(qk_mult.sem, 1)
                pool.wait_ge(*attn_made(c, 1))
                for j in range(CH):
                    if j >= 2:
                        pool.wait_ge(*av_summed(c, j - 1))
                    a = S[:, :, j * H:(j + 1) * H].rearrange("p g h -> p h g")
                    v = qkv[:, j, 2 * E:3 * E].rearrange("p (g d) -> p d g", d=D)
                    pool.tensor_tensor(prod[:, j % 2, :].rearrange("p (h d g) -> p h d g", h=H, g=G),
                                       bc(a, 2, D), bc(v, 1, H), ALU.mult).then_inc(av_mult.sem, 1)
                pool.wait_ge(*var_made(c, 1))
                pool.tensor_tensor(rstd[:], veps[:], neg_half[:], ALU.pow).then_inc(rstd_made.sem, 1)

        @block.scalar
        def _(act):
            with act.Fori(0, TURNS) as c:
                for n in range(2):
                    act.wait_ge(*xT_made(c, n + 1))
                    act.wait_ge(*qkv_made(c, 0))
                    nc.scalar.copy(xT[:, 4 * n:4 * n + 4, :], xT_ps[:, n, :, :]).then_inc(xT_kept.sem, 1)
                act.wait_ge(*delta_made(c, 1))
                nc.scalar.activation(U[:], U[:], ACT.Sqrt).then_inc(root_made.sem, 1)

        @block.tensor
        def _(pe):
            pe.wait_ge(consts, 96)
            with pe.Fori(0, TURNS) as c:
                pe.wait_ge(*masked(c, 1))
                pe.wait_ge(*xT_kept(c, 0))
                for j in range(CH):
                    t = nc.tensor.transpose(xT_ps[:, j // 4, j % 4, :], xm[:, j, :], ident[:])
                    if j % 4 == 3:
                        t.then_inc(xT_made.sem, 1)
                for j in range(CH):
                    pe.wait_ge(*xT_kept(c, j // 4 + 1))
                    if j >= 4:
                        pe.wait_ge(*qkv_kept(c, j - 3))
                    else:
                        pe.wait_ge(*qkv_kept(c, 0))
                    nc.tensor.matmul(qkv_ps[:, j % 4, 0:QKV], xT[:, j, :], w[:], start=True, stop=True) \
                        .then_inc(qkv_made.sem, 1)

        def dve_turn(dve, c):
            link = Chain(dve, dve_step, c)
            tt, ts = nc.vector.tensor_tensor, nc.vector.tensor_scalar
            for j in range(CH):
                dve.wait_ge(*qkv_made(c, j + 1))
                if j == 0:
                    dve.wait_ge(*av_mult(c, 0))
                tt(qkv[:, j, :], qkv_ps[:, j % 4, 0:QKV], bias[:], ALU.add).then_inc(qkv_kept.sem, 1)
            for j in range(CH):
                dve.wait_ge(*qk_mult(c, j + 1))
                ins = nc.vector.tensor_reduce(S[:, :, j * H:(j + 1) * H].rearrange("p g h -> p h g"),
                                              prod[:, j % 2, :].rearrange("p (h g d) -> p h g d", h=H, g=G),
                                              op=ALU.add, axis=X_AXIS)
                ins.then_inc(qk_summed.sem, 1)
            dve.wait_ge(*qk_summed(c, CH))
            link(nc.vector.tensor_reduce(top[:], S[:].rearrange("p g r -> p r g"), op=ALU.max, axis=X_AXIS))
            link(tt(S[:], S[:], bc(top[:], 1, G), ALU.subtract))
            link(ts(S[:], S[:], SCALE, None, ALU.mult))
            src, dst = S, U
            for k in (2, 4, 8, 16):
                j = k // 2
                while j:
                    for up in (0, 1) if k < G else (0,):
                        v = lambda t, hi: (t[:].rearrange("p (a u b z l) r -> p a u b z (l r)", u=2, b=k // (2 * j), z=2, l=j)[:, :, up, :, hi, :]
                                           if k < G else
                                           t[:].rearrange("p (b z l) r -> p b z (l r)", z=2, l=j)[:, :, hi, :])
                        link(tt(v(dst, up), v(src, 0), v(src, 1), ALU.max))
                        link(tt(v(dst, 1 - up), v(src, 0), v(src, 1), ALU.min))
                    src, dst = dst, (V if dst is U else U)
                    j //= 2
            xs, tmp = src, dst
            assert xs is V and tmp is U
            link(tt(C2[:], xs[:], xs[:], ALU.mult))
            link(nc.vector.tensor_copy(C1[:, 0, :], xs[:, 0, :]))
            for k in range(1, G):
                link.free(tt(C1[:, k, :], C1[:, k - 1, :], xs[:, k, :], ALU.add))
                link(tt(C2[:, k, :], C2[:, k - 1, :], C2[:, k, :], ALU.add))
            ik = bc(invk[:], 2, R)
            link(tt(tmp[:], C1[:], ik, ALU.mult))
            link(tt(C1[:], C1[:], tmp[:], ALU.mult))
            link(tt(C2[:], C2[:], C1[:], ALU.subtract))
            link(ts(C2[:], C2[:], -1.0, 1.0, ALU.mult, ALU.add))
            link(tt(C1[:], C2[:], ik, ALU.mult))
            link(nc.vector.tensor_copy(C2[:], tmp[:]))
            ts(U[:], C1[:], 0.0, None, ALU.max).then_inc(delta_made.sem, 1)
            dve.wait_ge(*root_made(c, 1))
            link(tt(C2[:], C2[:], U[:], ALU.subtract))
            link(tt(U[:], C2[:], xs[:], ALU.is_le))
            link(nc.vector.tensor_reduce(top[:], U[:].rearrange("p g r -> p r g"), op=ALU.add, axis=X_AXIS))
            link(tt(U[:], bc(top[:], 1, G), bc(idx[:], 2, R), ALU.is_equal))
            link(tt(U[:], U[:], C2[:], ALU.mult))
            link(nc.vector.tensor_reduce(tau[:], U[:].rearrange("p g r -> p r g"), op=ALU.add, axis=X_AXIS))
            link(tt(S[:], S[:], bc(tau[:], 1, G), ALU.subtract))
            link(ts(S[:], S[:], 0.0, None, ALU.max))
            tt(S[:], S[:], S[:], ALU.mult).then_inc(attn_made.sem, 1)
            for j in range(CH):
                dve.wait_ge(*av_mult(c, j + 1))
                nc.vector.tensor_reduce(o[:, j, :].rearrange("p (h d) -> p h d", d=D),
                                        prod[:, j % 2, :].rearrange("p (h d g) -> p h d g", h=H, g=G),
                                        op=ALU.add, axis=X_AXIS).then_inc(av_summed.sem, 1)
            dve.wait_ge(*av_summed(c, CH))
            xv = X[:, bass.ds(c * CH, CH), :]
            link(tt(o[:], o[:], xv, ALU.add))
            layer_norm(nc, dve, link, o, stats, mv, veps, rstd, scrap, CH, var_made, rstd_made, c)
            link(tt(xv, o[:], bc(rstd[:], 2, E), ALU.mult))
            assert link.n == DVE_STEPS, link.n

        @block.vector
        def _(dve):
            dve.wait_ge(consts, 96)
            with dve.Fori(0, TURNS) as c:
                dve_turn(dve, c)


def layer_stack(nc, X, X0, a):
    H, D, W = 16, 64, 32
    NW = T // W
    PAIRS = H // 2
    QUADS, OCTS = 4, 2
    INNER = H * D
    F = int(E * 4 * 2 / 3)
    FC = [(f, min(P, F - f)) for f in range(0, F, P)]
    PROJ = QUADS * HALVES
    with Core(nc, "stack") as m:
        ident, identb = m.sb("ident", [P]), m.sb("identb", [P], BF16)
        mask = m.sb("mask", [PAIRS // OCTS, 2, 2 * W], BF16)
        cos0 = m.sb("cos0", [HALVES, 2, D])
        sin0 = m.sb("sin0", [HALVES, 2, D])
        cosq = m.sb("cosq", [HALVES, 2, D])
        sinq = m.sb("sinq", [HALVES, 2, D])
        qks = m.sb("qks", [2, D])
        wqk = m.sb("wqk", [QUADS, 2, 4 * D])
        wv = m.sb("wv", [INNER])
        wo = m.sb("wo", [PAIRS, E])
        w1 = m.sb("w1", [2 * F])
        w2 = m.sb("w2", [len(FC), E])
        lng, lnb = m.sb("lng", [1]), m.sb("lnb", [1])
        b1 = m.sb("b1", [2, len(FC)])
        b2 = m.sb("b2", [E])
        neg_half = m.sb("neg_half", [8])
        scrap = m.sb("scrap", [1])
        consts, const_set = m.sem("consts"), m.sem("const_set")
        CONSTS = 6 * 16
        (attn_weights, ffn_weights, tables_made), sig1 = m.signals(attn_weights=16 * 5, ffn_weights=16 * 6, tables_made=1)

        xs = m.sb("xs", [HALVES, E])
        hT = m.sb("hT", [W + T])
        sq = m.sb("sq", [2, 8 * D])
        ss = m.sb("ss", [PROJ, 8])
        rn = m.sb("rn", [PROJ, 8])
        raw = m.sb("raw", [2, 8 * D])
        qn = m.sb("qn", [2, 8 * D])
        t1 = m.sb("t1", [2, 8 * D])
        t2 = m.sb("t2", [2, 8 * D])
        QT = m.sb("QT", [PAIRS, T])
        KT = m.sb("KT", [PAIRS, W + T])
        V = m.sb("V", [2, HALVES, INNER])
        pr = m.sb("pr", [OCTS, 2, 4 * P])
        top = m.sb("top", [OCTS, 2, 8])
        den = m.sb("den", [OCTS, 2, 8])
        inv = m.sb("inv", [OCTS, 2, 8])
        PT = m.sb("PT", [OCTS, 2, 4, P])
        OT = m.sb("OT", [PAIRS, T])
        FS = 2
        FT = FS * HALVES
        fx = m.sb("fx", [FT, E])
        fhT = m.sb("fhT", [FS, T])
        stats = m.sb("stats", [FT, 6])
        mv = m.sb("mv", [FT, 2])
        veps = m.sb("veps", [FT])
        rstd = m.sb("rstd", [FT])
        xn = m.sb("xn", [FT, E])
        xnT = m.sb("xnT", [FS * T])
        gl = m.sb("gl", [len(FC), FS * T])
        hh = m.sb("hh", [len(FC), FS * T])
        yb = m.sb("yb", [FT, E])

        qk_ps = [m.ps(f"qk_ps{i}", [512]) for i in range(2)]
        tr_ps = [m.ps(f"tr_ps{i}", [4, P]) for i in range(2)]
        s_ps = [m.ps(f"s_ps{i}", [512]) for i in range(2)]
        o_ps = [m.ps(f"o_ps{i}", [512]) for i in range(2)]

        (xs_made, hT_made, qk_made, raw_made, sq_made, ss_made, rn_made, t1_made, t2_made, added, r_made, qkT_made, qkT_kept,
         pT_made, pT_kept,
         v_made, v_kept, s_made, p_shifted, p_exp, inv_made, p_normed, o_made, o_kept, y_made, x_made,
         xT_made, xT_kept, q_step, p_step), sig2 = m.signals(
            xs_made=1, hT_made=1, qk_made=8, raw_made=8, sq_made=8, ss_made=8, rn_made=8, t1_made=8,
            t2_made=8, added=8, r_made=8,
            qkT_made=8, qkT_kept=8, pT_made=4, pT_kept=4, v_made=8, v_kept=8, s_made=4, p_shifted=4, p_exp=4, inv_made=4,
            p_normed=4, o_made=4, o_kept=4, y_made=1, x_made=1, xT_made=1, xT_kept=1,
            q_step=PROJ, p_step=4 * OCTS)
        NF = len(FC)
        (fx_made, fT_made, fT_kept, fh_made, fvar_made, frstd_made, fxn_made, fnT_made, fnT_kept,
         f1_made, fgelu_made, fhh_made, fy_made, fx_done, fdve_step, fy_step), sig3 = m.signals(
            fx_made=1, fT_made=1, fT_kept=2, fh_made=1, fvar_made=1, frstd_made=1, fxn_made=FT, fnT_made=1,
            fnT_kept=1, f1_made=NF, fgelu_made=NF, fhh_made=NF, fy_made=1, fx_done=1,
            fdve_step=2 * FT, fy_step=1)

        SLOTS = [
            [("xs", 0, 0), ("pT", 0, 1), ("xT", 0, 0), ("proj", 0, 0), ("pv", 0, 1)],
            [("proj", 1, 0), ("pv", 1, 1)],
            [("proj", 2, 0), ("scores", 2, 1)],
            [("proj", 3, 0), ("scores", 3, 1)],
            [("proj", 4, 0), ("shift", 1, 1), ("v", 0, 0), ("v", 1, 0)],
            [("proj", 5, 0), ("sum", 1, 1), ("v", 2, 0), ("v", 3, 0)],
            [("proj", 6, 0), ("pT", 1, 1), ("scores", 0, 0), ("scores", 1, 0)],
            [("proj", 7, 0), ("pv", 2, 1)],
            [("pv", 3, 1), ("shift", 0, 0)],
            [("out", 0, 1), ("sum", 0, 0), ("v", 4, 0), ("v", 5, 0), ("v", 6, 0), ("v", 7, 0)]]
        BODY = []
        for i, slot in enumerate(SLOTS):
            BODY += slot
            if i < PROJ:
                BODY += [("rope", i, 0), ("norm", i, 0)]
            if 1 <= i <= PROJ:
                BODY += [("add", i - 1, 0)]
            if i >= 2:
                BODY += [("qkT", i - 2, 0)]
        FIRST = [s for s in BODY if s[2] == 0]
        LAST = [s for s in BODY if s[2] == 1]

        def v_part(n):
            c = n // 4
            return n % 4 // 2, n % 2, c, (n + c) % 2

        def over_sequences(eng, l, steps):
            steps(FIRST, l * B, 0)
            with eng.Fori(1, B) as b:
                steps(BODY, l * B + b, b)
            steps(LAST, (l + 1) * B, B)

        F_BODY = [("in", 0, 0), ("up", 0, 1), ("in", 1, 0), ("up", 1, 1), ("in", 2, 0), ("up", 2, 1), ("in", 3, 0), ("down", 0, 1)]
        F_FIRST = [s for s in F_BODY if s[2] == 0]
        F_LAST = [s for s in F_BODY if s[2] == 1]

        def over_groups(eng, l, steps):
            steps(F_FIRST, l * (B // FS), 0)
            with eng.Fori(1, B // FS) as b:
                steps(F_BODY, l * (B // FS) + b, b)
            steps(F_LAST, (l + 1) * (B // FS), B // FS)

        def head_groups(ap):
            return ap.rearrange("p (g d) -> p g d", d=D)

        def swap_halves(out, x, table, t):
            for half in range(2):
                o = out.rearrange("p (c g z d) -> p c g z d", c=2, g=4, z=2)[:, :, :, half, :]
                i = x.rearrange("p (c g z d) -> p c g z d", c=2, g=4, z=2)[:, :, :, 1 - half, :]
                s = table[:, t, :, :].rearrange("p c (z d) -> p c z d", z=2)[:, :, half, :]
                yield o, i, bc(s, 2, 4)

        block = m.block()

        @block.sync
        def _(sp):
            for signal in sig1 + sig2 + sig3:
                sp.sem_inc(signal.sem, signal.start)
            sp.dma_start(X0[:], X[:]).then_inc(consts, 16)
            for dst, src in ((ident, "ident"), (identb, "identb"), (mask, "win_mask"), (cos0, "cos0"), (sin0, "sin0")):
                sp.dma_start(dst[:], a[src]).then_inc(consts, 16)
            with sp.Fori(0, DEPTH) as l:
                one = lambda ap: ap[bass.ds(l, 1)].rearrange("o p n -> (o p) n")
                row = lambda ap: ap[bass.ds(l, 1), :].rearrange("o n -> (o n)")
                sp.wait_ge(*y_made(l * B, 0))
                up = attn_weights.sem
                wsrc = one(a["wqkv"])
                for c in range(2):
                    sp.dma_start(wqk[:, :, c, :], wsrc[:, c * INNER:(c + 1) * INNER].rearrange("p (q n) -> p q n", q=QUADS)).then_inc(up, 16)
                sp.dma_start(qks[:].rearrange("p c d -> p (c d)"), row(a["qk_scale"]).partition_broadcast(P)).then_inc(up, 16)
                sp.dma_start(wv[:], wsrc[:, 2 * INNER:3 * INNER]).then_inc(up, 16)
                sp.dma_start(wo[:], one(a["wo"]).rearrange("(c p) n -> p c n", p=P)).then_inc(up, 16)
                sp.wait_ge(*fx_done(l * (B // FS), 0))
                up = ffn_weights.sem
                sp.dma_start(w1[:], one(a["w1"])).then_inc(up, 16)
                sp.dma_start(w2[:], one(a["w2"]).rearrange("(c p) n -> p c n", p=P)).then_inc(up, 16)
                sp.dma_start(b2[:], row(a["b2"]).partition_broadcast(P)).then_inc(up, 16)
                sp.dma_start(lng[:], one(a["ln_g"])).then_inc(up, 16)
                sp.dma_start(lnb[:], one(a["ln_b"])).then_inc(up, 16)
                sp.dma_start(b1[:].rearrange("p c k -> p (c k)"), one(a["b1"])).then_inc(up, 16)

        @block.gpsimd
        def _(pool):
            pool.memset(neg_half[:], -0.5).then_inc(const_set, 1)
            pool.memset(KT[:, :, 0:W], 0.0).then_inc(const_set, 1)
            pool.memset(hT[:, 0:W + 1], 0.0).then_inc(const_set, 1)
            pool.memset(fhT[:, :, 0:1], 0.0).then_inc(const_set, 1)
            pool.wait_ge(const_set, 4)

            def attend(order, turn, b):
                for step, n, age in order:
                    i = turn - age
                    if step == "norm":
                        pool.wait_ge(*ss_made(i, n + 1))
                        pool.tensor_tensor(rn[:, n, :], ss[:, n, :], neg_half[:], ALU.pow).then_inc(rn_made.sem, 1)
                    elif step == "rope":
                        pool.wait_ge(*raw_made(i, n + 1))
                        pool.wait_ge(*tables_made(layer[0], 1))
                        pool.wait_ge(*added(i, max(n - 1, 0)))
                        for o, x, s in swap_halves(t2[:, n % 2, :], raw[:, n % 2, :], sinq, n % 2):
                            last = pool.tensor_tensor(o, x, s, ALU.mult)
                        last.then_inc(t2_made.sem, 1)
                    elif step == "sum":
                        for h in range(2):
                            pool.wait_ge(*inv_made(i, 2 * n + h + 1))
                            v = pr[:, n, h, :].rearrange("p (g k) -> p g k", k=2 * W)
                            pool.tensor_tensor(v, v, bc(inv[:, n, h, :], 2, 2 * W), ALU.mult).then_inc(p_normed.sem, 1)

            def feed(order, turn, b):
                for step, n, age in order:
                    if (step, n) == ("in", 2):
                        pool.wait_ge(*fvar_made(turn, 1))
                        pool.tensor_tensor(rstd[:], veps[:], neg_half[:, 0:FT], ALU.pow).then_inc(frstd_made.sem, 1)

            layer = [0]
            with pool.Fori(0, DEPTH) as l:
                layer[0] = l
                over_sequences(pool, l, attend)
                over_groups(pool, l, feed)

        @block.scalar
        def _(act):
            act.wait_ge(const_set, 4)
            layer = [0]

            def attend(order, turn, b):
                for step, n, age in order:
                    i = turn - age
                    if step == "xs":
                        act.wait_ge(*xT_made(i, 0))
                        nc.scalar.copy(xs[:], X[:, bass.ds(b * HALVES, HALVES), :]).then_inc(xs_made.sem, 1)
                    elif step == "xT":
                        act.wait_ge(*xT_made(i, 1))
                        act.wait_ge(*v_made(i, 0))
                        xv = tr_ps[0][:, 0:HALVES, :].rearrange("p t c -> p (t c)")
                        nc.scalar.copy(hT[0:64, W:W + T], xv[0:64, :]).then_inc(hT_made.sem, 1)
                        nc.scalar.copy(hT[64:128, W + 1:W + T], xv[64:128, 0:T - 1]).then_inc(xT_kept.sem, 1)
                    elif step == "proj":
                        act.wait_ge(*qk_made(i, n + 1))
                        act.wait_ge(*t1_made(i, max(n - 1, 0)))
                        act.wait_ge(*t2_made(i, max(n - 1, 0)))
                        nc.scalar.copy(raw[:, n % 2, :], qk_ps[n % 2][:]).then_inc(raw_made.sem, 1)
                        act.wait_ge(*ss_made(i, max(n - 1, 0)))
                        nc.scalar.activation(sq[:, n % 2, :], qk_ps[n % 2][:], ACT.Square).then_inc(sq_made.sem, 1)
                    elif step == "v":
                        act.wait_ge(*v_made(i, n + 1))
                        act.wait_ge(*o_made(i, -2 if n < 4 else 0))
                        back, t, c, bank = v_part(n)
                        nc.scalar.copy(V[:, back, t, c * 512:(c + 1) * 512], o_ps[bank][:]) \
                            .then_inc(v_kept.sem, 1)
                    elif step == "qkT":
                        act.wait_ge(*qkT_made(i, n + 1))
                        act.wait_ge(*s_made(i, -2 if n < 4 else 0))
                        q, t = n // 2, n % 2
                        nc.scalar.copy(QT[:, 2 * q:2 * q + 2, t * P:(t + 1) * P], tr_ps[0][:, 0:2, :])
                        nc.scalar.copy(KT[:, 2 * q:2 * q + 2, W + t * P:W + (t + 1) * P], tr_ps[0][:, 2:4, :]) \
                            .then_inc(qkT_kept.sem, 1)
                    elif step == "shift":
                        for h in range(2):
                            act.wait_ge(*p_shifted(i, 2 * n + h + 1))
                            nc.scalar.activation(pr[:, n, h, :], pr[:, n, h, :], ACT.Exp).then_inc(p_exp.sem, 1)
                    elif step == "pT":
                        for h in range(2):
                            act.wait_ge(*pT_made(i, 2 * n + h + 1))
                            if h == 0:
                                act.wait_ge(*o_made(i, 0))
                            nc.scalar.copy(PT[:, n, h, :, :], tr_ps[1][:]).then_inc(pT_kept.sem, 1)
                    elif step == "pv":
                        o, j = n // 2, n % 2
                        act.wait_ge(*o_made(i, n + 1))
                        act.wait_ge(*y_made(i, 0))
                        ov = OT[:, 4 * o:4 * o + 4, :].rearrange("p c (t j x) -> p c t j x", t=HALVES, j=2)
                        nc.scalar.copy(ov[:, :, :, j, :], o_ps[j][:].rearrange("p (c t x) -> p c t x", c=4, t=HALVES)) \
                            .then_inc(o_kept.sem, 1)

            def feed(order, turn, b):
                for step, n, age in order:
                    i = turn - age
                    if (step, n) == ("in", 0):
                        act.wait_ge(*x_made((layer[0] + 1) * B, 0))
                        act.wait_ge(*fT_made(i, 0))
                        nc.scalar.copy(fx[:], X[:, bass.ds(b * FT, FT), :]).then_inc(fx_made.sem, 1)
                        act.wait_ge(*fT_made(i, 1))
                        act.wait_ge(*fh_made(i, 0))
                        xv = tr_ps[0][:].rearrange("p (s t) c -> p s (t c)", s=FS)
                        nc.scalar.copy(fhT[0:64, :, :], xv[0:64]).then_inc(fT_kept.sem, 1)
                        nc.scalar.copy(fhT[64:128, :, 1:T], xv[64:128, :, 0:T - 1]).then_inc(fT_kept.sem, 1)
                    elif (step, n) == ("in", 3):
                        act.wait_ge(*fnT_made(i, 1))
                        act.wait_ge(*f1_made(i, 0))
                        act.wait_ge(*ffn_weights(layer[0], 96))
                        nc.scalar.activation(xnT[:], tr_ps[0][:].rearrange("p t c -> p (t c)"), ACT.Identity,
                                             bias=lnb[:, 0:1], scale=lng[:, 0:1]).then_inc(fnT_kept.sem, 1)
                    elif step == "up":
                        f, size = FC[n]
                        act.wait_ge(*f1_made(i, n + 1))
                        nc.scalar.activation(gl[0:size, n, :], qk_ps[n % 2][0:size, :], ACT.Gelu,
                                             bias=b1[0:size, 1, n:n + 1]).then_inc(fgelu_made.sem, 1)

            with act.Fori(0, DEPTH) as l:
                layer[0] = l
                act.wait_ge(*fx_done(l * (B // FS), 0))
                over_sequences(act, l, attend)
                over_groups(act, l, feed)

        @block.tensor
        def _(pe):
            pe.wait_ge(consts, CONSTS)
            pe.wait_ge(const_set, 4)
            mm, flip = nc.tensor.matmul, nc.tensor.transpose
            layer = [0]

            def attend(order, turn, b):
                for step, n, age in order:
                    i = turn - age
                    if step == "xT":
                        pe.wait_ge(*attn_weights(layer[0], 80))
                        pe.wait_ge(*qkT_kept(i, 0))
                        pe.wait_ge(*xs_made(i, 1))
                        for t in range(HALVES):
                            last = flip(tr_ps[0][:, t, :], xs[:, t, :], ident[:])
                        last.then_inc(xT_made.sem, 1)
                        pe.wait_ge(*hT_made(i, 1))
                        pe.wait_ge(*xT_kept(i, 1))
                    elif step == "proj":
                        pe.wait_ge(*sq_made(i, max(n - 1, 0)))
                        t = n % 2
                        mm(qk_ps[n % 2][:], hT[:, W + t * P:W + (t + 1) * P],
                           wqk[:, n // 2, :, :].rearrange("p c n -> p (c n)"), start=True, stop=True).then_inc(qk_made.sem, 1)
                    elif step == "v":
                        back, t, c, bank = v_part(n)
                        pe.wait_ge(*{0: o_kept(i, -3), 1: o_kept(i, -2), 4: o_kept(i, 0), 5: x_made(i, 0)}.get(n, v_kept(i, n - 1)))
                        at = W * (1 - back) + t * P
                        mm(o_ps[bank][:], hT[:, at:at + P], wv[:, c * 512:(c + 1) * 512], start=True, stop=True) \
                            .then_inc(v_made.sem, 1)
                    elif step == "qkT":
                        pe.wait_ge(*r_made(i, n + 1))
                        pe.wait_ge(*qkT_kept(i, n))
                        for c in range(4):
                            last = flip(tr_ps[0][:, c, :], qn[:, n % 2, c * P:(c + 1) * P], ident[:])
                        last.then_inc(qkT_made.sem, 1)
                    elif step == "scores":
                        o, part = n // 2, n % 2
                        if part == 0:
                            pe.wait_ge(*qkT_kept(i, 4 * o + 4))
                            pe.wait_ge(*p_shifted(i, 2 * o))
                            for h in range(2):
                                mm(s_ps[h][:], identb[:], mask[:].rearrange("p c j k -> p (c j k)"),
                                   start=True, stop=False, skip_group_check=True)
                        for c in range(2 * part, 2 * part + 2):
                            for j in range(2):
                                for ts in range(4):
                                    for h in range(2):
                                        w = 4 * (ts // 2) + 2 * j + ts % 2
                                        r = slice(64 * h, 64 * h + 64)
                                        last = mm(s_ps[h][32 * ts:32 * ts + 32, c * P + 64 * j:c * P + 64 * j + 64],
                                                  QT[r, 4 * o + c, W * w:W * w + W], KT[r, 4 * o + c, W * w:W * w + 2 * W],
                                                  start=False, stop=(c == 3 and j == 1), skip_group_check=True,
                                                  tile_position=(64 * h, 32 * ts))
                                        if c == 3 and j == 1 and ts == 3:
                                            last.then_inc(s_made.sem, 1)
                    elif step == "pT":
                        for h in range(2):
                            pe.wait_ge(*p_normed(i, 2 * n + h + 1))
                            pe.wait_ge(*pT_kept(i, 2 * n + h))
                            for c in range(4):
                                last = flip(tr_ps[1][:, c, :], pr[:, n, h, c * P:(c + 1) * P], ident[:])
                            last.then_inc(pT_made.sem, 1)
                    elif step == "pv":
                        o, j = n // 2, n % 2
                        pe.wait_ge(*pT_kept(i, 2 * o + 2))
                        pe.wait_ge(*(v_kept(i, 8) if o == 0 or order is LAST else v_kept(i + 1, 3 + j)))
                        mm(o_ps[j][:, 0:1], identb[:], identb[:, 0:1], start=True, stop=True)
                        for c in range(4):
                            for ts in range(4):
                                for h in range(2):
                                    r = slice(64 * j, 64 * j + 64)
                                    g = (4 * o + c) * P + 64 * h
                                    last = mm(o_ps[j][64 * h:64 * h + 64, c * P + 32 * ts:c * P + 32 * ts + 32],
                                              V[r, 1 - ts % 2, ts // 2, g:g + 64], PT[r, o, h, c, 32 * ts:32 * ts + 32],
                                              start=True, stop=True, tile_position=(64 * j, 64 * h))
                        last.then_inc(o_made.sem, 1)
                    elif step == "out":
                        pe.wait_ge(*o_kept(i, 4))
                        for t in range(HALVES):
                            for c in range(PAIRS):
                                last = mm(o_ps[0][:, t * P:(t + 1) * P], OT[:, c, t * P:(t + 1) * P], wo[:, c, :],
                                          start=(c == 0), stop=(c == PAIRS - 1))
                        last.then_inc(y_made.sem, 1)

            def feed(order, turn, b):
                for step, n, age in order:
                    i = turn - age
                    if (step, n) == ("in", 0):
                        pe.wait_ge(*x_made((layer[0] + 1) * B, 0))
                        pe.wait_ge(*fx_made(i, 1))
                        pe.wait_ge(*fnT_kept(i, 0))
                        for t in range(FT):
                            last = flip(tr_ps[0][:, t, :], fx[:, t, :], ident[:])
                        last.then_inc(fT_made.sem, 1)
                    elif (step, n) == ("in", 1):
                        pe.wait_ge(*fT_kept(i, 2))
                        pe.wait_ge(*fxn_made(i, 0))
                        for t in range(FT):
                            last = flip(tr_ps[1][:, t, :], fhT[:, t // 2, (t % 2) * P:(t % 2) * P + P], ident[:])
                        last.then_inc(fh_made.sem, 1)
                    elif (step, n) == ("in", 3):
                        pe.wait_ge(*fxn_made(i, FT))
                        for t in range(FT):
                            last = flip(tr_ps[0][:, t, :], xn[:, t, :], ident[:])
                        last.then_inc(fnT_made.sem, 1)
                    elif step == "up":
                        f, size = FC[n]
                        if n == 0:
                            pe.wait_ge(*ffn_weights(layer[0], 96))
                            pe.wait_ge(*fnT_kept(i, 1))
                        pe.wait_ge(*fhh_made(i, max(n - 1, 0)))
                        mm(qk_ps[n % 2][0:size, :], w1[:, F + f:F + f + size], xnT[:], start=True, stop=True)
                        mm(s_ps[n % 2][0:size, :], w1[:, f:f + size], xnT[:], start=True, stop=True).then_inc(f1_made.sem, 1)
                    elif step == "down":
                        pe.wait_ge(*fx_done(i, 0))
                        pe.wait_ge(*fhh_made(i, NF))
                        for t in range(FT):
                            for c, (f, size) in enumerate(FC):
                                last = mm(o_ps[0][:, t * P:(t + 1) * P], hh[0:size, c, t * P:(t + 1) * P], w2[0:size, c, :],
                                          start=(c == 0), stop=(c == NF - 1))
                        last.then_inc(fy_made.sem, 1)

            with pe.Fori(0, DEPTH) as l:
                layer[0] = l
                over_sequences(pe, l, attend)
                over_groups(pe, l, feed)

        @block.vector
        def _(dve):
            tt, ts_, red = nc.vector.tensor_tensor, nc.vector.tensor_scalar, nc.vector.tensor_reduce
            dve.wait_ge(consts, CONSTS)
            layer = [0]

            def attend(order, turn, b):
                for step, n, age in order:
                    i = turn - age
                    if step == "norm":
                        dve.wait_ge(*sq_made(i, n + 1))
                        red(ss[:, n, :], head_groups(sq[:, n % 2, :]), op=ALU.add, axis=X_AXIS).then_inc(q_step.sem, 1)
                        dve.wait_ge(*q_step(i, n + 1))
                        ts_(ss[:, n, :], ss[:, n, :], 1e-24, None, ALU.max).then_inc(ss_made.sem, 1)
                    elif step == "rope":
                        dve.wait_ge(*raw_made(i, n + 1))
                        dve.wait_ge(*r_made(i, max(n - 1, 0)))
                        v = lambda ap: ap.rearrange("p (c g d) -> p c g d", c=2, g=4)
                        tt(v(t1[:, n % 2, :]), v(raw[:, n % 2, :]), bc(cosq[:, n % 2], 2, 4), ALU.mult).then_inc(t1_made.sem, 1)
                    elif step == "add":
                        dve.wait_ge(*t1_made(i, n + 1))
                        dve.wait_ge(*t2_made(i, n + 1))
                        tt(t1[:, n % 2, :], t1[:, n % 2, :], t2[:, n % 2, :], ALU.add).then_inc(added.sem, 1)
                        dve.wait_ge(*added(i, n + 1))
                        dve.wait_ge(*rn_made(i, n + 1))
                        dve.wait_ge(*qkT_made(i, max(n - 1, 0)))
                        tt(head_groups(qn[:, n % 2, :]), head_groups(t1[:, n % 2, :]), bc(rn[:, n, :], 2, D), ALU.mult) \
                            .then_inc(r_made.sem, 1)
                    elif step == "shift":
                        for h in range(2):
                            dve.wait_ge(*s_made(i, 2 * n + h + 1))
                            v = lambda ap: ap.rearrange("p (g k) -> p g k", k=2 * W)
                            red(top[:, n, h, :], v(s_ps[h][:]), op=ALU.max, axis=X_AXIS).then_inc(p_step.sem, 1)
                            dve.wait_ge(*p_step(i, 4 * n + h + 1))
                            tt(v(pr[:, n, h, :]), v(s_ps[h][:]), bc(top[:, n, h, :], 2, 2 * W), ALU.subtract) \
                                .then_inc(p_shifted.sem, 1)
                    elif step == "sum":
                        for h in range(2):
                            dve.wait_ge(*p_exp(i, 2 * n + h + 1))
                            red(den[:, n, h, :], pr[:, n, h, :].rearrange("p (g k) -> p g k", k=2 * W), op=ALU.add, axis=X_AXIS) \
                                .then_inc(p_step.sem, 1)
                            dve.wait_ge(*p_step(i, 4 * n + h + 3))
                            nc.vector.reciprocal(inv[:, n, h, :], den[:, n, h, :]).then_inc(inv_made.sem, 1)
                    elif step == "out":
                        dve.wait_ge(*y_made(i, 1))
                        xv = X[:, bass.ds((b - age) * HALVES, HALVES), :].rearrange("p t e -> p (t e)")
                        tt(xv, xv, o_ps[0][:, 0:HALVES * E], ALU.add).then_inc(x_made.sem, 1)

            def feed(order, turn, b):
                for step, n, age in order:
                    i = turn - age
                    if (step, n) == ("in", 2):
                        dve.wait_ge(*fh_made(i, 1))
                        for t in range(FT):
                            nc.vector.bn_stats(stats[:, t, :], tr_ps[1][:, t, :]).then_inc(fdve_step.sem, 1)
                        dve.wait_ge(*fdve_step(i, FT))
                        hold(nc.vector, scrap)
                        for t in range(FT):
                            nc.vector.bn_aggr(mv[:, t, :], stats[:, t, :]).then_inc(fdve_step.sem, 1)
                        dve.wait_ge(*fdve_step(i, 2 * FT))
                        ts_(veps[:], mv[:, :, 1], LN_EPS, None, ALU.add).then_inc(fvar_made.sem, 1)
                    elif (step, n) == ("in", 3):
                        dve.wait_ge(*frstd_made(i, 1))
                        dve.wait_ge(*fnT_made(i, 0))
                        for t in range(FT):
                            ts_(xn[:, t, :], tr_ps[1][:, t, :], mv[:, t, 0:1], rstd[:, t:t + 1], ALU.subtract, ALU.mult) \
                                .then_inc(fxn_made.sem, 1)
                    elif step == "up":
                        f, size = FC[n]
                        dve.wait_ge(*fgelu_made(i, n + 1))
                        nc.vector.scalar_tensor_tensor(hh[0:size, n, :], s_ps[n % 2][0:size, :], b1[0:size, 0, n:n + 1], gl[0:size, n, :],
                                                       ALU.add, ALU.mult).then_inc(fhh_made.sem, 1)
                    elif step == "down":
                        dve.wait_ge(*fy_made(i, 1))
                        tt(yb[:], o_ps[0][:].rearrange("p (t e) -> p t e", e=E), bc(b2[:], 1, FT), ALU.add).then_inc(fy_step.sem, 1)
                        dve.wait_ge(*fy_step(i, 1))
                        xv = X[:, bass.ds((b - age) * FT, FT), :]
                        tt(xv, xv, yb[:], ALU.add).then_inc(fx_done.sem, 1)

            with dve.Fori(0, DEPTH) as l:
                layer[0] = l
                dve.wait_ge(*attn_weights(l, 80))
                dve.wait_ge(*t2_made(l * B, 0))
                for t in range(HALVES):
                    tt(cosq[:, t], cos0[:, t], qks[:], ALU.mult)
                    for half in range(2):
                        v = lambda ap: ap.rearrange("p c (z d) -> p c z d", z=2)
                        last = tt(v(sinq[:, t])[:, :, half, :], v(sin0[:, t])[:, :, half, :], v(qks[:])[:, :, 1 - half, :], ALU.mult)
                last.then_inc(tables_made.sem, 1)
                dve.wait_ge(*tables_made(l, 1))
                over_sequences(dve, l, attend)
                over_groups(dve, l, feed)


def add_norm(nc, X0, X, stage):
    N = 8
    with Core(nc, stage) as m:
        h = m.sb("h", [N, E])
        neg_half = m.sb("neg_half", [N])
        scrap = m.sb("scrap", [1])
        stats, mv = m.sb("stats", [N, 6]), m.sb("mv", [N, 2])
        veps, rstd = m.sb("veps", [N]), m.sb("rstd", [N])
        const_set = m.sem("const_set")
        STEPS = 2 * N + 3
        (var_made, rstd_made, step_done), signals = m.signals(var_made=1, rstd_made=1, step_done=STEPS)
        block = m.block()

        @block.sync
        def _(sp):
            for signal in signals:
                sp.sem_inc(signal.sem, signal.start)

        @block.gpsimd
        def _(pool):
            pool.memset(neg_half[:], -0.5).then_inc(const_set, 1)
            pool.wait_ge(const_set, 1)
            with pool.Fori(0, TILES // N) as c:
                pool.wait_ge(*var_made(c, 1))
                pool.tensor_tensor(rstd[:], veps[:], neg_half[:], ALU.pow).then_inc(rstd_made.sem, 1)

        @block.vector
        def _(dve):
            with dve.Fori(0, TILES // N) as c:
                link = Chain(dve, step_done, c)
                link(nc.vector.tensor_tensor(h[:], X0[:, bass.ds(c * N, N), :], X[:, bass.ds(c * N, N), :], ALU.add))
                layer_norm(nc, dve, link, h, stats, mv, veps, rstd, scrap, N, var_made, rstd_made, c)
                link(nc.vector.tensor_tensor(X[:, bass.ds(c * N, N), :], h[:], bc(rstd[:], 2, E), ALU.mult))
                assert link.n == STEPS, link.n


def small_heads(nc, X, a, causal):
    H, D, HP = 16, 8, 32
    KV = 4 if causal else H
    G = H // 4
    QKV = (H + 2 * KV) * D
    QK = H + KV
    SCALE = 1.0 / float(D) ** 0.5
    with Core(nc, "causal" if causal else "rotary") as m:
        ident, identb = m.sb("ident", [P]), m.sb("identb", [P], BF16)
        w = m.sb("w", [QKV])
        w_out = m.sb("w_out", [E])
        aff = m.sb("aff", [4])
        cos, sin = m.sb("cos", [HALVES, D]), m.sb("sin", [HALVES, D])
        neg_half = m.sb("neg_half", [2 * QK])
        scrap = m.sb("scrap", [1])
        if causal:
            mask = m.sb("mask", [HALVES, T], BF16)
            maskT = m.sb("maskT", [HALVES, T], BF16)
            dmas = [(mask, "causal"), (maskT, "causal_t")]
            rows = []
        else:
            bias = m.sb("bias", [QKV])
            b_out = m.sb("b_out", [E])
            w_rad = m.sb("w_rad", [E])
            b_rad = m.sb("b_rad", [1])
            w_ln, b_ln = m.sb("w_ln", [D]), m.sb("b_ln", [D])
            dmas = []
            rows = [(bias, "rot_bias"), (b_out, "rot_b_out"), (w_rad, "rot_w_rad"), (b_rad, "rot_b_rad"),
                    (w_ln, "rot_w_ln"), (b_ln, "rot_b_ln")]
        pre = "cau" if causal else "rot"
        dmas += [(ident, "ident"), (identb, "identb"), (w, f"{pre}_w"), (w_out, f"{pre}_w_out"), (aff, f"{pre}_aff"),
                 (cos, f"{pre}_cos"), (sin, f"{pre}_sin")]
        xh = m.sb("xh", [HALVES, E])
        sqx = m.sb("sqx", [HALVES, E])
        stats, mv = m.sb("stats", [HALVES, 6]), m.sb("mv", [HALVES, 2])
        veps, rstd = m.sb("veps", [HALVES]), m.sb("rstd", [HALVES])
        xqT, xkT = m.sb("xqT", [T]), m.sb("xkT", [T])
        rad = m.sb("rad", [HALVES])
        qkv = m.sb("qkv", [HALVES, QKV])
        t1, t2 = m.sb("t1", [HALVES, QK * D]), m.sb("t2", [HALVES, QK * D])
        mean = m.sb("mean", [HALVES, QK])
        hvar = m.sb("hvar", [HALVES, QK])
        hrstd = m.sb("hrstd", [HALVES, QK])
        QK_pad = m.sb("QK_pad", [HALVES, 2, H, HP])
        V_pad = m.sb("V_pad", [HALVES, KV, HP])
        QT, KT, QmT = m.sb("QT", [G, T]), m.sb("KT", [G, T]), m.sb("QmT", [G, T])
        top = m.sb("top", [H, HALVES])
        PT = m.sb("PT", [3, HALVES, T])
        OT = m.sb("OT", [G, T])
        rec = m.sb("rec", [HALVES, H])
        att = m.sb("att", [HALVES, E])
        attT = m.sb("attT", [T])
        y = m.sb("y", [HALVES, E])

        s1_ps = [m.ps(f"s1_ps{i}", [HALVES, T]) for i in range(2)]
        s2_ps = [m.ps(f"s2_ps{i}", [HALVES, T]) for i in range(2)]
        o_ps = [m.ps(f"o_ps{i}", [512]) for i in range(2)]
        tr_ps = [m.ps(f"tr_ps{i}", [4, P]) for i in range(2)]

        USES = [("x", 0)] + [("qk", n) for n in range(4)] + [("qm", g) for g in range(G)] + [("o", 0), ("o", 1), ("att", 0)]
        use_of = {u: i for i, u in enumerate(USES)}
        TRU = len(USES)
        assert TRU % 2 == 0
        DVE_STEPS = 15 if causal else 39
        consts, const_set = m.sem("consts"), m.sem("const_set")
        CONSTS = 16 * (len(dmas) + len(rows))
        (var_made, rstd_made, xh_made, tr_made, tr_kept, xT_kept, qkv_made, qkv_kept, hvar_made, hrstd_made,
         pad_made, v_padded, s1_made, top_made, negm_made, s2_made, p_made, o_made, o_kept, att_made, y_made,
         var2_made, rstd2_made, x_made, step_done), signals = m.signals(
            var_made=1, rstd_made=1, xh_made=1, tr_made=TRU, tr_kept=TRU, xT_kept=1, qkv_made=1, qkv_kept=1,
            hvar_made=1, hrstd_made=1, pad_made=1, v_padded=1, s1_made=H, top_made=H, negm_made=G, s2_made=H,
            p_made=H, o_made=H, o_kept=G, att_made=2, y_made=1, var2_made=1, rstd2_made=1, x_made=1,
            step_done=DVE_STEPS)
        LAG = 5
        ORDER = []
        for h in range(H + LAG + 1):
            if h < H:
                ORDER.append(("s1", h))
                if h % 4 == 3:
                    ORDER.append(("qm", h // 4))
            if 0 <= h - LAG < H:
                ORDER.append(("s2", h - LAG))
            if h - LAG - 1 >= 0:
                ORDER.append(("pv", h - LAG - 1))
        block = m.block()

        @block.sync
        def _(sp):
            for signal in signals:
                sp.sem_inc(signal.sem, signal.start)
            for dst, name in dmas:
                sp.dma_start(dst[:], a[name]).then_inc(consts, 16)
            for dst, name in rows:
                sp.dma_start(dst[:], a[name].partition_broadcast(P)).then_inc(consts, 16)

        @block.gpsimd
        def _(pool):
            pool.memset(neg_half[:], -0.5).then_inc(const_set, 1)
            pool.memset(QK_pad[:], 0.0).then_inc(const_set, 1)
            pool.memset(V_pad[:], 0.0).then_inc(const_set, 1)
            pool.wait_ge(const_set, 3)
            pool.memset(QK_pad[:, :, 1, :, D:D + 1], 1.0).then_inc(const_set, 1)
            pool.memset(V_pad[:, :, :, D:D + 1], 1.0).then_inc(const_set, 1)
            power = lambda o, i, n: pool.tensor_tensor(o, i, neg_half[:, 0:n], ALU.pow)
            with pool.Fori(0, B) as b:
                pool.wait_ge(*var_made(b, 1))
                power(rstd[:], veps[:], HALVES).then_inc(rstd_made.sem, 1)
                if not causal:
                    pool.wait_ge(*hvar_made(b, 1))
                    power(hrstd[:].rearrange("p t h -> p (t h)"), hvar[:].rearrange("p t h -> p (t h)"), 2 * QK) \
                        .then_inc(hrstd_made.sem, 1)
                    pool.wait_ge(*var2_made(b, 1))
                    power(rstd[:], veps[:], HALVES).then_inc(rstd2_made.sem, 1)

        @block.scalar
        def _(act):
            act.wait_ge(consts, CONSTS)
            ident_fn = ACT.Identity
            with act.Fori(0, B) as b:
                act.wait_ge(*tr_made(b, 1))
                act.wait_ge(*qkv_made(b, 0))
                xT = tr_ps[0][:, 0:HALVES, :].rearrange("p t c -> p (t c)")
                nc.scalar.activation(xqT[:], xT, ident_fn, bias=aff[:, 1:2], scale=aff[:, 0:1])
                last = nc.scalar.activation(xkT[:], xT, ident_fn, bias=aff[:, 3:4], scale=aff[:, 2:3])
                last.then_inc(tr_kept.sem, 1)
                for n in range(4):
                    u = use_of["qk", n]
                    act.wait_ge(*tr_made(b, u + 1))
                    dst = (QT, KT)[n // 2]
                    nc.scalar.copy(dst[:, :, (n % 2) * P:(n % 2) * P + P], tr_ps[u % 2][:]).then_inc(tr_kept.sem, 1)
                for step, n in ORDER:
                    if step == "qm":
                        u = use_of["qm", n]
                        act.wait_ge(*tr_made(b, u + 1))
                        nc.scalar.copy(QmT[:, n, :], tr_ps[u % 2][:, 0:HALVES, :].rearrange("p t c -> p (t c)")) \
                            .then_inc(tr_kept.sem, 1)
                    elif step == "s2":
                        act.wait_ge(*s2_made(b, n + 1))
                        act.wait_ge(*o_made(b, max(n - 2, 0)))
                        nc.scalar.activation(PT[:, n % 3], s2_ps[n % 2][:], ACT.Exp, scale=SCALE).then_inc(p_made.sem, 1)
                    elif step == "pv" and n % 4 == 3:
                        g = n // 4
                        act.wait_ge(*o_made(b, n + 1))
                        act.wait_ge(*tr_made(b, 0))
                        nc.scalar.copy(OT[:, g, :], o_ps[g % 2][:, 0:T]).then_inc(o_kept.sem, 1)
                act.wait_ge(*tr_made(b, TRU))
                nc.scalar.copy(attT[:], tr_ps[(TRU - 1) % 2][:, 0:HALVES, :].rearrange("p t c -> p (t c)")) \
                    .then_inc(tr_kept.sem, 1)

        @block.tensor
        def _(pe):
            mm, flip = nc.tensor.matmul, nc.tensor.transpose
            pe.wait_ge(consts, CONSTS)
            pe.wait_ge(const_set, 5)
            with pe.Fori(0, B) as b:
                pe.wait_ge(*xh_made(b, 1))
                pe.wait_ge(*tr_kept(b, 0))
                for t in range(HALVES):
                    last = flip(tr_ps[0][:, t, :], xh[:, t, :], ident[:])
                last.then_inc(tr_made.sem, 1)
                pe.wait_ge(*tr_kept(b, 1))
                pe.wait_ge(*x_made(b, 0))
                for t in range(HALVES):
                    mm(s1_ps[t][:, 0, 0:E], xqT[:, t * P:(t + 1) * P], w[:, 0:E], start=True, stop=True)
                    last = mm(s1_ps[t][:, 1, 0:QKV - E], xkT[:, t * P:(t + 1) * P], w[:, E:QKV], start=True, stop=True)
                last.then_inc(qkv_made.sem, 1)
                pe.wait_ge(*pad_made(b, 1))
                for n in range(4):
                    u = use_of["qk", n]
                    pe.wait_ge(*tr_kept(b, max(u - 1, 0)))
                    for g in range(G):
                        last = flip(tr_ps[u % 2][:, g, :], QK_pad[:, n % 2, n // 2, 4 * g:4 * g + 4, :].rearrange("p h d -> p (h d)"), ident[:])
                    last.then_inc(tr_made.sem, 1)
                pe.wait_ge(*tr_kept(b, use_of["qk", 3] + 1))
                for step, n in ORDER:
                    g, r = n // 4, n % 4
                    if step == "s1":
                        pe.wait_ge(*top_made(b, max(n - 1, 0)))
                        if causal:
                            mm(s1_ps[n % 2][:].rearrange("p a k -> p (a k)"), identb[:], mask[:].rearrange("p a k -> p (a k)"),
                               start=True, stop=False, skip_group_check=True)
                        else:
                            pe.wait_ge(consts, CONSTS)
                        for t in range(HALVES):
                            last = mm(s1_ps[n % 2][:, t, :], QT[HP * r:HP * r + D, g, t * P:(t + 1) * P], KT[HP * r:HP * r + D, g, :],
                                      start=not causal, stop=True, skip_group_check=True, tile_position=(HP * r, 0))
                        last.then_inc(s1_made.sem, 1)
                    elif step == "qm":
                        u = use_of["qm", n]
                        pe.wait_ge(*negm_made(b, n + 1))
                        pe.wait_ge(*tr_kept(b, u - 1))
                        for t in range(HALVES):
                            last = flip(tr_ps[u % 2][:, t, :], QK_pad[:, t, 0, 4 * n:4 * n + 4, :].rearrange("p h d -> p (h d)"), ident[:])
                        last.then_inc(tr_made.sem, 1)
                    elif step == "s2":
                        if r == 0:
                            pe.wait_ge(*tr_kept(b, use_of["qm", g] + 1))
                        pe.wait_ge(*p_made(b, max(n - 1, 0)))
                        if causal:
                            mm(s2_ps[n % 2][:].rearrange("p a k -> p (a k)"), identb[:], maskT[:].rearrange("p a k -> p (a k)"),
                               start=True, stop=False, skip_group_check=True)
                        for t in range(HALVES):
                            last = mm(s2_ps[n % 2][:, t, :], KT[HP * r:HP * r + D + 1, g, t * P:(t + 1) * P], QmT[HP * r:HP * r + D + 1, g, :],
                                      start=not causal, stop=True, skip_group_check=True, tile_position=(HP * r, 0))
                        last.then_inc(s2_made.sem, 1)
                    elif step == "pv":
                        pe.wait_ge(*p_made(b, n + 1))
                        if r == 0:
                            pe.wait_ge(*o_kept(b, max(g - 1, 0)))
                            if n == 0:
                                pe.wait_ge(*v_padded(b, 1))
                        for t in range(HALVES):
                            last = mm(o_ps[g % 2][HP * r:HP * r + HP, 0:T], V_pad[:, t, n * KV // H, :], PT[:, n % 3, t, :],
                                      start=(t == 0), stop=(t == 1), skip_group_check=True, tile_position=(0, HP * r))
                        last.then_inc(o_made.sem, 1)
                for t in range(HALVES):
                    u = use_of["o", t]
                    if t == 0:
                        pe.wait_ge(*o_kept(b, G))
                    pe.wait_ge(*tr_kept(b, u - 1))
                    for g in range(G):
                        last = flip(tr_ps[u % 2][:, g, :], OT[:, g, t * P:(t + 1) * P], ident[:])
                    last.then_inc(tr_made.sem, 1)
                u = use_of["att", 0]
                pe.wait_ge(*att_made(b, 2))
                for t in range(HALVES):
                    last = flip(tr_ps[u % 2][:, t, :], att[:, t, :], ident[:])
                last.then_inc(tr_made.sem, 1)
                pe.wait_ge(*tr_kept(b, TRU))
                for t in range(HALVES):
                    last = mm(s1_ps[0][:, t, 0:E], attT[:, t * P:(t + 1) * P], w_out[:], start=True, stop=True)
                last.then_inc(y_made.sem, 1)

        @block.vector
        def _(dve):
            tt, ts, red = nc.vector.tensor_tensor, nc.vector.tensor_scalar, nc.vector.tensor_reduce
            dve.wait_ge(consts, CONSTS)
            dve.wait_ge(const_set, 5)
            with dve.Fori(0, B) as b:
                link = Chain(dve, step_done, b)
                xv = X[:, bass.ds(b * HALVES, HALVES), :]
                if causal:
                    link(tt(sqx[:], xv, xv, ALU.mult))
                    link(red(mv[:, :, 0], sqx[:], op=ALU.add, axis=X_AXIS))
                    ts(veps[:], mv[:, :, 0], 1.0 / E, LN_EPS, ALU.mult, ALU.add).then_inc(var_made.sem, 1)
                    dve.wait_ge(*rstd_made(b, 1))
                    tt(xh[:], xv, bc(rstd[:], 2, E), ALU.mult).then_inc(xh_made.sem, 1)
                else:
                    link(nc.vector.tensor_copy(xh[:], xv))
                    layer_norm(nc, dve, link, xh, stats, mv, veps, rstd, scrap, HALVES, var_made, rstd_made, b)
                    tt(xh[:], xh[:], bc(rstd[:], 2, E), ALU.mult).then_inc(xh_made.sem, 1)
                    link(tt(sqx[:], xv, bc(w_rad[:], 1, HALVES), ALU.mult))
                    link(red(rad[:], sqx[:], op=ALU.add, axis=X_AXIS))
                    link(ts(rad[:], rad[:], b_rad[:, 0:1], None, ALU.add))
                    link(ts(rad[:], rad[:], 0.01, 0.5, ALU.mult, ALU.max))
                    link(ts(rad[:], rad[:], 2.0, None, ALU.min))
                dve.wait_ge(*qkv_made(b, 1))
                dve.wait_ge(*s1_made(b, 0))
                for t in range(HALVES):
                    for lo, hi, o in ((0, E, 0), (E, QKV, 1)):
                        src = s1_ps[t][:, o, 0:hi - lo]
                        if causal:
                            link.free(nc.vector.tensor_copy(qkv[:, t, lo:hi], src))
                        else:
                            link.free(tt(qkv[:, t, lo:hi], src, bias[:, lo:hi], ALU.add))
                dve.wait_ge(*step_done(b, link.n))
                dve.wait_ge(*o_made(b, 0))
                heads = lambda ap, n: ap.rearrange("p t (h d) -> p t h d", h=n)
                nc.vector.tensor_copy(V_pad[:, :, :, 0:D], heads(qkv[:, :, QK * D:QKV], KV)).then_inc(v_padded.sem, 1)
                qk = qkv[:, :, 0:QK * D]
                for t in range(HALVES):
                    link.free(tt(t1[:, t].rearrange("p (h d) -> p h d", h=QK), qk[:, t].rearrange("p (h d) -> p h d", h=QK),
                                 bc(cos[:, t], 1, QK), ALU.mult))
                    for z in range(2):
                        if causal:
                            v = lambda ap: ap.rearrange("p (h z d) -> p h z d", h=QK, z=2)
                            s = sin[:, t].rearrange("p (z d) -> p z d", z=2)[:, z]
                            link.free(tt(v(t2[:, t])[:, :, z], v(qk[:, t])[:, :, 1 - z], bc(s, 1, QK), ALU.mult))
                        else:
                            v = lambda ap: ap.rearrange("p (h d z) -> p h d z", h=QK, z=2)
                            s = sin[:, t].rearrange("p (d z) -> p d z", z=2)[:, :, z]
                            link.free(tt(v(t2[:, t])[:, :, :, z], v(qk[:, t])[:, :, :, 1 - z], bc(s, 1, QK), ALU.mult))
                dve.wait_ge(*step_done(b, link.n))
                dve.wait_ge(*tr_made(b, 0))
                if causal:
                    tt(QK_pad[:, :, 0, :, 0:D], heads(t1[:, :, 0:E], H), heads(t2[:, :, 0:E], H), ALU.add)
                    for t in range(HALVES):
                        v = lambda ap: bc(ap[:, t, E:QK * D].rearrange("p (h d) -> p h d", h=KV), 2, H // KV)
                        last = tt(QK_pad[:, t, 1, :, 0:D].rearrange("p (h r) d -> p h r d", h=KV), v(t1), v(t2), ALU.add)
                    last.then_inc(pad_made.sem, 1)
                else:
                    link(tt(t1[:], t1[:], t2[:], ALU.add))
                    link(tt(t1[:], t1[:], bc(rad[:], 2, QK * D), ALU.mult))
                    th = heads(t1[:], QK)
                    link(red(mean[:], th, op=ALU.add, axis=X_AXIS))
                    link(ts(mean[:], mean[:], 1.0 / D, None, ALU.mult))
                    link(tt(th, th, bc(mean[:], 3, D), ALU.subtract))
                    link(tt(t2[:], t1[:], t1[:], ALU.mult))
                    link(red(hvar[:], heads(t2[:], QK), op=ALU.add, axis=X_AXIS))
                    ts(hvar[:], hvar[:], 1.0 / D, LN_EPS, ALU.mult, ALU.add).then_inc(hvar_made.sem, 1)
                    dve.wait_ge(*hrstd_made(b, 1))
                    link(tt(th, th, bc(hrstd[:], 3, D), ALU.mult))
                    flat = t1[:].rearrange("p t (h d) -> p (t h) d", h=QK)
                    link(tt(flat, flat, bc(w_ln[:], 1, 2 * QK), ALU.mult))
                    tt(QK_pad[:].rearrange("p t c h d -> p (t c h) d")[:, :, 0:D], flat, bc(b_ln[:], 1, 2 * QK), ALU.add) \
                        .then_inc(pad_made.sem, 1)
                for step, n in ORDER:
                    if step == "s1":
                        dve.wait_ge(*s1_made(b, n + 1))
                        red(top[:, n, :], s1_ps[n % 2][:], op=ALU.max, axis=X_AXIS).then_inc(top_made.sem, 1)
                    elif step == "qm":
                        dve.wait_ge(*top_made(b, 4 * n + 4))
                        ts(QK_pad[:, :, 0, 4 * n:4 * n + 4, D], top[:, 4 * n:4 * n + 4, :].rearrange("p h t -> p t h"), -1.0, None, ALU.mult) \
                            .then_inc(negm_made.sem, 1)
                for t in range(HALVES):
                    u = use_of["o", t]
                    dve.wait_ge(*tr_made(b, u + 1))
                    o = tr_ps[u % 2][:].rearrange("p g (r d) -> p (g r) d", d=HP)
                    link(nc.vector.reciprocal(rec[:, t, :], o[:, :, D]))
                    tt(att[:, t].rearrange("p (h d) -> p h d", d=D), o[:, :, 0:D], bc(rec[:, t, :], 2, D), ALU.mult) \
                        .then_inc(att_made.sem, 1)
                    dve.wait_ge(*att_made(b, t + 1))
                    nc.vector.memset(scrap[:], 0.0).then_inc(tr_kept.sem, 1)
                dve.wait_ge(*y_made(b, 1))
                yv = s1_ps[0][:, :, 0:E]
                if causal:
                    link(tt(y[:], yv, xv, ALU.add))
                    ts(xv, y[:], 100.0, -100.0, ALU.min, ALU.max).then_inc(x_made.sem, 1)
                else:
                    link(tt(y[:], yv, bc(b_out[:], 1, HALVES), ALU.add))
                    link(tt(y[:], y[:], xv, ALU.add))
                    layer_norm(nc, dve, link, y, stats, mv, veps, rstd, scrap, HALVES, var2_made, rstd2_made, b)
                    tt(xv, y[:], bc(rstd[:], 2, E), ALU.mult).then_inc(x_made.sem, 1)
                dve.wait_ge(*x_made(b, 1))
                assert link.n == DVE_STEPS, link.n


def experts(nc, X, a):
    N, F = 8, 256
    FK = F // P
    FS = 2
    FT = FS * HALVES
    TURNS = B // FS
    with Core(nc, "moe") as m:
        ident = m.sb("ident", [P])
        w_r = m.sb("w_r", [N])
        w_g, w_u = m.sb("w_g", [N, F]), m.sb("w_u", [N, F])
        w_d = m.sb("w_d", [N, FK, E])
        g2 = m.sb("g2", [1])
        lower = m.sb("lower", [N, N])
        neg_half = m.sb("neg_half", [FT])
        sqx, xh = m.sb("sqx", [FT, E]), m.sb("xh", [FT, E])
        ssq, veps, rstd = m.sb("ssq", [FT]), m.sb("veps", [FT]), m.sb("rstd", [FT])
        xT = m.sb("xT", [FT * P])
        prob, top, den = m.sb("prob", [FT, N]), m.sb("top", [FT]), m.sb("den", [FT])
        cmp1, cmp2 = m.sb("cmp1", [FT, N, N]), m.sb("cmp2", [FT, N, N])
        rank, gate = m.sb("rank", [FT, N]), m.sb("gate", [FT, N])
        act_g = m.sb("act_g", [2, FT * P])
        hid = m.sb("hid", [2, FK, FT * P])
        acc = m.sb("acc", [FT, E])
        g_ps = [m.ps(f"g_ps{i}", [FT * P]) for i in range(2)]
        u_ps = [m.ps(f"u_ps{i}", [FT * P]) for i in range(2)]
        d_ps = [m.ps(f"d_ps{i}", [FT, E]) for i in range(2)]
        tr_ps = m.ps("tr_ps", [FT, P])
        r_ps = m.ps("r_ps", [FT, N])
        consts, const_set = m.sem("consts"), m.sem("const_set")
        STEPS = 17 + (FT - 1) * N
        (var_made, rstd_made, xh_made, xT_made, xT_kept, route_made, shift_made, exp_made, gu_made, silu_made,
         hid_made, down_made, added, x_made, step_done), signals = m.signals(
            var_made=1, rstd_made=1, xh_made=1, xT_made=1, xT_kept=1, route_made=1, shift_made=1, exp_made=1,
            gu_made=N * FK, silu_made=N * FK, hid_made=N * FK, down_made=N, added=N, x_made=1, step_done=STEPS)
        dmas = [(ident, "ident"), (w_r, "moe_w_r"), (g2, "moe_g2")]
        block = m.block()

        @block.sync
        def _(sp):
            for signal in signals:
                sp.sem_inc(signal.sem, signal.start)
            for dst, name in dmas:
                sp.dma_start(dst[:], a[name]).then_inc(consts, 16)
            sp.dma_start(w_g[:], a["moe_w_g"].rearrange("e p f -> p e f")).then_inc(consts, 16)
            sp.dma_start(w_u[:], a["moe_w_u"].rearrange("e p f -> p e f")).then_inc(consts, 16)
            sp.dma_start(w_d[:], a["moe_w_d"].rearrange("e (k p) n -> p e k n", p=P)).then_inc(consts, 16)
            sp.dma_start(lower[:].rearrange("p a b -> p (a b)"), a["moe_lower"].partition_broadcast(P)).then_inc(consts, 16)

        @block.gpsimd
        def _(pool):
            pool.memset(neg_half[:], -0.5).then_inc(const_set, 1)
            pool.wait_ge(const_set, 1)
            with pool.Fori(0, TURNS) as c:
                pool.wait_ge(*var_made(c, 1))
                pool.tensor_tensor(rstd[:], veps[:], neg_half[:], ALU.pow).then_inc(rstd_made.sem, 1)

        @block.scalar
        def _(act):
            act.wait_ge(consts, 112)
            with act.Fori(0, TURNS) as c:
                act.wait_ge(*xT_made(c, 1))
                act.wait_ge(*down_made(c, 0))
                nc.scalar.activation(xT[:], tr_ps[:].rearrange("p t c -> p (t c)"), ACT.Copy, scale=g2[:, 0:1]) \
                    .then_inc(xT_kept.sem, 1)
                act.wait_ge(*shift_made(c, 1))
                nc.scalar.activation(prob[:], prob[:], ACT.Exp).then_inc(exp_made.sem, 1)
                for n in range(N * FK):
                    act.wait_ge(*gu_made(c, n + 1))
                    act.wait_ge(*hid_made(c, max(n - 1, 0)))
                    nc.scalar.activation(act_g[:, n % 2, :], g_ps[n % 2][:], ACT.Silu).then_inc(silu_made.sem, 1)

        @block.tensor
        def _(pe):
            mm = nc.tensor.matmul
            pe.wait_ge(consts, 112)

            def down(c, e):
                pe.wait_ge(*hid_made(c, FK * e + FK))
                pe.wait_ge(*added(c, max(e - 1, 0)))
                for t in range(FT):
                    for k in range(FK):
                        last = mm(d_ps[e % 2][:, t, :], hid[:, e % 2, k, t * P:(t + 1) * P], w_d[:, e, k, :],
                                  start=(k == 0), stop=(k == FK - 1))
                last.then_inc(down_made.sem, 1)

            with pe.Fori(0, TURNS) as c:
                pe.wait_ge(*xh_made(c, 1))
                pe.wait_ge(*xT_kept(c, 0))
                for t in range(FT):
                    last = nc.tensor.transpose(tr_ps[:, t, :], xh[:, t, :], ident[:])
                last.then_inc(xT_made.sem, 1)
                pe.wait_ge(*xT_kept(c, 1))
                for t in range(FT):
                    last = mm(r_ps[:, t, :], xT[:, t * P:(t + 1) * P], w_r[:], start=True, stop=True)
                last.then_inc(route_made.sem, 1)
                for e in range(N):
                    for k in range(FK):
                        n = FK * e + k
                        pe.wait_ge(*hid_made(c, max(n - 1, 0)))
                        mm(g_ps[n % 2][:], w_g[:, e, k * P:(k + 1) * P], xT[:], start=True, stop=True)
                        mm(u_ps[n % 2][:], w_u[:, e, k * P:(k + 1) * P], xT[:], start=True, stop=True).then_inc(gu_made.sem, 1)
                    if e:
                        down(c, e - 1)
                down(c, N - 1)

        @block.vector
        def _(dve):
            tt, ts, red = nc.vector.tensor_tensor, nc.vector.tensor_scalar, nc.vector.tensor_reduce
            dve.wait_ge(consts, 112)

            def add_expert(c, link, e):
                dve.wait_ge(*down_made(c, e + 1))
                for t in range(FT):
                    if e == 0:
                        ins = ts(acc[:, t, :], d_ps[0][:, t, :], gate[:, t, e:e + 1], None, ALU.mult)
                    else:
                        ins = nc.vector.scalar_tensor_tensor(acc[:, t, :], d_ps[e % 2][:, t, :], gate[:, t, e:e + 1], acc[:, t, :],
                                                             ALU.mult, ALU.add)
                    if t == FT - 1:
                        ins.then_inc(added.sem, 1)
                    else:
                        link.free(ins)
                dve.wait_ge(*added(c, e + 1))

            with dve.Fori(0, TURNS) as c:
                link = Chain(dve, step_done, c)
                xv = X[:, bass.ds(c * FT, FT), :]
                link(tt(sqx[:], xv, xv, ALU.mult))
                link(red(ssq[:], sqx[:], op=ALU.add, axis=X_AXIS))
                ts(veps[:], ssq[:], 1.0 / E, LN_EPS, ALU.mult, ALU.add).then_inc(var_made.sem, 1)
                dve.wait_ge(*rstd_made(c, 1))
                tt(xh[:], xv, bc(rstd[:], 2, E), ALU.mult).then_inc(xh_made.sem, 1)
                dve.wait_ge(*route_made(c, 1))
                link(red(top[:], r_ps[:], op=ALU.max, axis=X_AXIS))
                tt(prob[:], r_ps[:], bc(top[:], 2, N), ALU.subtract).then_inc(shift_made.sem, 1)
                dve.wait_ge(*exp_made(c, 1))
                link(red(den[:], prob[:], op=ALU.add, axis=X_AXIS))
                link(nc.vector.reciprocal(den[:], den[:]))
                link(tt(prob[:], prob[:], bc(den[:], 2, N), ALU.mult))
                other, own = bc(prob[:], 2, N), bc(prob[:], 3, N)
                link(tt(cmp1[:], other, own, ALU.is_gt))
                link(tt(cmp2[:], other, own, ALU.is_equal))
                link(tt(cmp2[:], cmp2[:], bc(lower[:], 1, FT), ALU.mult))
                link(tt(cmp1[:], cmp1[:], cmp2[:], ALU.add))
                link(red(rank[:], cmp1[:], op=ALU.add, axis=X_AXIS))
                link(ts(rank[:], rank[:], 2.0, None, ALU.is_lt))
                link(tt(gate[:], prob[:], rank[:], ALU.mult))
                link(red(den[:], gate[:], op=ALU.add, axis=X_AXIS))
                link(nc.vector.reciprocal(den[:], den[:]))
                link(tt(gate[:], gate[:], bc(den[:], 2, N), ALU.mult))
                for e in range(N):
                    for k in range(FK):
                        n = FK * e + k
                        dve.wait_ge(*silu_made(c, n + 1))
                        dve.wait_ge(*down_made(c, max(e - 1, 0)))
                        tt(hid[:, e % 2, k, :], act_g[:, n % 2, :], u_ps[n % 2][:], ALU.mult).then_inc(hid_made.sem, 1)
                    if e:
                        add_expert(c, link, e - 1)
                add_expert(c, link, N - 1)
                link(tt(acc[:], acc[:], xv, ALU.add))
                ts(xv, acc[:], 100.0, -100.0, ALU.min, ALU.max).then_inc(x_made.sem, 1)
                dve.wait_ge(*x_made(c, 1))
                assert link.n == STEPS, link.n


def build(nc, a, out):
    with Core(nc, "all") as m:
        X = m.sb("X", [TILES, E])
        X0 = m.sb("X0", [TILES, E])
        load_x(nc, a["x"], X)
        if 1 in STAGES:
            head_mixer(nc, X, a["ident"], None, a["mix_mask"], a["mix_w"], a["mix_bias"], a["inv_count"], a["count"])
        if 2 in STAGES:
            layer_stack(nc, X, X0, a)
            add_norm(nc, X0, X, "norm_stack")
        if 3 in STAGES:
            small_heads(nc, X, a, causal=False)
        if 4 in STAGES:
            copy_x(nc, X, X0)
            small_heads(nc, X, a, causal=True)
            experts(nc, X, a)
            add_norm(nc, X0, X, "norm_moe")
        store_x(nc, X, out)


def kernel(**inputs):
    import numpy as np
    import ml_dtypes
    import concourse.bacc as bacc
    from concourse.bass_utils import run_bass_kernel_spmd

    f = lambda n: np.asarray(inputs[n])
    a = {"x": f("L0_attn_y_de").reshape(B * T, E), "ident": np.eye(P, dtype=np.float32)}
    w = np.zeros((E, 3, 16, 8), np.float32)
    for j, n in enumerate("qkv"):
        for h in range(16):
            w[8 * h:8 * h + 8, j, h, :] = f(f"L0_attn_W{n}").T
    a["mix_w"] = w.reshape(E, 3 * E)
    a["mix_bias"] = np.concatenate([np.tile(f(f"L0_attn_b{n}"), 16) for n in "qkv"])
    t = np.arange(T)[:, None]
    a["mix_mask"] = (np.arange(E)[None, :] < t).astype(np.float32).reshape(HALVES, P, E).transpose(1, 0, 2).copy()
    a["inv_count"] = (1.0 / np.arange(1, 17)).astype(np.float32)
    a["count"] = np.arange(1, 17).astype(np.float32)

    a["identb"] = np.eye(P).astype(ml_dtypes.bfloat16)
    W = 32
    rows, keys = np.arange(P), np.arange(2 * W)
    q = rows % W
    win = np.zeros((P, 4, 2, 2 * W))
    for j in range(2):
        bad = (keys[None, :] < q[:, None]) | (keys[None, :] > q[:, None] + W)
        bad |= (rows[:, None] < W) & (j == 0) & (keys[None, :] < W)
        win[:, :, j, :] = np.where(bad, MASKED, 0.0)[:, None, :]
    a["win_mask"] = win.astype(ml_dtypes.bfloat16)
    half = np.arange(0, 64, 2, dtype=np.float64)
    freqs = (np.arange(T, dtype=np.float32)[:, None] * (1.0 / 10000.0 ** (half / 64)).astype(np.float32)[None, :]).astype(np.float64)
    base = (half + 0.4 * 64) / (1.4 * 64)
    scale = base[None, :] ** ((np.arange(T) - T // 2) / 16)[:, None]
    two = lambda x: np.concatenate([x, x], 1)
    cos, scale = two(np.cos(freqs)), two(scale)
    sin = np.concatenate([-np.sin(freqs), np.sin(freqs)], 1)
    tok = lambda x: np.stack(x, 1).reshape(HALVES, P, len(x), -1).transpose(1, 0, 2, 3).astype(np.float32)
    a["cos0"] = tok([cos * scale * 8.0, cos / scale])
    a["sin0"] = tok([sin * scale * 8.0, sin / scale])
    F, FP = 341, 384
    a["wqkv"], a["wo"], a["w1"] = f("L0_ffn_Wqkv"), f("L0_ffn_Wo"), f("L0_ffn_W1")
    w2 = np.zeros((6, FP, E), np.float32)
    w2[:, :F] = f("L0_ffn_W2")
    b1 = np.zeros((6, 2, FP), np.float32)
    b1[:, :, :F] = f("L0_ffn_b1").reshape(6, 2, F)
    a["w2"], a["b1"], a["b2"] = w2, b1.reshape(6, 2, 3, P).transpose(0, 3, 1, 2).reshape(6, P, 6), f("L0_ffn_b2")
    a["qk_scale"] = np.concatenate([f("L0_ffn_q_scale"), f("L0_ffn_k_scale")], 1)
    a["ln_g"], a["ln_b"] = f("L0_ffn_ln_g")[:, :, None], f("L0_ffn_ln_b")[:, :, None]

    mel = 2595.0 * np.log10(1.0 + 4000.0 / 200.0)
    fb = 200.0 * (10.0 ** (np.linspace(0.0, mel, 4) / 2595.0) - 1.0) / 1000.0
    ang = (np.arange(T, dtype=np.float32)[:, None] * fb.astype(np.float32)[None, :]).astype(np.float64)
    pairs = lambda x, y: np.stack([x, y], -1).reshape(T, -1)
    halves = lambda x: x.reshape(HALVES, P, -1).transpose(1, 0, 2).astype(np.float32)
    a["rot_cos"], a["rot_sin"] = halves(pairs(np.cos(ang), np.cos(ang))), halves(pairs(-np.sin(ang), np.sin(ang)))
    a["rot_w"] = np.concatenate([f("L1_attn_q_w"), f("L1_attn_kv_w")], 1)
    a["rot_bias"] = np.concatenate([f("L1_attn_q_b"), f("L1_attn_kv_b")])
    a["rot_w_out"], a["rot_b_out"] = f("L1_attn_out_w"), f("L1_attn_out_b")
    a["rot_w_rad"], a["rot_b_rad"] = f("L1_attn_rh_w")[:, 0], f("L1_attn_rh_b")
    a["rot_w_ln"], a["rot_b_ln"] = f("L1_attn_ln_w"), f("L1_attn_ln_b")
    a["rot_aff"] = np.stack([f(f"L1_attn_{n}") for n in ("qn_w", "qn_b", "kvn_w", "kvn_b")], 1)
    ang = (np.arange(T, dtype=np.float32)[:, None] * (1.0 / 10000.0 ** (np.arange(0, 8, 2) / 8)).astype(np.float32)[None, :]).astype(np.float64)
    a["cau_cos"] = halves(np.concatenate([np.cos(ang), np.cos(ang)], 1))
    a["cau_sin"] = halves(np.concatenate([-np.sin(ang), np.sin(ang)], 1))
    a["cau_w"] = np.concatenate([f(f"L1_ffn_W{n}") for n in "qkv"], 1)
    a["cau_w_out"] = f("L1_ffn_Wo")
    g1, zero = f("L1_ffn_ln1_w"), np.zeros(E, np.float32)
    a["cau_aff"] = np.stack([g1, zero, g1, zero], 1)
    t = np.arange(T)
    see = np.where(t[None, :] <= t[:, None], 0.0, MASKED)
    fold = lambda x: x.reshape(HALVES, P, T).transpose(1, 0, 2).astype(ml_dtypes.bfloat16)
    a["causal"], a["causal_t"] = fold(see), fold(see.T)
    a["moe_w_r"], a["moe_g2"] = f("L1_ffn_Wr"), f("L1_ffn_ln2_w")[:, None]
    a["moe_w_g"], a["moe_w_u"], a["moe_w_d"] = f("L1_ffn_Wg"), f("L1_ffn_Wu"), f("L1_ffn_Wd")
    a["moe_lower"] = (np.arange(8)[None, :] < np.arange(8)[:, None]).astype(np.float32).reshape(-1)

    nc = bacc.Bacc("TRN2", target_bir_lowering=False, num_devices=1)
    arrays, aps = {}, {}
    for n, v in a.items():
        v = np.ascontiguousarray(v)
        arrays[f"in_{n}"] = v
        aps[n] = nc.dram_tensor(f"in_{n}", v.shape, mybir.dt.from_np(v.dtype), kind="ExternalInput").ap()
    out = nc.dram_tensor("out_x", (B * T, E), F32, kind="ExternalOutput").ap()
    build(nc, aps, out)
    r = run_bass_kernel_spmd(nc, [arrays], core_ids=[0])
    return np.asarray(r.results[0]["out_x"]).reshape(B, T, E)
```

```python
from contextlib import ExitStack

import concourse.bass as bass
from concourse import mybir

ALU = mybir.AluOpType
ACT = mybir.ActivationFunctionType
F32 = mybir.dt.float32
BF16 = mybir.dt.bfloat16
X_AXIS = mybir.AxisListType.X

P = 128
B, T, E = 16, 256, 128
HALVES = T // P
TILES = B * HALVES
LN_EPS = 1e-5
MASKED = -1e30
STAGES = (1, 2, 3, 4)
DEPTH = 6


class Core:

    def __init__(self, nc, stage):
        self.nc, self.stage, self.ctx = nc, stage, ExitStack()

    def __enter__(self):
        return self

    def __exit__(self, *a):
        return self.ctx.__exit__(*a)

    def sb(self, name, shape, dt=F32):
        return self.ctx.enter_context(self.nc.sbuf_tensor(f"{self.stage}_{name}", [P] + list(shape), dt))

    def ps(self, name, shape, dt=F32):
        return self.ctx.enter_context(self.nc.psum_tensor(f"{self.stage}_{name}", [P] + list(shape), dt))

    def sem(self, name):
        return self.ctx.enter_context(self.nc.semaphore(f"{self.stage}_{name}"))

    def signals(self, **per_turn):
        made = [Signal(self.sem(n), k) for n, k in per_turn.items()]
        return made, made

    def block(self):
        return self.ctx.enter_context(self.nc.Block())


class Signal:

    def __init__(self, sem, per_turn):
        self.sem, self.per_turn, self.start = sem, per_turn, 3 * per_turn + 1

    def __call__(self, turn, k):
        return self.sem, turn * self.per_turn + (self.start + k)


class Chain:

    def __init__(self, eng, ends, turn):
        self.eng, self.ends, self.turn, self.n = eng, ends, turn, 0

    def __call__(self, ins):
        self.free(ins)
        self.eng.wait_ge(*self.ends(self.turn, self.n))

    def free(self, ins):
        self.n += 1
        ins.then_inc(self.ends.sem, 1)


def hold(eng, scrap):
    eng.memset(scrap[:], 0.0)


def bc(ap, axis, n):
    ap = ap.unsqueeze(axis)
    return ap.broadcast_to([n if i == axis else d for i, d in enumerate(ap.shape)])


def layer_norm(nc, dve, link, h, stats, mv, veps, rstd, scrap, n, var_made, rstd_made, turn):
    for j in range(n):
        link.free(nc.vector.bn_stats(stats[:, j, :], h[:, j, :]))
    dve.wait_ge(*link.ends(turn, link.n))
    hold(nc.vector, scrap)
    for j in range(n):
        link.free(nc.vector.bn_aggr(mv[:, j, :], stats[:, j, :]))
    dve.wait_ge(*link.ends(turn, link.n))
    nc.vector.tensor_scalar(veps[:], mv[:, :, 1], LN_EPS, None, ALU.add).then_inc(var_made.sem, 1)
    link(nc.vector.tensor_tensor(h[:], h[:], bc(mv[:, :, 0], 2, E), ALU.subtract))
    dve.wait_ge(*rstd_made(turn, 1))


def load_x(nc, x_in, X, neg_half):
    with Core(nc, "load") as m:
        landed = m.sem("landed")
        block = m.block()

        @block.sync
        def _(sp):
            sp.dma_start(X[:], x_in.rearrange("(i p) e -> p i e", p=P)).then_inc(landed, 16)
            sp.wait_ge(landed, 17)

        @block.gpsimd
        def _(pool):
            pool.memset(neg_half[:], -0.5).then_inc(landed, 1)


def store_x(nc, X, out):
    with Core(nc, "store") as m:
        stored = m.sem("stored")
        block = m.block()

        @block.sync
        def _(sp):
            sp.dma_start(out.rearrange("(i p) e -> p i e", p=P), X[:]).then_inc(stored, 16)
            sp.wait_ge(stored, 16)


def head_mixer(nc, X, neg_half, ident_in, mask_in, w_in, bias_in, invk_in, idx_in):
    H, D = 16, 8
    G = H
    CH = 8
    TURNS = TILES // CH
    R = CH * H
    SCALE = 0.5 / float(E) ** 0.5
    QKV = 3 * E
    with Core(nc, "mix") as m:
        ident = m.sb("ident", [P])
        mask = m.sb("mask", [HALVES, E])
        w = m.sb("w", [QKV])
        bias = m.sb("bias", [QKV])
        invk = m.sb("invk", [G])
        idx = m.sb("idx", [G])
        xm = m.sb("xm", [CH, E])
        xT = m.sb("xT", [CH, P])
        qkv = m.sb("qkv", [CH, QKV])
        prod = m.sb("prod", [3, H * G * D])
        S = m.sb("S", [G, R])
        U = m.sb("U", [G, R])
        V = m.sb("V", [G, R])
        C1 = m.sb("C1", [G, R])
        C2 = m.sb("C2", [G, R])
        top = m.sb("top", [R])
        tau = m.sb("tau", [R])
        o = m.sb("o", [CH, E])
        scrap = m.sb("scrap", [1])
        stats = m.sb("stats", [CH, 6])
        mv = m.sb("mv", [CH, 2])
        veps = m.sb("veps", [CH])
        rstd = m.sb("rstd", [CH])
        xT_ps = m.ps("xT_ps", [2, 4, P])
        qkv_ps = m.ps("qkv_ps", [4, 512])

        consts = m.sem("consts")
        DVE_STEPS = 100 + CH
        (masked, xT_made, xT_kept, qkv_made, qkv_kept, mult, qk_summed, attn_made, av_summed,
         delta_made, root_made, var_made, rstd_made, dve_step), signals = m.signals(
            masked=1, xT_made=2, xT_kept=2, qkv_made=CH, qkv_kept=CH, mult=CH, qk_summed=CH, attn_made=1,
            av_summed=CH, delta_made=1, root_made=1, var_made=1, rstd_made=1, dve_step=DVE_STEPS)
        block = m.block()

        def qk_product(eng, j):
            q = qkv[:, j, 0:E].rearrange("p (h d) -> p h d", d=D)
            k = qkv[:, j, E:2 * E].rearrange("p (g d) -> p g d", d=D)
            return eng.tensor_tensor(buf(j).rearrange("p (h g d) -> p h g d", h=H, g=G), bc(q, 2, G), bc(k, 1, H), ALU.mult)

        def av_product(eng, j):
            a = S[:, :, j * H:(j + 1) * H].rearrange("p g h -> p h g")
            v = qkv[:, j, 2 * E:3 * E].rearrange("p (g d) -> p d g", d=D)
            return eng.tensor_tensor(buf(j).rearrange("p (h d g) -> p h d g", h=H, g=G), bc(a, 2, D), bc(v, 1, H), ALU.mult)

        def buf(j):
            return prod[:, 1 + j // 2 % 2 if j % 2 else 0, :]

        @block.sync
        def _(sp):
            for signal in signals:
                sp.sem_inc(signal.sem, signal.start)
            for dst, src in ((ident, ident_in), (mask, mask_in), (w, w_in)):
                sp.dma_start(dst[:], src).then_inc(consts, 16)
            for dst, src in ((bias, bias_in), (invk, invk_in), (idx, idx_in)):
                sp.dma_start(dst[:], src.partition_broadcast(P)).then_inc(consts, 16)

        @block.gpsimd
        def _(pool):
            pool.wait_ge(consts, 96)
            with pool.Fori(0, TURNS) as c:
                pool.wait_ge(*xT_made(c, 0))
                pool.tensor_tensor(xm[:].rearrange("p (a b) e -> p a b e", b=HALVES),
                                   X[:, bass.ds(c * CH, CH), :].rearrange("p (a b) e -> p a b e", b=HALVES),
                                   bc(mask[:], 1, CH // HALVES), ALU.mult).then_inc(masked.sem, 1)
                for j in range(1, CH, 2):
                    pool.wait_ge(*qkv_kept(c, j + 1))
                    pool.wait_ge(*(qk_summed(c, j - 3) if j >= 4 else av_summed(c, 0)))
                    qk_product(pool, j).then_inc(mult.sem, 1)
                pool.wait_ge(*attn_made(c, 1))
                for j in range(1, CH, 2):
                    if j >= 4:
                        pool.wait_ge(*av_summed(c, j - 3))
                    av_product(pool, j).then_inc(mult.sem, 1)
                pool.wait_ge(*var_made(c, 1))
                pool.tensor_tensor(rstd[:], veps[:], neg_half[:], ALU.pow).then_inc(rstd_made.sem, 1)

        @block.scalar
        def _(act):
            with act.Fori(0, TURNS) as c:
                for n in range(2):
                    act.wait_ge(*xT_made(c, n + 1))
                    act.wait_ge(*qkv_made(c, 0))
                    nc.scalar.copy(xT[:, 4 * n:4 * n + 4, :], xT_ps[:, n, :, :]).then_inc(xT_kept.sem, 1)
                act.wait_ge(*delta_made(c, 1))
                nc.scalar.activation(U[:], U[:], ACT.Sqrt).then_inc(root_made.sem, 1)

        @block.tensor
        def _(pe):
            pe.wait_ge(consts, 96)
            with pe.Fori(0, TURNS) as c:
                pe.wait_ge(*masked(c, 1))
                pe.wait_ge(*xT_kept(c, 0))
                for j in range(CH):
                    t = nc.tensor.transpose(xT_ps[:, j // 4, j % 4, :], xm[:, j, :], ident[:])
                    if j % 4 == 3:
                        t.then_inc(xT_made.sem, 1)
                for j in range(CH):
                    pe.wait_ge(*xT_kept(c, j // 4 + 1))
                    if j >= 4:
                        pe.wait_ge(*qkv_kept(c, j - 3))
                    else:
                        pe.wait_ge(*qkv_kept(c, 0))
                    nc.tensor.matmul(qkv_ps[:, j % 4, 0:QKV], xT[:, j, :], w[:], start=True, stop=True) \
                        .then_inc(qkv_made.sem, 1)

        def dve_turn(dve, c):
            link = Chain(dve, dve_step, c)
            tt, ts = nc.vector.tensor_tensor, nc.vector.tensor_scalar
            for j in range(CH):
                dve.wait_ge(*qkv_made(c, j + 1))
                if j == 0:
                    dve.wait_ge(*mult(c, 0))
                tt(qkv[:, j, :], qkv_ps[:, j % 4, 0:QKV], bias[:], ALU.add).then_inc(qkv_kept.sem, 1)
            for j in range(CH):
                if j % 2:
                    dve.wait_ge(*mult(c, j // 2 + 1))
                else:
                    dve.wait_ge(*(qk_summed(c, j - 1) if j else av_summed(c, 0)))
                    dve.wait_ge(*qkv_kept(c, j + 1))
                    link(qk_product(nc.vector, j))
                ins = nc.vector.tensor_reduce(S[:, :, j * H:(j + 1) * H].rearrange("p g h -> p h g"),
                                              buf(j).rearrange("p (h g d) -> p h g d", h=H, g=G),
                                              op=ALU.add, axis=X_AXIS)
                ins.then_inc(qk_summed.sem, 1)
            dve.wait_ge(*qk_summed(c, CH))
            link(nc.vector.tensor_reduce(top[:], S[:].rearrange("p g r -> p r g"), op=ALU.max, axis=X_AXIS))
            link(tt(S[:], S[:], bc(top[:], 1, G), ALU.subtract))
            link(ts(S[:], S[:], SCALE, None, ALU.mult))
            src, dst = S, U
            for k in (2, 4, 8, 16):
                j = k // 2
                while j:
                    for up in (0, 1) if k < G else (0,):
                        v = lambda t, hi: (t[:].rearrange("p (a u b z l) r -> p a u b z (l r)", u=2, b=k // (2 * j), z=2, l=j)[:, :, up, :, hi, :]
                                           if k < G else
                                           t[:].rearrange("p (b z l) r -> p b z (l r)", z=2, l=j)[:, :, hi, :])
                        link(tt(v(dst, up), v(src, 0), v(src, 1), ALU.max))
                        link(tt(v(dst, 1 - up), v(src, 0), v(src, 1), ALU.min))
                    src, dst = dst, (V if dst is U else U)
                    j //= 2
            xs, tmp = src, dst
            assert xs is V and tmp is U
            link(tt(C2[:], xs[:], xs[:], ALU.mult))
            link(nc.vector.tensor_copy(C1[:, 0, :], xs[:, 0, :]))
            for k in range(1, G):
                link.free(tt(C1[:, k, :], C1[:, k - 1, :], xs[:, k, :], ALU.add))
                link(tt(C2[:, k, :], C2[:, k - 1, :], C2[:, k, :], ALU.add))
            ik = bc(invk[:], 2, R)
            link(tt(tmp[:], C1[:], ik, ALU.mult))
            link(tt(C1[:], C1[:], tmp[:], ALU.mult))
            link(tt(C2[:], C2[:], C1[:], ALU.subtract))
            link(ts(C2[:], C2[:], -1.0, 1.0, ALU.mult, ALU.add))
            link(tt(C1[:], C2[:], ik, ALU.mult))
            link(nc.vector.tensor_copy(C2[:], tmp[:]))
            ts(U[:], C1[:], 0.0, None, ALU.max).then_inc(delta_made.sem, 1)
            dve.wait_ge(*root_made(c, 1))
            link(tt(C2[:], C2[:], U[:], ALU.subtract))
            link(tt(U[:], C2[:], xs[:], ALU.is_le))
            link(nc.vector.tensor_reduce(top[:], U[:].rearrange("p g r -> p r g"), op=ALU.add, axis=X_AXIS))
            link(tt(U[:], bc(top[:], 1, G), bc(idx[:], 2, R), ALU.is_equal))
            link(tt(U[:], U[:], C2[:], ALU.mult))
            link(nc.vector.tensor_reduce(tau[:], U[:].rearrange("p g r -> p r g"), op=ALU.add, axis=X_AXIS))
            link(tt(S[:], S[:], bc(tau[:], 1, G), ALU.subtract))
            link(ts(S[:], S[:], 0.0, None, ALU.max))
            tt(S[:], S[:], S[:], ALU.mult).then_inc(attn_made.sem, 1)
            for j in range(CH):
                if j % 2:
                    dve.wait_ge(*mult(c, (CH + j) // 2 + 1))
                else:
                    if j:
                        dve.wait_ge(*av_summed(c, j - 1))
                    else:
                        dve.wait_ge(*attn_made(c, 1))
                    link(av_product(nc.vector, j))
                nc.vector.tensor_reduce(o[:, j, :].rearrange("p (h d) -> p h d", d=D),
                                        buf(j).rearrange("p (h d g) -> p h d g", h=H, g=G),
                                        op=ALU.add, axis=X_AXIS).then_inc(av_summed.sem, 1)
            dve.wait_ge(*av_summed(c, CH))
            xv = X[:, bass.ds(c * CH, CH), :]
            link(tt(o[:], o[:], xv, ALU.add))
            layer_norm(nc, dve, link, o, stats, mv, veps, rstd, scrap, CH, var_made, rstd_made, c)
            link(tt(xv, o[:], bc(rstd[:], 2, E), ALU.mult))
            assert link.n == DVE_STEPS, link.n

        @block.vector
        def _(dve):
            dve.wait_ge(consts, 96)
            with dve.Fori(0, TURNS) as c:
                dve_turn(dve, c)


def layer_stack(nc, X, X0, neg_half, a):
    H, D, W = 16, 64, 32
    NW = T // W
    PAIRS = H // 2
    QUADS, OCTS = 4, 2
    INNER = H * D
    F = int(E * 4 * 2 / 3)
    FC = [(f, min(P, F - f)) for f in range(0, F, P)]
    PROJ = QUADS * HALVES
    with Core(nc, "stack") as m:
        ident, identb = m.sb("ident", [P]), m.sb("identb", [P], BF16)
        mask = m.sb("mask", [PAIRS // OCTS, 2, 2 * W], BF16)
        cos0 = m.sb("cos0", [HALVES, 2, D])
        sin0 = m.sb("sin0", [HALVES, 2, D])
        cosq = m.sb("cosq", [HALVES, 2, D])
        sinq = m.sb("sinq", [HALVES, 2, D])
        qks = m.sb("qks", [2, D])
        wqk = m.sb("wqk", [QUADS, 2, 4 * D])
        wv = m.sb("wv", [INNER])
        wo = m.sb("wo", [PAIRS, E])
        w1 = m.sb("w1", [2 * F])
        w2 = m.sb("w2", [len(FC), E])
        lng, lnb = m.sb("lng", [1]), m.sb("lnb", [1])
        b1 = m.sb("b1", [2, len(FC)])
        b2 = m.sb("b2", [E])
        scrap = m.sb("scrap", [1])
        consts = m.sem("consts")
        CONSTS = 6 * 16 + 4
        (attn_weights, ffn_weights, tables_made), sig1 = m.signals(attn_weights=16 * 5, ffn_weights=16 * 6, tables_made=1)

        xs = m.sb("xs", [HALVES, E])
        hT = m.sb("hT", [W + T])
        sq = m.sb("sq", [2, 8 * D])
        ss = m.sb("ss", [PROJ, 8])
        rn = m.sb("rn", [PROJ, 8])
        raw = m.sb("raw", [2, 8 * D])
        qn = m.sb("qn", [2, 8 * D])
        t1 = m.sb("t1", [2, 8 * D])
        t2 = m.sb("t2", [2, 8 * D])
        QT = m.sb("QT", [PAIRS, T])
        KT = m.sb("KT", [PAIRS, W + T])
        V = m.sb("V", [2, HALVES, INNER])
        pr = m.sb("pr", [OCTS, 2, 4 * P])
        top = m.sb("top", [OCTS, 2, 8])
        den = m.sb("den", [OCTS, 2, 8])
        inv = m.sb("inv", [OCTS, 2, 8])
        PT = m.sb("PT", [OCTS, 2, 4, P])
        O = m.sb("O", [2, 4 * P])
        OT = m.sb("OT", [PAIRS, T])
        FS = 2
        FT = FS * HALVES
        fx = m.sb("fx", [FT, E])
        fhT = m.sb("fhT", [FS, T])
        stats = m.sb("stats", [FT, 6])
        mv = m.sb("mv", [FT, 2])
        veps = m.sb("veps", [FT])
        rstd = m.sb("rstd", [FT])
        xn = m.sb("xn", [FT, E])
        xnT = m.sb("xnT", [FS * T])
        gl = m.sb("gl", [len(FC), FS * T])
        hh = m.sb("hh", [len(FC), FS * T])
        yb = m.sb("yb", [FT, E])

        qk_ps = [m.ps(f"qk_ps{i}", [512]) for i in range(2)]
        tr_ps = [m.ps(f"tr_ps{i}", [4, P]) for i in range(2)]
        s_ps = [m.ps(f"s_ps{i}", [512]) for i in range(2)]
        o_ps = [m.ps(f"o_ps{i}", [512]) for i in range(2)]

        (xs_made, hT_made, qk_made, raw_made, sq_made, ss_made, rn_made, t1_made, t2_made, added, r_made, qkT_made, qkT_kept,
         pT_made, pT_kept,
         v_made, v_kept, v_moved0, v_moved1, s_made, p_shifted, p_exp, inv_made, o_made, o_scaled, oT_made, oT_kept, y_made, x_made,
         xT_made, xT_kept, q_step, p_step), sig2 = m.signals(
            xs_made=1, hT_made=1, qk_made=8, raw_made=8, sq_made=8, ss_made=8, rn_made=8, t1_made=8,
            t2_made=8, added=8, r_made=8,
            qkT_made=8, qkT_kept=8, pT_made=4, pT_kept=4, v_made=4, v_kept=4, v_moved0=16 * 2, v_moved1=16 * 2, s_made=4, p_shifted=4, p_exp=4, inv_made=4,
            o_made=2, o_scaled=4, oT_made=4, oT_kept=4, y_made=1, x_made=1, xT_made=1, xT_kept=1,
            q_step=PROJ, p_step=4 * OCTS)
        NF = len(FC)
        (fx_made, fT_made, fT_kept, fh_made, fvar_made, frstd_made, fxn_made, fnT_made, fnT_kept,
         f1_made, fgelu_made, fhh_made, fy_made, fx_done, fdve_step, fy_step), sig3 = m.signals(
            fx_made=1, fT_made=1, fT_kept=2, fh_made=1, fvar_made=1, frstd_made=1, fxn_made=FT, fnT_made=1,
            fnT_kept=1, f1_made=NF, fgelu_made=NF, fhh_made=NF, fy_made=1, fx_done=1,
            fdve_step=2 * FT, fy_step=1)

        SLOTS = [
            [("xs", 0, 0), ("pT", 0, 1), ("xT", 0, 0), ("out", 0, 2), ("proj", 0, 0), ("pv", 0, 1)],
            [("proj", 1, 0), ("pv", 1, 1)],
            [("proj", 2, 0), ("scale", 0, 1), ("scores", 2, 1)],
            [("proj", 3, 0), ("oT", 0, 1), ("scores", 3, 1)],
            [("proj", 4, 0), ("shift", 1, 1), ("v", 0, 0)],
            [("proj", 5, 0), ("sum", 1, 1), ("v", 1, 0)],
            [("proj", 6, 0), ("pT", 1, 1), ("scores", 0, 0)],
            [("proj", 7, 0), ("scores", 1, 0), ("pv", 2, 1)],
            [("pv", 3, 1), ("shift", 0, 0)],
            [("scale", 1, 1), ("sum", 0, 0), ("v", 2, 0), ("v", 3, 0), ("oT", 1, 1)]]
        BODY = []
        for i, slot in enumerate(SLOTS):
            BODY += slot
            if i < PROJ:
                BODY += [("rope", i, 0), ("norm", i, 0)]
            if 1 <= i <= PROJ:
                BODY += [("add", i - 1, 0)]
            if i >= 2:
                BODY += [("qkT", i - 2, 0)]
        FIRST = [s for s in BODY if s[2] == 0]
        SECOND = [s for s in BODY if s[2] < 2]
        LAST = [s for s in BODY if s[2] > 0] + [("out", 0, 1)]

        def v_part(n):
            c = n // 2
            return n % 2, c, (o_ps, qk_ps)[c][n % 2]

        def over_sequences(eng, l, steps):
            steps(FIRST, l * B, 0)
            steps(SECOND, l * B + 1, 1)
            with eng.Fori(2, B) as b:
                steps(BODY, l * B + b, b)
            steps(LAST, (l + 1) * B, B)

        F_BODY = [("in", 0, 0), ("up", 0, 1), ("in", 1, 0), ("up", 1, 1), ("in", 2, 0), ("up", 2, 1), ("in", 3, 0), ("down", 0, 1)]
        F_FIRST = [s for s in F_BODY if s[2] == 0]
        F_LAST = [s for s in F_BODY if s[2] == 1]

        def over_groups(eng, l, steps):
            steps(F_FIRST, l * (B // FS), 0)
            with eng.Fori(1, B // FS) as b:
                steps(F_BODY, l * (B // FS) + b, b)
            steps(F_LAST, (l + 1) * (B // FS), B // FS)

        def head_groups(ap):
            return ap.rearrange("p (g d) -> p g d", d=D)

        def swap_halves(out, x, table, t):
            for half in range(2):
                o = out.rearrange("p (c g z d) -> p c g z d", c=2, g=4, z=2)[:, :, :, half, :]
                i = x.rearrange("p (c g z d) -> p c g z d", c=2, g=4, z=2)[:, :, :, 1 - half, :]
                s = table[:, t, :, :].rearrange("p c (z d) -> p c z d", z=2)[:, :, half, :]
                yield o, i, bc(s, 2, 4)

        block = m.block()

        @block.sync
        def _(sp):
            for signal in sig1 + sig2 + sig3:
                sp.sem_inc(signal.sem, signal.start)
            sp.dma_start(X0[:], X[:]).then_inc(consts, 16)
            for dst, src in ((ident, "ident"), (identb, "identb"), (mask, "win_mask"), (cos0, "cos0"), (sin0, "sin0")):
                sp.dma_start(dst[:], a[src]).then_inc(consts, 16)

            v_moved = v_moved0, v_moved1

            def move_v(order, turn, b):
                for step, n, age in order:
                    if step == "v" and n % 2:
                        c = slice(n // 2 * 512, n // 2 * 512 + 512)
                        sp.wait_ge(*v_kept(turn, n + 1))
                        sp.dma_start(V[W:P, 1, :, c], V[0:P - W, 0, :, c]).then_inc(v_moved[n // 2].sem, 16)
                        sp.dma_start(V[0:W, 1, 1, c], V[P - W:P, 0, 0, c]).then_inc(v_moved[n // 2].sem, 16)

            with sp.Fori(0, DEPTH) as l:
                one = lambda ap: ap[bass.ds(l, 1)].rearrange("o p n -> (o p) n")
                row = lambda ap: ap[bass.ds(l, 1), :].rearrange("o n -> (o n)")
                sp.wait_ge(*y_made(l * B, 0))
                up = attn_weights.sem
                wsrc = one(a["wqkv"])
                for c in range(2):
                    sp.dma_start(wqk[:, :, c, :], wsrc[:, c * INNER:(c + 1) * INNER].rearrange("p (q n) -> p q n", q=QUADS)).then_inc(up, 16)
                sp.dma_start(qks[:].rearrange("p c d -> p (c d)"), row(a["qk_scale"]).partition_broadcast(P)).then_inc(up, 16)
                sp.dma_start(wv[:], wsrc[:, 2 * INNER:3 * INNER]).then_inc(up, 16)
                sp.dma_start(wo[:], one(a["wo"]).rearrange("(c p) n -> p c n", p=P)).then_inc(up, 16)
                sp.wait_ge(*fx_done(l * (B // FS), 0))
                up = ffn_weights.sem
                sp.dma_start(w1[:], one(a["w1"])).then_inc(up, 16)
                sp.dma_start(w2[:], one(a["w2"]).rearrange("(c p) n -> p c n", p=P)).then_inc(up, 16)
                sp.dma_start(b2[:], row(a["b2"]).partition_broadcast(P)).then_inc(up, 16)
                sp.dma_start(lng[:], one(a["ln_g"])).then_inc(up, 16)
                sp.dma_start(lnb[:], one(a["ln_b"])).then_inc(up, 16)
                sp.dma_start(b1[:].rearrange("p c k -> p (c k)"), one(a["b1"])).then_inc(up, 16)
                over_sequences(sp, l, move_v)

        @block.gpsimd
        def _(pool):
            pool.memset(KT[:, :, 0:W], 0.0).then_inc(consts, 1)
            pool.memset(hT[:, 0:W + 1], 0.0).then_inc(consts, 1)
            pool.memset(fhT[:, :, 0:1], 0.0).then_inc(consts, 1)
            pool.memset(V[0:W, 1, 0, :], 0.0).then_inc(consts, 1)

            def attend(order, turn, b):
                for step, n, age in order:
                    i = turn - age
                    if step == "norm":
                        pool.wait_ge(*ss_made(i, n + 1))
                        pool.tensor_tensor(rn[:, n, :], ss[:, n, :], neg_half[:], ALU.pow).then_inc(rn_made.sem, 1)
                    elif step == "rope":
                        pool.wait_ge(*raw_made(i, n + 1))
                        pool.wait_ge(*tables_made(layer[0], 1))
                        pool.wait_ge(*added(i, max(n - 1, 0)))
                        for o, x, s in swap_halves(t2[:, n % 2, :], raw[:, n % 2, :], sinq, n % 2):
                            last = pool.tensor_tensor(o, x, s, ALU.mult)
                        last.then_inc(t2_made.sem, 1)

            def feed(order, turn, b):
                for step, n, age in order:
                    if (step, n) == ("in", 2):
                        pool.wait_ge(*fvar_made(turn, 1))
                        pool.tensor_tensor(rstd[:], veps[:], neg_half[:, 0:FT], ALU.pow).then_inc(frstd_made.sem, 1)

            layer = [0]
            with pool.Fori(0, DEPTH) as l:
                layer[0] = l
                over_sequences(pool, l, attend)
                over_groups(pool, l, feed)

        @block.scalar
        def _(act):
            act.wait_ge(consts, CONSTS)
            layer = [0]

            def attend(order, turn, b):
                for step, n, age in order:
                    i = turn - age
                    if step == "xs":
                        act.wait_ge(*xT_made(i, 0))
                        nc.scalar.copy(xs[:], X[:, bass.ds(b * HALVES, HALVES), :]).then_inc(xs_made.sem, 1)
                    elif step == "xT":
                        act.wait_ge(*xT_made(i, 1))
                        act.wait_ge(*v_made(i, 0))
                        xv = tr_ps[0][:, 0:HALVES, :].rearrange("p t c -> p (t c)")
                        nc.scalar.copy(hT[0:64, W:W + T], xv[0:64, :]).then_inc(hT_made.sem, 1)
                        nc.scalar.copy(hT[64:128, W + 1:W + T], xv[64:128, 0:T - 1]).then_inc(xT_kept.sem, 1)
                    elif step == "proj":
                        act.wait_ge(*qk_made(i, n + 1))
                        act.wait_ge(*t1_made(i, max(n - 1, 0)))
                        act.wait_ge(*t2_made(i, max(n - 1, 0)))
                        nc.scalar.copy(raw[:, n % 2, :], qk_ps[n % 2][:]).then_inc(raw_made.sem, 1)
                        act.wait_ge(*ss_made(i, max(n - 1, 0)))
                        nc.scalar.activation(sq[:, n % 2, :], qk_ps[n % 2][:], ACT.Square).then_inc(sq_made.sem, 1)
                    elif step == "v":
                        act.wait_ge(*v_made(i, n + 1))
                        act.wait_ge(*o_made(i, -1 if n < 2 else 0))
                        t, c, bank = v_part(n)
                        nc.scalar.copy(V[:, 0, t, c * 512:(c + 1) * 512], bank[:]).then_inc(v_kept.sem, 1)
                    elif step == "qkT":
                        act.wait_ge(*qkT_made(i, n + 1))
                        act.wait_ge(*s_made(i, -2 if n < 4 else 0))
                        q, t = n // 2, n % 2
                        nc.scalar.copy(QT[:, 2 * q:2 * q + 2, t * P:(t + 1) * P], tr_ps[0][:, 0:2, :])
                        nc.scalar.copy(KT[:, 2 * q:2 * q + 2, W + t * P:W + (t + 1) * P], tr_ps[0][:, 2:4, :]) \
                            .then_inc(qkT_kept.sem, 1)
                    elif step == "shift":
                        for h in range(2):
                            act.wait_ge(*p_shifted(i, 2 * n + h + 1))
                            nc.scalar.activation(pr[:, n, h, :], pr[:, n, h, :], ACT.Exp).then_inc(p_exp.sem, 1)
                    elif step == "pT":
                        for h in range(2):
                            act.wait_ge(*pT_made(i, 2 * n + h + 1))
                            if h == 0:
                                act.wait_ge(*o_made(i, 0))
                            nc.scalar.copy(PT[:, n, h, :, :], tr_ps[1][:]).then_inc(pT_kept.sem, 1)
                    elif step == "oT":
                        for j in range(2):
                            act.wait_ge(*oT_made(i, 2 * n + j + 1))
                            act.wait_ge(*y_made(i, 0))
                            ov = OT[:, 4 * n:4 * n + 4, :].rearrange("p c (t j x) -> p c t j x", t=HALVES, j=2)
                            nc.scalar.copy(ov[:, :, :, j, :], tr_ps[1][:].rearrange("p c (t x) -> p c t x", t=HALVES)) \
                                .then_inc(oT_kept.sem, 1)

            def feed(order, turn, b):
                for step, n, age in order:
                    i = turn - age
                    if (step, n) == ("in", 0):
                        act.wait_ge(*x_made((layer[0] + 1) * B, 0))
                        act.wait_ge(*fT_made(i, 0))
                        nc.scalar.copy(fx[:], X[:, bass.ds(b * FT, FT), :]).then_inc(fx_made.sem, 1)
                        act.wait_ge(*fT_made(i, 1))
                        act.wait_ge(*fh_made(i, 0))
                        xv = tr_ps[0][:].rearrange("p (s t) c -> p s (t c)", s=FS)
                        nc.scalar.copy(fhT[0:64, :, :], xv[0:64]).then_inc(fT_kept.sem, 1)
                        nc.scalar.copy(fhT[64:128, :, 1:T], xv[64:128, :, 0:T - 1]).then_inc(fT_kept.sem, 1)
                    elif (step, n) == ("in", 3):
                        act.wait_ge(*fnT_made(i, 1))
                        act.wait_ge(*f1_made(i, 0))
                        act.wait_ge(*ffn_weights(layer[0], 96))
                        nc.scalar.activation(xnT[:], tr_ps[0][:].rearrange("p t c -> p (t c)"), ACT.Identity,
                                             bias=lnb[:, 0:1], scale=lng[:, 0:1]).then_inc(fnT_kept.sem, 1)
                    elif step == "up":
                        f, size = FC[n]
                        act.wait_ge(*f1_made(i, n + 1))
                        nc.scalar.activation(gl[0:size, n, :], qk_ps[n % 2][0:size, :], ACT.Gelu,
                                             bias=b1[0:size, 1, n:n + 1]).then_inc(fgelu_made.sem, 1)

            with act.Fori(0, DEPTH) as l:
                layer[0] = l
                act.wait_ge(*fx_done(l * (B // FS), 0))
                over_sequences(act, l, attend)
                over_groups(act, l, feed)

        @block.tensor
        def _(pe):
            pe.wait_ge(consts, CONSTS)
            mm, flip = nc.tensor.matmul, nc.tensor.transpose
            layer = [0]

            def attend(order, turn, b):
                for step, n, age in order:
                    i = turn - age
                    if step == "xT":
                        pe.wait_ge(*attn_weights(layer[0], 80))
                        pe.wait_ge(*qkT_kept(i, 0))
                        pe.wait_ge(*xs_made(i, 1))
                        for t in range(HALVES):
                            last = flip(tr_ps[0][:, t, :], xs[:, t, :], ident[:])
                        last.then_inc(xT_made.sem, 1)
                        pe.wait_ge(*hT_made(i, 1))
                        pe.wait_ge(*xT_kept(i, 1))
                    elif step == "proj":
                        pe.wait_ge(*sq_made(i, max(n - 1, 0)))
                        if n < 2:
                            pe.wait_ge(*v_kept(i, n - 1))
                        t = n % 2
                        mm(qk_ps[n % 2][:], hT[:, W + t * P:W + (t + 1) * P],
                           wqk[:, n // 2, :, :].rearrange("p c n -> p (c n)"), start=True, stop=True).then_inc(qk_made.sem, 1)
                    elif step == "v":
                        t, c, bank = v_part(n)
                        pe.wait_ge(*(o_scaled(i, n - 3) if n < 2 else sq_made(i, n + 5)))
                        mm(bank[:], hT[:, W + t * P:W + (t + 1) * P], wv[:, c * 512:(c + 1) * 512], start=True, stop=True) \
                            .then_inc(v_made.sem, 1)
                    elif step == "qkT":
                        pe.wait_ge(*r_made(i, n + 1))
                        pe.wait_ge(*qkT_kept(i, n))
                        for c in range(4):
                            last = flip(tr_ps[0][:, c, :], qn[:, n % 2, c * P:(c + 1) * P], ident[:])
                        last.then_inc(qkT_made.sem, 1)
                    elif step == "scores":
                        o, part = n // 2, n % 2
                        if part == 0:
                            pe.wait_ge(*qkT_kept(i, 4 * o + 4))
                            pe.wait_ge(*p_shifted(i, 2 * o))
                            for h in range(2):
                                mm(s_ps[h][:], identb[:], mask[:].rearrange("p c j k -> p (c j k)"),
                                   start=True, stop=False, skip_group_check=True)
                        for c in range(2 * part, 2 * part + 2):
                            for j in range(2):
                                for ts in range(4):
                                    for h in range(2):
                                        w = 4 * (ts // 2) + 2 * j + ts % 2
                                        r = slice(64 * h, 64 * h + 64)
                                        last = mm(s_ps[h][32 * ts:32 * ts + 32, c * P + 64 * j:c * P + 64 * j + 64],
                                                  QT[r, 4 * o + c, W * w:W * w + W], KT[r, 4 * o + c, W * w:W * w + 2 * W],
                                                  start=False, stop=(c == 3 and j == 1), skip_group_check=True,
                                                  tile_position=(64 * h, 32 * ts))
                                        if c == 3 and j == 1 and ts == 3:
                                            last.then_inc(s_made.sem, 1)
                    elif step == "pT":
                        for h in range(2):
                            pe.wait_ge(*p_exp(i, 2 * n + h + 1))
                            pe.wait_ge(*(pT_kept(i, 2 * n + 1) if h else oT_kept(i, 2 * n)))
                            for c in range(4):
                                last = flip(tr_ps[1][:, c, :], pr[:, n, h, c * P:(c + 1) * P], ident[:])
                            last.then_inc(pT_made.sem, 1)
                    elif step == "pv":
                        o, part = n // 2, n % 2
                        if part == 0:
                            pe.wait_ge(*pT_kept(i, 2 * o + 2))
                            pe.wait_ge(*(v_moved0, v_moved1)[o](i, 32))
                            pe.wait_ge(*(x_made(i, 0) if o == 0 else o_scaled(i, 2) if order is LAST else v_kept(i + 1, 2)))
                            mm(o_ps[0][:, 0:1], identb[:], identb[:, 0:1], start=True, stop=True)
                        for c in range(2 * part, 2 * part + 2):
                            for h in range(2):
                                for ts in range(4):
                                    for j in range(2):
                                        r = slice(64 * j, 64 * j + 64)
                                        g = (4 * o + c) * P + 64 * h
                                        last = mm(o_ps[j][32 * ts:32 * ts + 32, c * P + 64 * h:c * P + 64 * h + 64],
                                                  PT[r, o, h, c, 32 * ts:32 * ts + 32], V[r, 1 - ts % 2, ts // 2, g:g + 64],
                                                  start=True, stop=True, tile_position=(64 * j, 32 * ts))
                        if part:
                            last.then_inc(o_made.sem, 1)
                    elif step == "oT":
                        for j in range(2):
                            pe.wait_ge(*o_scaled(i, 2 * n + j + 1))
                            pe.wait_ge(*(oT_kept(i, 2 * n + 1) if j else pT_kept(i, 2 * n + 2)))
                            for c in range(4):
                                last = flip(tr_ps[1][:, c, :], O[:, j, c * P:(c + 1) * P], ident[:])
                            last.then_inc(oT_made.sem, 1)
                    elif step == "out":
                        pe.wait_ge(*oT_kept(i, 4))
                        for t in range(HALVES):
                            for c in range(PAIRS):
                                last = mm(o_ps[0][:, t * P:(t + 1) * P], OT[:, c, t * P:(t + 1) * P], wo[:, c, :],
                                          start=(c == 0), stop=(c == PAIRS - 1))
                        last.then_inc(y_made.sem, 1)

            def feed(order, turn, b):
                for step, n, age in order:
                    i = turn - age
                    if (step, n) == ("in", 0):
                        pe.wait_ge(*x_made((layer[0] + 1) * B, 0))
                        pe.wait_ge(*fx_made(i, 1))
                        pe.wait_ge(*fnT_kept(i, 0))
                        for t in range(FT):
                            last = flip(tr_ps[0][:, t, :], fx[:, t, :], ident[:])
                        last.then_inc(fT_made.sem, 1)
                    elif (step, n) == ("in", 1):
                        pe.wait_ge(*fT_kept(i, 2))
                        pe.wait_ge(*fxn_made(i, 0))
                        for t in range(FT):
                            last = flip(tr_ps[1][:, t, :], fhT[:, t // 2, (t % 2) * P:(t % 2) * P + P], ident[:])
                        last.then_inc(fh_made.sem, 1)
                    elif (step, n) == ("in", 3):
                        pe.wait_ge(*fxn_made(i, FT))
                        for t in range(FT):
                            last = flip(tr_ps[0][:, t, :], xn[:, t, :], ident[:])
                        last.then_inc(fnT_made.sem, 1)
                    elif step == "up":
                        f, size = FC[n]
                        if n == 0:
                            pe.wait_ge(*ffn_weights(layer[0], 96))
                            pe.wait_ge(*fnT_kept(i, 1))
                        pe.wait_ge(*fhh_made(i, max(n - 1, 0)))
                        mm(qk_ps[n % 2][0:size, :], w1[:, F + f:F + f + size], xnT[:], start=True, stop=True)
                        mm(s_ps[n % 2][0:size, :], w1[:, f:f + size], xnT[:], start=True, stop=True).then_inc(f1_made.sem, 1)
                    elif step == "down":
                        pe.wait_ge(*fx_done(i, 0))
                        pe.wait_ge(*fhh_made(i, NF))
                        for t in range(FT):
                            for c, (f, size) in enumerate(FC):
                                last = mm(o_ps[0][:, t * P:(t + 1) * P], hh[0:size, c, t * P:(t + 1) * P], w2[0:size, c, :],
                                          start=(c == 0), stop=(c == NF - 1))
                        last.then_inc(fy_made.sem, 1)

            with pe.Fori(0, DEPTH) as l:
                layer[0] = l
                over_sequences(pe, l, attend)
                over_groups(pe, l, feed)

        @block.vector
        def _(dve):
            tt, ts_, red = nc.vector.tensor_tensor, nc.vector.tensor_scalar, nc.vector.tensor_reduce
            dve.wait_ge(consts, CONSTS)
            layer = [0]

            def attend(order, turn, b):
                for step, n, age in order:
                    i = turn - age
                    if step == "norm":
                        dve.wait_ge(*sq_made(i, n + 1))
                        red(ss[:, n, :], head_groups(sq[:, n % 2, :]), op=ALU.add, axis=X_AXIS).then_inc(q_step.sem, 1)
                        dve.wait_ge(*q_step(i, n + 1))
                        ts_(ss[:, n, :], ss[:, n, :], 1e-24, None, ALU.max).then_inc(ss_made.sem, 1)
                    elif step == "rope":
                        dve.wait_ge(*raw_made(i, n + 1))
                        dve.wait_ge(*r_made(i, max(n - 1, 0)))
                        v = lambda ap: ap.rearrange("p (c g d) -> p c g d", c=2, g=4)
                        tt(v(t1[:, n % 2, :]), v(raw[:, n % 2, :]), bc(cosq[:, n % 2], 2, 4), ALU.mult).then_inc(t1_made.sem, 1)
                    elif step == "add":
                        dve.wait_ge(*t1_made(i, n + 1))
                        dve.wait_ge(*t2_made(i, n + 1))
                        tt(t1[:, n % 2, :], t1[:, n % 2, :], t2[:, n % 2, :], ALU.add).then_inc(added.sem, 1)
                        dve.wait_ge(*added(i, n + 1))
                        dve.wait_ge(*rn_made(i, n + 1))
                        dve.wait_ge(*qkT_made(i, max(n - 1, 0)))
                        tt(head_groups(qn[:, n % 2, :]), head_groups(t1[:, n % 2, :]), bc(rn[:, n, :], 2, D), ALU.mult) \
                            .then_inc(r_made.sem, 1)
                    elif step == "shift":
                        for h in range(2):
                            dve.wait_ge(*s_made(i, 2 * n + h + 1))
                            v = lambda ap: ap.rearrange("p (g k) -> p g k", k=2 * W)
                            red(top[:, n, h, :], v(s_ps[h][:]), op=ALU.max, axis=X_AXIS).then_inc(p_step.sem, 1)
                            dve.wait_ge(*p_step(i, 4 * n + h + 1))
                            tt(v(pr[:, n, h, :]), v(s_ps[h][:]), bc(top[:, n, h, :], 2, 2 * W), ALU.subtract) \
                                .then_inc(p_shifted.sem, 1)
                    elif step == "sum":
                        for h in range(2):
                            dve.wait_ge(*p_exp(i, 2 * n + h + 1))
                            red(den[:, n, h, :], pr[:, n, h, :].rearrange("p (g k) -> p g k", k=2 * W), op=ALU.add, axis=X_AXIS) \
                                .then_inc(p_step.sem, 1)
                            dve.wait_ge(*p_step(i, 4 * n + h + 3))
                            nc.vector.reciprocal(inv[:, n, h, :], den[:, n, h, :]).then_inc(inv_made.sem, 1)
                    elif step == "out":
                        dve.wait_ge(*y_made(i, 1))
                        xv = X[:, bass.ds((b - age) * HALVES, HALVES), :].rearrange("p t e -> p (t e)")
                        tt(xv, xv, o_ps[0][:, 0:HALVES * E], ALU.add).then_inc(x_made.sem, 1)
                    elif step == "scale":
                        dve.wait_ge(*inv_made(i, 2 * n + 2))
                        dve.wait_ge(*o_made(i, n + 1))
                        for j in range(2):
                            dve.wait_ge(*oT_made(i, 2 * n + j - 1))
                            v = lambda ap: ap.rearrange("p (c h d) -> p c h d", c=4, h=2)
                            s = inv[:, n].rearrange("p h (c j) -> p c h j", j=2)[:, :, :, j]
                            tt(v(O[:, j, :]), v(o_ps[j][:]), bc(s, 3, D), ALU.mult).then_inc(o_scaled.sem, 1)

            def feed(order, turn, b):
                for step, n, age in order:
                    i = turn - age
                    if (step, n) == ("in", 2):
                        dve.wait_ge(*fh_made(i, 1))
                        for t in range(FT):
                            nc.vector.bn_stats(stats[:, t, :], tr_ps[1][:, t, :]).then_inc(fdve_step.sem, 1)
                        dve.wait_ge(*fdve_step(i, FT))
                        hold(nc.vector, scrap)
                        for t in range(FT):
                            nc.vector.bn_aggr(mv[:, t, :], stats[:, t, :]).then_inc(fdve_step.sem, 1)
                        dve.wait_ge(*fdve_step(i, 2 * FT))
                        ts_(veps[:], mv[:, :, 1], LN_EPS, None, ALU.add).then_inc(fvar_made.sem, 1)
                    elif (step, n) == ("in", 3):
                        dve.wait_ge(*frstd_made(i, 1))
                        dve.wait_ge(*fnT_made(i, 0))
                        for t in range(FT):
                            ts_(xn[:, t, :], tr_ps[1][:, t, :], mv[:, t, 0:1], rstd[:, t:t + 1], ALU.subtract, ALU.mult) \
                                .then_inc(fxn_made.sem, 1)
                    elif step == "up":
                        f, size = FC[n]
                        dve.wait_ge(*fgelu_made(i, n + 1))
                        nc.vector.scalar_tensor_tensor(hh[0:size, n, :], s_ps[n % 2][0:size, :], b1[0:size, 0, n:n + 1], gl[0:size, n, :],
                                                       ALU.add, ALU.mult).then_inc(fhh_made.sem, 1)
                    elif step == "down":
                        dve.wait_ge(*fy_made(i, 1))
                        tt(yb[:], o_ps[0][:].rearrange("p (t e) -> p t e", e=E), bc(b2[:], 1, FT), ALU.add).then_inc(fy_step.sem, 1)
                        dve.wait_ge(*fy_step(i, 1))
                        xv = X[:, bass.ds((b - age) * FT, FT), :]
                        tt(xv, xv, yb[:], ALU.add).then_inc(fx_done.sem, 1)

            with dve.Fori(0, DEPTH) as l:
                layer[0] = l
                dve.wait_ge(*attn_weights(l, 80))
                dve.wait_ge(*t2_made(l * B, 0))
                for t in range(HALVES):
                    tt(cosq[:, t], cos0[:, t], qks[:], ALU.mult)
                    for half in range(2):
                        v = lambda ap: ap.rearrange("p c (z d) -> p c z d", z=2)
                        last = tt(v(sinq[:, t])[:, :, half, :], v(sin0[:, t])[:, :, half, :], v(qks[:])[:, :, 1 - half, :], ALU.mult)
                last.then_inc(tables_made.sem, 1)
                dve.wait_ge(*tables_made(l, 1))
                over_sequences(dve, l, attend)
                over_groups(dve, l, feed)


def add_norm(nc, X0, X, neg_half, stage):
    N = 8
    with Core(nc, stage) as m:
        h = m.sb("h", [N, E])
        scrap = m.sb("scrap", [1])
        stats, mv = m.sb("stats", [N, 6]), m.sb("mv", [N, 2])
        veps, rstd = m.sb("veps", [N]), m.sb("rstd", [N])
        STEPS = 2 * N + 3
        (var_made, rstd_made, step_done), signals = m.signals(var_made=1, rstd_made=1, step_done=STEPS)
        block = m.block()

        @block.sync
        def _(sp):
            for signal in signals:
                sp.sem_inc(signal.sem, signal.start)

        @block.gpsimd
        def _(pool):
            with pool.Fori(0, TILES // N) as c:
                pool.wait_ge(*var_made(c, 1))
                pool.tensor_tensor(rstd[:], veps[:], neg_half[:], ALU.pow).then_inc(rstd_made.sem, 1)

        @block.vector
        def _(dve):
            with dve.Fori(0, TILES // N) as c:
                link = Chain(dve, step_done, c)
                link(nc.vector.tensor_tensor(h[:], X0[:, bass.ds(c * N, N), :], X[:, bass.ds(c * N, N), :], ALU.add))
                layer_norm(nc, dve, link, h, stats, mv, veps, rstd, scrap, N, var_made, rstd_made, c)
                link(nc.vector.tensor_tensor(X[:, bass.ds(c * N, N), :], h[:], bc(rstd[:], 2, E), ALU.mult))
                assert link.n == STEPS, link.n


def small_heads(nc, X, X0, neg_half, a, causal):
    H, D, HP = 16, 8, 32
    KV = 4 if causal else H
    G = H // 4
    PAIRS = H // 2
    QKV = (H + 2 * KV) * D
    QK = H + KV
    SCALE = 1.0 / float(D) ** 0.5
    with Core(nc, "causal" if causal else "rotary") as m:
        ident, identb = m.sb("ident", [P]), m.sb("identb", [P], BF16)
        w = m.sb("w", [QKV])
        w_out = m.sb("w_out", [E])
        aff = m.sb("aff", [4])
        cos, sin = m.sb("cos", [HALVES, D]), m.sb("sin", [HALVES, D])
        scrap = m.sb("scrap", [1])
        if causal:
            mask = m.sb("mask", [HALVES, T], BF16)
            maskT = m.sb("maskT", [HALVES, T], BF16)
            dmas = [(mask, "causal"), (maskT, "causal_t")]
            rows = []
        else:
            bias = m.sb("bias", [QKV])
            b_out = m.sb("b_out", [E])
            w_rad = m.sb("w_rad", [E])
            b_rad = m.sb("b_rad", [1])
            w_ln, b_ln = m.sb("w_ln", [D]), m.sb("b_ln", [D])
            dmas = []
            rows = [(bias, "rot_bias"), (b_out, "rot_b_out"), (w_rad, "rot_w_rad"), (b_rad, "rot_b_rad"),
                    (w_ln, "rot_w_ln"), (b_ln, "rot_b_ln")]
        pre = "cau" if causal else "rot"
        dmas += [(ident, "ident"), (identb, "identb"), (w, f"{pre}_w"), (w_out, f"{pre}_w_out"), (aff, f"{pre}_aff"),
                 (cos, f"{pre}_cos"), (sin, f"{pre}_sin")]
        xh = m.sb("xh", [HALVES, E])
        sqx = m.sb("sqx", [HALVES, E])
        stats, mv = m.sb("stats", [HALVES, 6]), m.sb("mv", [HALVES, 2])
        veps, rstd = m.sb("veps", [HALVES]), m.sb("rstd", [HALVES])
        stats2, mv2 = m.sb("stats2", [HALVES, 6]), m.sb("mv2", [HALVES, 2])
        veps2, rstd2 = m.sb("veps2", [HALVES]), m.sb("rstd2", [HALVES])
        xqT, xkT = m.sb("xqT", [T]), m.sb("xkT", [T])
        rad = m.sb("rad", [HALVES])
        qkv = m.sb("qkv", [HALVES, QKV])
        t1, t2 = m.sb("t1", [HALVES, QK * D]), m.sb("t2", [HALVES, QK * D])
        mean = m.sb("mean", [HALVES, QK])
        hvar = m.sb("hvar", [HALVES, QK])
        hstd = m.sb("hstd", [HALVES, QK])
        QK_pad = m.sb("QK_pad", [HALVES, 2, H, HP])
        V_pad = m.sb("V_pad", [HALVES, KV, HP])
        v_rest = m.sb("v_rest", [HALVES, KV // 2 * D])
        QT, QmT = m.sb("QT", [G, T]), m.sb("QmT", [G, T])
        KT = m.sb("KT", [H, T])
        top = m.sb("top", [H, HALVES])
        PT = m.sb("PT", [2, 2, HALVES, T])
        OT = m.sb("OT", [G, T])
        rec = m.sb("rec", [HALVES, H])
        att = m.sb("att", [HALVES, E])
        attT = m.sb("attT", [T])
        y = m.sb("y", [HALVES, E])

        s1_ps = [m.ps(f"s1_ps{i}", [HALVES, T]) for i in range(2)]
        s2_ps = [m.ps(f"s2_ps{i}", [HALVES, T]) for i in range(2)]
        o_ps = [m.ps(f"o_ps{i}", [512]) for i in range(2)]
        head_ps = m.ps("head_ps", [4, P])
        token_ps = m.ps("token_ps", [4, P])

        PREP_STEPS, TAIL_STEPS = (8, 3) if causal else (27, 9)
        consts = m.sem("consts")
        CONSTS = 16 * (len(dmas) + len(rows) + causal) + 7
        (var_made, rstd_made, xh_made, xT_made, xT_kept, qkv_made, qkv_kept,
         padded, v_padded, v_saved, qk_made, qk_kept, s1_made, top_made, negm_made, qm_made, qm_kept, s2_made, p_made,
         o_made, o_kept, ot_made, att_made, attf_made, attT_kept, y_made, y_read,
         prep_step, tail_step), signals = m.signals(
            var_made=1, rstd_made=1, xh_made=1, xT_made=1, xT_kept=1, qkv_made=2, qkv_kept=2,
            padded=G, v_padded=2, v_saved=1, qk_made=G, qk_kept=G, s1_made=H, top_made=H, negm_made=G, qm_made=G, qm_kept=G,
            s2_made=H, p_made=H, o_made=PAIRS, o_kept=G, ot_made=2, att_made=2, attf_made=1, attT_kept=1, y_made=1, y_read=1,
            prep_step=PREP_STEPS, tail_step=TAIL_STEPS)
        if not causal:
            (hvar_made, hstd_made, var2_made, rstd2_made), more = m.signals(hvar_made=1, hstd_made=1, var2_made=1, rstd2_made=1)
            signals = signals + more

        SLOTS = 8
        AT = [(0, 5, "x", 0), (1, 5, "xT", 0), (2, 1, "qkv", 0), (3, 1, "qkv", 1), (4, 6, "rope", 0), (5, 6, "root", 0),
              (6, 6, "last", 0), (8, 7, "v", 0), (12, 0, "v", 1),
              (20, 1, "o", 0), (21, 1, "o", 1), (22, 1, "att", 0), (23, 5, "y", 0)]
        for p in range(PAIRS):
            AT += [(8 + p, 0, "s1", p), (11 + p, 2, "s2", p), (12 + p, 4, "pv", p)]
        for g in range(G):
            AT += [(7 + g, 0 if g == 0 else 5, "pad", g), (7 + 2 * g, 1, "qk", g), (10 + 2 * g, 1, "qm", g)]
        AT.sort(key=lambda s: (s[0] % SLOTS, s[1], -s[0]))
        BODY = [(name, n, slot // SLOTS) for slot, _, name, n in AT]
        aged = lambda *ages: [s for s in BODY if s[2] in ages]

        def over_sequences(eng, steps):
            steps(aged(0), 0, (0,))
            steps(aged(0, 1), 1, (0, 1))
            with eng.Fori(2, B) as b:
                steps(BODY, b, (0, 1, 2))
            steps(aged(1, 2), B, (1, 2))
            steps(aged(2), B + 1, (2,))

        block = m.block()

        @block.sync
        def _(sp):
            for signal in signals:
                sp.sem_inc(signal.sem, signal.start)
            if causal:
                sp.dma_start(X0[:], X[:]).then_inc(consts, 16)
            for dst, name in dmas:
                sp.dma_start(dst[:], a[name]).then_inc(consts, 16)
            for dst, name in rows:
                sp.dma_start(dst[:], a[name].partition_broadcast(P)).then_inc(consts, 16)

        @block.gpsimd
        def _(pool):
            pool.memset(KT[:], 0.0).then_inc(consts, 1)
            pool.memset(QK_pad[:, :, 0, :, :], 0.0).then_inc(consts, 1)
            for lo, hi, value in ((0, D, 0.0), (D, D + 1, 1.0), (D + 1, HP, 0.0)):
                pool.memset(QK_pad[:, :, 1, :, lo:hi], value).then_inc(consts, 1)
            for lo, hi, value in ((D, D + 1, 1.0), (D + 1, HP, 0.0)):
                pool.memset(V_pad[:, :, :, lo:hi], value).then_inc(consts, 1)

            def steps(order, turn, ages):
                for step, n, age in order:
                    i = turn - age
                    if step == "x":
                        pool.wait_ge(*var_made(i, 1))
                        pool.tensor_tensor(rstd[:], veps[:], neg_half[:, 0:HALVES], ALU.pow).then_inc(rstd_made.sem, 1)
                    elif step == "y" and not causal:
                        pool.wait_ge(*var2_made(i, 1))
                        pool.tensor_tensor(rstd2[:], veps2[:], neg_half[:, 0:HALVES], ALU.pow).then_inc(rstd2_made.sem, 1)

            over_sequences(pool, steps)

        @block.scalar
        def _(act):
            act.wait_ge(consts, CONSTS)

            def steps(order, turn, ages):
                for step, n, age in order:
                    i = turn - age
                    if step == "xT":
                        act.wait_ge(*xT_made(i, 1))
                        act.wait_ge(*qkv_made(i, 0))
                        xT = token_ps[:, 0:HALVES, :].rearrange("p t c -> p (t c)")
                        nc.scalar.activation(xqT[:], xT, ACT.Identity, bias=aff[:, 1:2], scale=aff[:, 0:1])
                        nc.scalar.activation(xkT[:], xT, ACT.Identity, bias=aff[:, 3:4], scale=aff[:, 2:3]) \
                            .then_inc(xT_kept.sem, 1)
                    elif step == "root" and not causal:
                        act.wait_ge(*hvar_made(i, 1))
                        nc.scalar.activation(hstd[:], hvar[:], ACT.Sqrt).then_inc(hstd_made.sem, 1)
                    elif step == "qk":
                        act.wait_ge(*qk_made(i, n + 1))
                        act.wait_ge(*s1_made(i - 1, 4 * n + 4))
                        nc.scalar.copy(QT[:, n, :], head_ps[:, 0:2, :].rearrange("p t c -> p (t c)"))
                        act.wait_ge(*s2_made(i - 1, 4 * n + 4))
                        for r in range(4):
                            own = slice(HP * r, HP * r + HP)
                            last = nc.scalar.copy(KT[own, 4 * n + r, :], head_ps[own, 2:4, :].rearrange("p t c -> p (t c)"))
                        last.then_inc(qk_kept.sem, 1)
                    elif step == "qm":
                        act.wait_ge(*qm_made(i, n + 1))
                        act.wait_ge(*s2_made(i - 1, 4 * n + 4))
                        nc.scalar.copy(QmT[:, n, :], head_ps[:, 0:2, :].rearrange("p t c -> p (t c)")).then_inc(qm_kept.sem, 1)
                    elif step == "s2":
                        for e in range(2):
                            act.wait_ge(*s2_made(i, 2 * n + e + 1))
                            if e == 0:
                                act.wait_ge(*o_made(i, n - 1))
                            if causal:
                                nc.scalar.activation(PT[:, n % 2, e, 0, :], s2_ps[e][:, 0, :], ACT.Exp, scale=SCALE)
                                nc.scalar.activation(PT[:, n % 2, e, 1, P:T], s2_ps[e][:, 1, P:T], ACT.Exp, scale=SCALE) \
                                    .then_inc(p_made.sem, 1)
                            else:
                                nc.scalar.activation(PT[:, n % 2, e], s2_ps[e][:], ACT.Exp, scale=SCALE).then_inc(p_made.sem, 1)
                    elif step == "pv" and n % 2:
                        g = n // 2
                        act.wait_ge(*o_made(i, n + 1))
                        act.wait_ge(*ot_made(i, 0))
                        nc.scalar.copy(OT[:, g, :], o_ps[g % 2][:, 0:T]).then_inc(o_kept.sem, 1)
                    elif step == "att":
                        act.wait_ge(*attf_made(i, 1))
                        act.wait_ge(*y_made(i, 0))
                        nc.scalar.copy(attT[:], token_ps[:, 0:HALVES, :].rearrange("p t c -> p (t c)")).then_inc(attT_kept.sem, 1)

            over_sequences(act, steps)

        @block.tensor
        def _(pe):
            mm, flip = nc.tensor.matmul, nc.tensor.transpose
            pe.wait_ge(consts, CONSTS)

            def steps(order, turn, ages):
                for step, n, age in order:
                    i = turn - age
                    if step == "xT":
                        pe.wait_ge(*xh_made(i, 1))
                        pe.wait_ge(*y_read(i - 3, 1))
                        for t in range(HALVES):
                            last = flip(token_ps[:, t, :], xh[:, t, :], ident[:])
                        last.then_inc(xT_made.sem, 1)
                    elif step == "qkv":
                        pe.wait_ge(*(qkv_kept(i, 1) if n else xT_kept(i, 1)))
                        flat = token_ps[:].rearrange("p a c -> p (a c)")
                        mm(flat[:, 0:E], xqT[:, n * P:(n + 1) * P], w[:, 0:E], start=True, stop=True)
                        mm(flat[:, E:QKV], xkT[:, n * P:(n + 1) * P], w[:, E:QKV], start=True, stop=True).then_inc(qkv_made.sem, 1)
                    elif step == "qk":
                        pe.wait_ge(*padded(i, n + 1))
                        pe.wait_ge(*qm_kept(i, n - 1))
                        for c in range(4):
                            last = flip(head_ps[:, c, :], QK_pad[:, c % 2, c // 2, 4 * n:4 * n + 4, :].rearrange("p h d -> p (h d)"), ident[:])
                        last.then_inc(qk_made.sem, 1)
                    elif step == "s1":
                        g = n // 2
                        pe.wait_ge(*qk_kept(i, g + 1))
                        pe.wait_ge(*top_made(i, 2 * n))
                        for t in range(HALVES):
                            keys = P * (t + 1) if causal else T
                            for e in range(2):
                                last = mm(s1_ps[e][:, t, 0:keys], QT[:, g, t * P:(t + 1) * P], KT[:, 2 * n + e, 0:keys],
                                          start=True, stop=not causal, skip_group_check=True)
                                if causal:
                                    own = slice(t * P, (t + 1) * P)
                                    last = mm(s1_ps[e][:, t, own], identb[:], mask[:, t, own], start=False, stop=True,
                                              skip_group_check=True)
                                if t == HALVES - 1:
                                    last.then_inc(s1_made.sem, 1)
                    elif step == "qm":
                        pe.wait_ge(*negm_made(i, n + 1))
                        pe.wait_ge(*(qk_kept(i, n + 2) if n < G - 1 or 1 in ages else qm_kept(i, n)))
                        for t in range(HALVES):
                            last = flip(head_ps[:, t, :], QK_pad[:, t, 0, 4 * n:4 * n + 4, :].rearrange("p h d -> p (h d)"), ident[:])
                        last.then_inc(qm_made.sem, 1)
                    elif step == "s2":
                        g = n // 2
                        pe.wait_ge(*qm_kept(i, g + 1))
                        pe.wait_ge(*p_made(i, 2 * n))
                        for t in range(HALVES):
                            first = P * t if causal else 0
                            for e in range(2):
                                last = mm(s2_ps[e][:, t, first:T], KT[:, 2 * n + e, t * P:(t + 1) * P], QmT[:, g, first:T],
                                          start=True, stop=not causal, skip_group_check=True)
                                if causal:
                                    own = slice(t * P, (t + 1) * P)
                                    last = mm(s2_ps[e][:, t, own], identb[:], maskT[:, t, own], start=False, stop=True,
                                              skip_group_check=True)
                                if t == HALVES - 1:
                                    last.then_inc(s2_made.sem, 1)
                    elif step == "pv":
                        g = n // 2
                        pe.wait_ge(*p_made(i, 2 * n + 2))
                        pe.wait_ge(*v_padded(i, g // 2 + 1))
                        if n % 2 == 0:
                            pe.wait_ge(*o_kept(i, g - 1))
                        for t in range(HALVES):
                            first = P * t if causal else 0
                            for e in range(2):
                                h = 2 * n + e
                                r = HP * (h % 4)
                                last = mm(o_ps[g % 2][r:r + HP, first:T], V_pad[:, t, h * KV // H, :], PT[:, n % 2, e, t, first:T],
                                          start=(t == 0), stop=(t == 1), skip_group_check=True, tile_position=(0, r))
                        last.then_inc(o_made.sem, 1)
                    elif step == "o":
                        pe.wait_ge(*o_kept(i, G))
                        pe.wait_ge(*(att_made(i, 1) if n else qkv_kept(i + 2, 2) if 0 in ages else y_read(i - 1, 1)))
                        for g in range(G):
                            last = flip(token_ps[:, g, :], OT[:, g, n * P:(n + 1) * P], ident[:])
                        last.then_inc(ot_made.sem, 1)
                    elif step == "att":
                        pe.wait_ge(*att_made(i, 2))
                        for t in range(HALVES):
                            last = flip(token_ps[:, t, :], att[:, t, :], ident[:])
                        last.then_inc(attf_made.sem, 1)
                    elif step == "y":
                        pe.wait_ge(*attT_kept(i, 1))
                        for t in range(HALVES):
                            last = mm(token_ps[:, t, :], attT[:, t * P:(t + 1) * P], w_out[:], start=True, stop=True)
                        last.then_inc(y_made.sem, 1)

            over_sequences(pe, steps)

        @block.vector
        def _(dve):
            tt, ts, red = nc.vector.tensor_tensor, nc.vector.tensor_scalar, nc.vector.tensor_reduce
            dve.wait_ge(consts, CONSTS)
            heads = lambda ap, n: ap.rearrange("p t (h d) -> p t h d", h=n)

            def steps(order, turn, ages):
                prep, tail = Chain(dve, prep_step, turn), Chain(dve, tail_step, turn - 2)
                for step, n, age in order:
                    i = turn - age
                    if step == "x":
                        xv = X[:, bass.ds(i * HALVES, HALVES), :]
                        dve.wait_ge(*xT_made(i, 0))
                        if causal:
                            prep(tt(sqx[:], xv, xv, ALU.mult))
                            prep(red(mv[:, :, 0], sqx[:], op=ALU.add, axis=X_AXIS))
                            ts(veps[:], mv[:, :, 0], 1.0 / E, LN_EPS, ALU.mult, ALU.add).then_inc(var_made.sem, 1)
                            dve.wait_ge(*rstd_made(i, 1))
                            tt(xh[:], xv, bc(rstd[:], 2, E), ALU.mult).then_inc(xh_made.sem, 1)
                        else:
                            prep(nc.vector.tensor_copy(xh[:], xv))
                            layer_norm(nc, dve, prep, xh, stats, mv, veps, rstd, scrap, HALVES, var_made, rstd_made, i)
                            tt(xh[:], xh[:], bc(rstd[:], 2, E), ALU.mult).then_inc(xh_made.sem, 1)
                            prep(tt(sqx[:], xv, bc(w_rad[:], 1, HALVES), ALU.mult))
                            prep(red(rad[:], sqx[:], op=ALU.add, axis=X_AXIS))
                            prep(ts(rad[:], rad[:], b_rad[:, 0:1], None, ALU.add))
                            prep(ts(rad[:], rad[:], 0.01, 0.5, ALU.mult, ALU.max))
                            prep(ts(rad[:], rad[:], 2.0, None, ALU.min))
                    elif step == "qkv":
                        dve.wait_ge(*qkv_made(i, n + 1))
                        dve.wait_ge(*v_padded(i, -1))
                        dve.wait_ge(*v_saved(i, 0))
                        src = token_ps[:].rearrange("p a c -> p (a c)")[:, 0:QKV]
                        ins = nc.vector.tensor_copy(qkv[:, n, :], src) if causal else tt(qkv[:, n, :], src, bias[:], ALU.add)
                        ins.then_inc(qkv_kept.sem, 1)
                    elif step == "rope":
                        dve.wait_ge(*qkv_kept(i, 2))
                        dve.wait_ge(*padded(i, 0))
                        qk = qkv[:, :, 0:QK * D]
                        for t in range(HALVES):
                            prep.free(tt(t1[:, t].rearrange("p (h d) -> p h d", h=QK), qk[:, t].rearrange("p (h d) -> p h d", h=QK),
                                         bc(cos[:, t], 1, QK), ALU.mult))
                            for z in range(2):
                                if causal:
                                    v = lambda ap: ap.rearrange("p (h z d) -> p h z d", h=QK, z=2)
                                    s = sin[:, t].rearrange("p (z d) -> p z d", z=2)[:, z]
                                    prep.free(tt(v(t2[:, t])[:, :, z], v(qk[:, t])[:, :, 1 - z], bc(s, 1, QK), ALU.mult))
                                else:
                                    v = lambda ap: ap.rearrange("p (h d z) -> p h d z", h=QK, z=2)
                                    s = sin[:, t].rearrange("p (d z) -> p d z", z=2)[:, :, z]
                                    prep.free(tt(v(t2[:, t])[:, :, :, z], v(qk[:, t])[:, :, :, 1 - z], bc(s, 1, QK), ALU.mult))
                        dve.wait_ge(*prep_step(i, prep.n))
                        if not causal:
                            prep(tt(t1[:], t1[:], t2[:], ALU.add))
                            prep(tt(t1[:], t1[:], bc(rad[:], 2, QK * D), ALU.mult))
                            th = heads(t1[:], QK)
                            prep(red(mean[:], th, op=ALU.add, axis=X_AXIS))
                            prep(ts(mean[:], mean[:], 1.0 / D, None, ALU.mult))
                            prep(tt(th, th, bc(mean[:], 3, D), ALU.subtract))
                            prep(tt(t2[:], t1[:], t1[:], ALU.mult))
                            prep(red(hvar[:], heads(t2[:], QK), op=ALU.add, axis=X_AXIS))
                            ts(hvar[:], hvar[:], 1.0 / D, LN_EPS, ALU.mult, ALU.add).then_inc(hvar_made.sem, 1)
                    elif step == "last":
                        if not causal:
                            dve.wait_ge(*hstd_made(i, 1))
                            prep(nc.vector.reciprocal(hstd[:], hstd[:]))
                            th = heads(t1[:], QK)
                            prep(tt(th, th, bc(hstd[:], 3, D), ALU.mult))
                            flat = t1[:].rearrange("p t (h d) -> p (t h) d", h=QK)
                            prep(tt(flat, flat, bc(w_ln[:], 1, 2 * QK), ALU.mult))
                        assert prep.n == PREP_STEPS, prep.n
                    elif step == "pad":
                        dve.wait_ge(*qm_made(i - 1, n + 1))
                        nc.vector.memset(QK_pad[:, :, 0, 4 * n:4 * n + 4, D], 0.0)
                        if causal:
                            q = lambda ap: ap[:, :, 4 * n * D:4 * (n + 1) * D].rearrange("p t (h d) -> p t h d", h=4)
                            k = lambda ap: bc(ap[:, :, E + n * D:E + (n + 1) * D], 2, 4)
                            tt(QK_pad[:, :, 0, 4 * n:4 * n + 4, 0:D], q(t1), q(t2), ALU.add)
                            tt(QK_pad[:, :, 1, 4 * n:4 * n + 4, 0:D], k(t1), k(t2), ALU.add).then_inc(padded.sem, 1)
                        else:
                            src = t1[:].rearrange("p t (c h d) -> p (t c) h d", c=2, d=D)[:, :, 4 * n:4 * n + 4, :]
                            dst = QK_pad[:].rearrange("p t c h d -> p (t c) h d")[:, :, 4 * n:4 * n + 4, 0:D]
                            b4 = bc(bc(b_ln[:], 1, 4), 1, 2 * HALVES)
                            tt(dst, src, b4, ALU.add).then_inc(padded.sem, 1)
                    elif step == "v":
                        dve.wait_ge(*o_made(i, -4 if n == 0 else 0))
                        v = qkv[:, :, QK * D:QKV] if n == 0 else v_rest[:]
                        half = slice(n * KV // 2, (n + 1) * KV // 2)
                        if n:
                            dve.wait_ge(*v_saved(i, 1))
                        nc.vector.tensor_copy(V_pad[:, :, half, 0:D], heads(v[:, :, 0:KV // 2 * D], KV // 2)).then_inc(v_padded.sem, 1)
                        if n == 0:
                            dve.wait_ge(*v_padded(i, 0))
                            nc.vector.tensor_copy(v_rest[:], v[:, :, KV // 2 * D:]).then_inc(v_saved.sem, 1)
                    elif step == "s1":
                        for e in range(2):
                            h = 2 * n + e
                            dve.wait_ge(*s1_made(i, h + 1))
                            if causal:
                                red(top[:, h, 0:1], s1_ps[e][:, 0, 0:P], op=ALU.max, axis=X_AXIS)
                                red(top[:, h, 1:2], s1_ps[e][:, 1, :], op=ALU.max, axis=X_AXIS).then_inc(top_made.sem, 1)
                            else:
                                red(top[:, h, :], s1_ps[e][:], op=ALU.max, axis=X_AXIS).then_inc(top_made.sem, 1)
                        if n % 2:
                            g = n // 2
                            dve.wait_ge(*top_made(i, 4 * g + 4))
                            ts(QK_pad[:, :, 0, 4 * g:4 * g + 4, D], top[:, 4 * g:4 * g + 4, :].rearrange("p h t -> p t h"), -1.0, None,
                               ALU.mult).then_inc(negm_made.sem, 1)
                    elif step == "o":
                        dve.wait_ge(*ot_made(i, n + 1))
                        dve.wait_ge(*attf_made(i, 0))
                        o = token_ps[:].rearrange("p g (r d) -> p (g r) d", d=HP)
                        tail(nc.vector.reciprocal(rec[:, n, :], o[:, :, D]))
                        tt(att[:, n].rearrange("p (h d) -> p h d", d=D), o[:, :, 0:D], bc(rec[:, n, :], 2, D), ALU.mult) \
                            .then_inc(att_made.sem, 1)
                    elif step == "y":
                        dve.wait_ge(*y_made(i, 1))
                        xv = X[:, bass.ds(i * HALVES, HALVES), :]
                        yv = token_ps[:, 0:HALVES, :]
                        if causal:
                            tt(y[:], yv, xv, ALU.add).then_inc(y_read.sem, 1)
                            dve.wait_ge(*y_read(i, 1))
                            tail(ts(xv, y[:], 100.0, -100.0, ALU.min, ALU.max))
                        else:
                            tt(y[:], yv, bc(b_out[:], 1, HALVES), ALU.add).then_inc(y_read.sem, 1)
                            dve.wait_ge(*y_read(i, 1))
                            tail(tt(y[:], y[:], xv, ALU.add))
                            layer_norm(nc, dve, tail, y, stats2, mv2, veps2, rstd2, scrap, HALVES, var2_made, rstd2_made, i)
                            tail(tt(xv, y[:], bc(rstd2[:], 2, E), ALU.mult))
                        assert tail.n == TAIL_STEPS, tail.n

            over_sequences(dve, steps)


def experts(nc, X, neg_half, a):
    N, F = 8, 256
    FK = F // P
    FS = 2
    FT = FS * HALVES
    TURNS = B // FS
    with Core(nc, "moe") as m:
        ident = m.sb("ident", [P])
        w_r = m.sb("w_r", [N])
        w_g, w_u = m.sb("w_g", [N, F]), m.sb("w_u", [N, F])
        w_d = m.sb("w_d", [N, FK, E])
        g2 = m.sb("g2", [1])
        lower = m.sb("lower", [N, N])
        sqx, xh = m.sb("sqx", [FT, E]), m.sb("xh", [FT, E])
        ssq, veps, rstd = m.sb("ssq", [FT]), m.sb("veps", [FT]), m.sb("rstd", [FT])
        xT, xT_next = m.sb("xT", [FT * P]), m.sb("xT_next", [FT * P])
        prob, top, den = m.sb("prob", [FT, N]), m.sb("top", [FT]), m.sb("den", [FT])
        cmp1, cmp2 = m.sb("cmp1", [FT, N, N]), m.sb("cmp2", [FT, N, N])
        rank, gate = m.sb("rank", [FT, N]), m.sb("gate", [FT, N])
        gate_next = m.sb("gate_next", [FT, N])
        act_g = m.sb("act_g", [2, FT * P])
        hid = m.sb("hid", [2, FK, FT * P])
        acc = m.sb("acc", [FT, E])
        g_ps = [m.ps(f"g_ps{i}", [FT * P]) for i in range(2)]
        u_ps = [m.ps(f"u_ps{i}", [FT * P]) for i in range(2)]
        d_ps = [m.ps(f"d_ps{i}", [FT, E]) for i in range(2)]
        tr_ps = m.ps("tr_ps", [FT, P])
        r_ps = m.ps("r_ps", [FT, N])
        consts = m.sem("consts")
        ROUTE_STEPS, STEPS = 14, 3 + (FT - 1) * N
        (var_made, rstd_made, xh_made, xT_made, xT_next_kept, xT_kept, route_made, shift_made, exp_made, gu_made,
         silu_made, hid_made, down_made, added, route_step, step_done), signals = m.signals(
            var_made=3, rstd_made=1, xh_made=1, xT_made=1, xT_next_kept=1, xT_kept=1, route_made=1, shift_made=1, exp_made=1,
            gu_made=N * FK, silu_made=N * FK, hid_made=N * FK, down_made=N, added=N, route_step=ROUTE_STEPS, step_done=STEPS)
        dmas = [(ident, "ident"), (w_r, "moe_w_r"), (g2, "moe_g2")]

        NORM_AT, FLIP_AT, ROUTE_AT = 3, 4, 5

        def over_turns(eng, first, turn):
            first(0)
            with eng.Fori(0, TURNS - 1) as c:
                turn(c, True)
            turn(TURNS - 1, False)

        block = m.block()

        @block.sync
        def _(sp):
            for signal in signals:
                sp.sem_inc(signal.sem, signal.start)
            for dst, name in dmas:
                sp.dma_start(dst[:], a[name]).then_inc(consts, 16)
            sp.dma_start(w_g[:], a["moe_w_g"].rearrange("e p f -> p e f")).then_inc(consts, 16)
            sp.dma_start(w_u[:], a["moe_w_u"].rearrange("e p f -> p e f")).then_inc(consts, 16)
            sp.dma_start(w_d[:], a["moe_w_d"].rearrange("e (k p) n -> p e k n", p=P)).then_inc(consts, 16)
            sp.dma_start(lower[:].rearrange("p a b -> p (a b)"), a["moe_lower"].partition_broadcast(P)).then_inc(consts, 16)

        @block.gpsimd
        def _(pool):
            with pool.Fori(0, TURNS) as c:
                pool.wait_ge(*var_made(c, 3))
                pool.tensor_tensor(rstd[:], veps[:], neg_half[:, 0:FT], ALU.pow).then_inc(rstd_made.sem, 1)

        @block.scalar
        def _(act):
            act.wait_ge(consts, 112)
            tr = tr_ps[:].rearrange("p t c -> p (t c)")

            def next_xT(c):
                act.wait_ge(*xT_made(c, 1))
                act.wait_ge(*route_made(c, 0))
                nc.scalar.activation(xT_next[:], tr, ACT.Copy, scale=g2[:, 0:1]).then_inc(xT_next_kept.sem, 1)

            def next_exp(c):
                act.wait_ge(*shift_made(c, 1))
                nc.scalar.activation(prob[:], prob[:], ACT.Exp).then_inc(exp_made.sem, 1)

            def keep_xT(c):
                act.wait_ge(*gu_made(c, 0))
                nc.scalar.activation(xT[:], tr, ACT.Copy, scale=g2[:, 0:1]).then_inc(xT_kept.sem, 1)

            def first(c):
                next_xT(c)
                next_exp(c)
                keep_xT(c)

            def turn(c, more):
                for e in range(N):
                    for k in range(FK):
                        n = FK * e + k
                        act.wait_ge(*gu_made(c, n + 1))
                        act.wait_ge(*hid_made(c, max(n - 1, 0)))
                        nc.scalar.activation(act_g[:, n % 2, :], g_ps[n % 2][:], ACT.Silu).then_inc(silu_made.sem, 1)
                    if more and e == FLIP_AT:
                        next_xT(c + 1)
                    if more and e == ROUTE_AT:
                        next_exp(c + 1)
                if more:
                    keep_xT(c + 1)

            over_turns(act, first, turn)

        @block.tensor
        def _(pe):
            mm = nc.tensor.matmul
            pe.wait_ge(consts, 112)

            def down(c, e):
                pe.wait_ge(*hid_made(c, FK * e + FK))
                pe.wait_ge(*added(c, max(e - 1, 0)))
                for t in range(FT):
                    for k in range(FK):
                        last = mm(d_ps[e % 2][:, t, :], hid[:, e % 2, k, t * P:(t + 1) * P], w_d[:, e, k, :],
                                  start=(k == 0), stop=(k == FK - 1))
                last.then_inc(down_made.sem, 1)

            def flips(c):
                pe.wait_ge(*xh_made(c, 1))
                pe.wait_ge(*xT_kept(c, 0))
                for t in range(FT):
                    last = nc.tensor.transpose(tr_ps[:, t, :], xh[:, t, :], ident[:])
                last.then_inc(xT_made.sem, 1)

            def route(c):
                pe.wait_ge(*xT_next_kept(c, 1))
                for t in range(FT):
                    last = mm(r_ps[:, t, :], xT_next[:, t * P:(t + 1) * P], w_r[:], start=True, stop=True)
                last.then_inc(route_made.sem, 1)

            def first(c):
                flips(c)
                route(c)

            def turn(c, more):
                pe.wait_ge(*xT_kept(c, 1))
                for e in range(N):
                    for k in range(FK):
                        n = FK * e + k
                        pe.wait_ge(*hid_made(c, max(n - 1, 0)))
                        mm(g_ps[n % 2][:], w_g[:, e, k * P:(k + 1) * P], xT[:], start=True, stop=True)
                        mm(u_ps[n % 2][:], w_u[:, e, k * P:(k + 1) * P], xT[:], start=True, stop=True).then_inc(gu_made.sem, 1)
                    if e:
                        down(c, e - 1)
                    if more and e == FLIP_AT:
                        flips(c + 1)
                    if more and e == ROUTE_AT:
                        route(c + 1)
                down(c, N - 1)

            over_turns(pe, first, turn)

        @block.vector
        def _(dve):
            tt, ts, red = nc.vector.tensor_tensor, nc.vector.tensor_scalar, nc.vector.tensor_reduce
            dve.wait_ge(consts, 112)

            def add_expert(c, link, e):
                dve.wait_ge(*down_made(c, e + 1))
                for t in range(FT):
                    if e == 0:
                        ins = ts(acc[:, t, :], d_ps[0][:, t, :], gate[:, t, e:e + 1], None, ALU.mult)
                    else:
                        ins = nc.vector.scalar_tensor_tensor(acc[:, t, :], d_ps[e % 2][:, t, :], gate[:, t, e:e + 1], acc[:, t, :],
                                                             ALU.mult, ALU.add)
                    if t == FT - 1:
                        ins.then_inc(added.sem, 1)
                    else:
                        link.free(ins)
                dve.wait_ge(*added(c, e + 1))

            def norm(c):
                xv = X[:, bass.ds(c * FT, FT), :]
                tt(sqx[:], xv, xv, ALU.mult).then_inc(var_made.sem, 1)
                dve.wait_ge(*var_made(c, 1))
                red(ssq[:], sqx[:], op=ALU.add, axis=X_AXIS).then_inc(var_made.sem, 1)
                dve.wait_ge(*var_made(c, 2))
                ts(veps[:], ssq[:], 1.0 / E, LN_EPS, ALU.mult, ALU.add).then_inc(var_made.sem, 1)
                dve.wait_ge(*rstd_made(c, 1))
                dve.wait_ge(*xT_made(c, 0))
                tt(xh[:], xv, bc(rstd[:], 2, E), ALU.mult).then_inc(xh_made.sem, 1)

            def route(c):
                link = Chain(dve, route_step, c)
                dve.wait_ge(*route_made(c, 1))
                link(red(top[:], r_ps[:], op=ALU.max, axis=X_AXIS))
                tt(prob[:], r_ps[:], bc(top[:], 2, N), ALU.subtract).then_inc(shift_made.sem, 1)
                dve.wait_ge(*exp_made(c, 1))
                link(red(den[:], prob[:], op=ALU.add, axis=X_AXIS))
                link(nc.vector.reciprocal(den[:], den[:]))
                link(tt(prob[:], prob[:], bc(den[:], 2, N), ALU.mult))
                other, own = bc(prob[:], 2, N), bc(prob[:], 3, N)
                link(tt(cmp1[:], other, own, ALU.is_gt))
                link(tt(cmp2[:], other, own, ALU.is_equal))
                link(tt(cmp2[:], cmp2[:], bc(lower[:], 1, FT), ALU.mult))
                link(tt(cmp1[:], cmp1[:], cmp2[:], ALU.add))
                link(red(rank[:], cmp1[:], op=ALU.add, axis=X_AXIS))
                link(ts(rank[:], rank[:], 2.0, None, ALU.is_lt))
                link(tt(gate_next[:], prob[:], rank[:], ALU.mult))
                link(red(den[:], gate_next[:], op=ALU.add, axis=X_AXIS))
                link(nc.vector.reciprocal(den[:], den[:]))
                tt(gate_next[:], gate_next[:], bc(den[:], 2, N), ALU.mult).then_inc(route_step.sem, 1)
                assert link.n + 1 == ROUTE_STEPS, link.n

            def first(c):
                norm(c)
                route(c)

            def turn(c, more):
                link = Chain(dve, step_done, c)
                dve.wait_ge(*route_step(c, ROUTE_STEPS))
                link(nc.vector.tensor_copy(gate[:], gate_next[:]))
                for e in range(N):
                    for k in range(FK):
                        n = FK * e + k
                        dve.wait_ge(*silu_made(c, n + 1))
                        dve.wait_ge(*down_made(c, max(e - 1, 0)))
                        tt(hid[:, e % 2, k, :], act_g[:, n % 2, :], u_ps[n % 2][:], ALU.mult).then_inc(hid_made.sem, 1)
                    if e:
                        add_expert(c, link, e - 1)
                    if more and e == NORM_AT:
                        norm(c + 1)
                    if more and e == ROUTE_AT:
                        route(c + 1)
                add_expert(c, link, N - 1)
                xv = X[:, bass.ds(c * FT, FT), :]
                link(tt(acc[:], acc[:], xv, ALU.add))
                link(ts(xv, acc[:], 100.0, -100.0, ALU.min, ALU.max))
                assert link.n == STEPS, link.n

            over_turns(dve, first, turn)


def build(nc, a, out):
    with Core(nc, "all") as m:
        X = m.sb("X", [TILES, E])
        X0 = m.sb("X0", [TILES, E])
        neg_half = m.sb("neg_half", [8])
        load_x(nc, a["x"], X, neg_half)
        if 1 in STAGES:
            head_mixer(nc, X, neg_half, a["ident"], a["mix_mask"], a["mix_w"], a["mix_bias"], a["inv_count"], a["count"])
        if 2 in STAGES:
            layer_stack(nc, X, X0, neg_half, a)
            add_norm(nc, X0, X, neg_half, "norm_stack")
        if 3 in STAGES:
            small_heads(nc, X, X0, neg_half, a, causal=False)
        if 4 in STAGES:
            small_heads(nc, X, X0, neg_half, a, causal=True)
            experts(nc, X, neg_half, a)
            add_norm(nc, X0, X, neg_half, "norm_moe")
        store_x(nc, X, out)


def kernel(**inputs):
    import numpy as np
    import ml_dtypes
    import concourse.bacc as bacc
    from concourse.bass_utils import run_bass_kernel_spmd

    f = lambda n: np.asarray(inputs[n])
    a = {"x": f("L0_attn_y_de").reshape(B * T, E), "ident": np.eye(P, dtype=np.float32)}
    w = np.zeros((E, 3, 16, 8), np.float32)
    for j, n in enumerate("qkv"):
        for h in range(16):
            w[8 * h:8 * h + 8, j, h, :] = f(f"L0_attn_W{n}").T
    a["mix_w"] = w.reshape(E, 3 * E)
    a["mix_bias"] = np.concatenate([np.tile(f(f"L0_attn_b{n}"), 16) for n in "qkv"])
    t = np.arange(T)[:, None]
    a["mix_mask"] = (np.arange(E)[None, :] < t).astype(np.float32).reshape(HALVES, P, E).transpose(1, 0, 2).copy()
    a["inv_count"] = (1.0 / np.arange(1, 17)).astype(np.float32)
    a["count"] = np.arange(1, 17).astype(np.float32)

    a["identb"] = np.eye(P).astype(ml_dtypes.bfloat16)
    W = 32
    rows, keys = np.arange(P), np.arange(2 * W)
    q = rows % W
    win = np.zeros((P, 4, 2, 2 * W))
    for j in range(2):
        bad = (keys[None, :] < q[:, None]) | (keys[None, :] > q[:, None] + W)
        bad |= (rows[:, None] < W) & (j == 0) & (keys[None, :] < W)
        win[:, :, j, :] = np.where(bad, MASKED, 0.0)[:, None, :]
    a["win_mask"] = win.astype(ml_dtypes.bfloat16)
    half = np.arange(0, 64, 2, dtype=np.float64)
    freqs = (np.arange(T, dtype=np.float32)[:, None] * (1.0 / 10000.0 ** (half / 64)).astype(np.float32)[None, :]).astype(np.float64)
    base = (half + 0.4 * 64) / (1.4 * 64)
    scale = base[None, :] ** ((np.arange(T) - T // 2) / 16)[:, None]
    two = lambda x: np.concatenate([x, x], 1)
    cos, scale = two(np.cos(freqs)), two(scale)
    sin = np.concatenate([-np.sin(freqs), np.sin(freqs)], 1)
    tok = lambda x: np.stack(x, 1).reshape(HALVES, P, len(x), -1).transpose(1, 0, 2, 3).astype(np.float32)
    a["cos0"] = tok([cos * scale * 8.0, cos / scale])
    a["sin0"] = tok([sin * scale * 8.0, sin / scale])
    F, FP = 341, 384
    a["wqkv"], a["wo"], a["w1"] = f("L0_ffn_Wqkv"), f("L0_ffn_Wo"), f("L0_ffn_W1")
    w2 = np.zeros((6, FP, E), np.float32)
    w2[:, :F] = f("L0_ffn_W2")
    b1 = np.zeros((6, 2, FP), np.float32)
    b1[:, :, :F] = f("L0_ffn_b1").reshape(6, 2, F)
    a["w2"], a["b1"], a["b2"] = w2, b1.reshape(6, 2, 3, P).transpose(0, 3, 1, 2).reshape(6, P, 6), f("L0_ffn_b2")
    a["qk_scale"] = np.concatenate([f("L0_ffn_q_scale"), f("L0_ffn_k_scale")], 1)
    a["ln_g"], a["ln_b"] = f("L0_ffn_ln_g")[:, :, None], f("L0_ffn_ln_b")[:, :, None]

    mel = 2595.0 * np.log10(1.0 + 4000.0 / 200.0)
    fb = 200.0 * (10.0 ** (np.linspace(0.0, mel, 4) / 2595.0) - 1.0) / 1000.0
    ang = (np.arange(T, dtype=np.float32)[:, None] * fb.astype(np.float32)[None, :]).astype(np.float64)
    pairs = lambda x, y: np.stack([x, y], -1).reshape(T, -1)
    halves = lambda x: x.reshape(HALVES, P, -1).transpose(1, 0, 2).astype(np.float32)
    a["rot_cos"], a["rot_sin"] = halves(pairs(np.cos(ang), np.cos(ang))), halves(pairs(-np.sin(ang), np.sin(ang)))
    a["rot_w"] = np.concatenate([f("L1_attn_q_w"), f("L1_attn_kv_w")], 1)
    a["rot_bias"] = np.concatenate([f("L1_attn_q_b"), f("L1_attn_kv_b")])
    a["rot_w_out"], a["rot_b_out"] = f("L1_attn_out_w"), f("L1_attn_out_b")
    a["rot_w_rad"], a["rot_b_rad"] = f("L1_attn_rh_w")[:, 0], f("L1_attn_rh_b")
    a["rot_w_ln"], a["rot_b_ln"] = f("L1_attn_ln_w"), f("L1_attn_ln_b")
    a["rot_aff"] = np.stack([f(f"L1_attn_{n}") for n in ("qn_w", "qn_b", "kvn_w", "kvn_b")], 1)
    ang = (np.arange(T, dtype=np.float32)[:, None] * (1.0 / 10000.0 ** (np.arange(0, 8, 2) / 8)).astype(np.float32)[None, :]).astype(np.float64)
    a["cau_cos"] = halves(np.concatenate([np.cos(ang), np.cos(ang)], 1))
    a["cau_sin"] = halves(np.concatenate([-np.sin(ang), np.sin(ang)], 1))
    a["cau_w"] = np.concatenate([f(f"L1_ffn_W{n}") for n in "qkv"], 1)
    a["cau_w_out"] = f("L1_ffn_Wo")
    g1, zero = f("L1_ffn_ln1_w"), np.zeros(E, np.float32)
    a["cau_aff"] = np.stack([g1, zero, g1, zero], 1)
    t = np.arange(T)
    see = np.where(t[None, :] <= t[:, None], 0.0, MASKED)
    fold = lambda x: x.reshape(HALVES, P, T).transpose(1, 0, 2).astype(ml_dtypes.bfloat16)
    a["causal"], a["causal_t"] = fold(see), fold(see.T)
    a["moe_w_r"], a["moe_g2"] = f("L1_ffn_Wr"), f("L1_ffn_ln2_w")[:, None]
    a["moe_w_g"], a["moe_w_u"], a["moe_w_d"] = f("L1_ffn_Wg"), f("L1_ffn_Wu"), f("L1_ffn_Wd")
    a["moe_lower"] = (np.arange(8)[None, :] < np.arange(8)[:, None]).astype(np.float32).reshape(-1)

    nc = bacc.Bacc("TRN2", target_bir_lowering=False, num_devices=1)
    arrays, aps = {}, {}
    for n, v in a.items():
        v = np.ascontiguousarray(v)
        arrays[f"in_{n}"] = v
        aps[n] = nc.dram_tensor(f"in_{n}", v.shape, mybir.dt.from_np(v.dtype), kind="ExternalInput").ap()
    out = nc.dram_tensor("out_x", (B * T, E), F32, kind="ExternalOutput").ap()
    build(nc, aps, out)
    r = run_bass_kernel_spmd(nc, [arrays], core_ids=[0])
    return np.asarray(r.results[0]["out_x"]).reshape(B, T, E)
```
